# Optimizing a Trainium2 kernel written in Bass

```python
import numpy as np
import jax
import jax.numpy as jnp

def _softmax(x, axis=-1):
    return jax.nn.softmax(x, axis=axis)
def _gelu(x):
    return jax.nn.gelu(x, approximate=True)
def _silu(x):
    return jax.nn.silu(x)
def _sigmoid(x):
    return jax.nn.sigmoid(x)
def _layernorm(x, axis=-1, eps=1e-5):
    m = jnp.mean(x, axis=axis, keepdims=True)
    v = jnp.var(x, axis=axis, keepdims=True)
    return (x - m) / jnp.sqrt(v + eps)
def _scatter_add(tgt, idx, src, axis=0):
    return tgt.at[idx].add(src)
def _segment_sum(src, seg, n):
    return jax.ops.segment_sum(src, seg, n)

kernel_name = 'mk_conv_preact_d2_conv_nchw192_3fbcc0'

def setup_inputs(seed: int = 0):
    np.random.seed(seed)
    _w = jnp.asarray
    def _rec_inputs():
        import jax
        import jax.numpy as jnp
        _gk = jax.random.key(seed)
        x = -0.0001476 + 0.9999 * jax.random.normal(jax.random.fold_in(_gk, 1), (64, 192, 56, 56), jnp.float32)
        return x
    x = _rec_inputs()
    def _L0_conv_setup():
        import math
        import jax, jax.numpy as jnp
        import numpy as np

        def _positionalencoding2d(d_model, height, width):
            pe = np.zeros((d_model, height, width), dtype=np.float32)
            dm = d_model // 2
            div_term = np.exp(np.arange(0.0, dm, 2.0) * -(math.log(10000.0) / dm))
            pos_w = np.arange(0.0, width)[:, None]
            pos_h = np.arange(0.0, height)[:, None]
            sw = np.sin(pos_w * div_term).T[:, None, :]
            cw = np.cos(pos_w * div_term).T[:, None, :]
            sh = np.sin(pos_h * div_term).T[:, :, None]
            ch = np.cos(pos_h * div_term).T[:, :, None]
            pe[0:dm:2] = np.repeat(sw, height, axis=1)
            pe[1:dm:2] = np.repeat(cw, height, axis=1)
            pe[dm::2] = np.repeat(sh, width, axis=2)
            pe[dm + 1::2] = np.repeat(ch, width, axis=2)
            return pe

        def _distance_tensor(k):
            i = np.arange(k, dtype=np.float32) + 0.5 - k / 2.0
            d = np.sqrt(i[:, None] ** 2 + i[None, :] ** 2)
            return d.astype(np.float32)
        B, DIM, H, W = (64, 192, 56, 56)
        K, FEMB, FORD = (55, 32, 64)
        key = jax.random.key(seed)
        ks = jax.random.split(key, 5)
        x = jax.random.normal(ks[0], (B, DIM, H, W), dtype=jnp.float32)
        z = jnp.asarray(_positionalencoding2d(FEMB, K, K))[None]
        distance_map = jnp.asarray(_distance_tensor(K))[None, None]
        fast, slow, target = (0.3, 1.5, 0.01)
        max_d, min_d = (math.log(target) / fast, math.log(target) / slow)
        deltas = (jnp.linspace(min_d, max_d, DIM, dtype=jnp.float32) / K)[None, :, None, None]
        s1 = 1.0 / math.sqrt(FEMB)
        s2 = 1.0 / math.sqrt(FORD)
        W1 = jax.random.normal(ks[1], (FORD, FEMB), dtype=jnp.float32) * s1
        W2 = jax.random.normal(ks[2], (FORD, FORD), dtype=jnp.float32) * s2
        W3 = jax.random.normal(ks[3], (DIM, FORD), dtype=jnp.float32) * s2
        b1 = jnp.zeros((FORD,), jnp.float32)
        b2 = jnp.zeros((FORD,), jnp.float32)
        f1 = jnp.ones((1, FORD, 1, 1), jnp.float32)
        f2 = jnp.ones((1, FORD, 1, 1), jnp.float32)
        shift = jnp.zeros((1, DIM, 1, 1), jnp.float32)
        bias = jax.random.normal(ks[4], (1, DIM, 1, 1), dtype=jnp.float32)
        return {'x': x, 'z': z, 'W1': W1, 'b1': b1, 'f1': f1, 'W2': W2, 'b2': b2, 'f2': f2, 'W3': W3, 'deltas': deltas, 'shift': shift, 'bias': bias, 'distance_map': distance_map}
    _L0_conv_all = _L0_conv_setup()
    _L0_conv_in = {k: v for k, v in _L0_conv_all.items() if k in ('z', 'W1', 'b1', 'f1', 'W2', 'b2', 'f2', 'W3', 'deltas', 'shift', 'bias', 'distance_map', )}
    del _L0_conv_all

    def _L1_conv_setup():
        import jax, jax.numpy as jnp
        import numpy as np
        B, C, N, M = (4, 192, 160, 160)
        HEADS, DH = (4, 32)
        HID = HEADS * DH
        NMEM = 4
        SCALE = DH ** (-0.5)

        def _rms(x, g):
            n = jnp.sqrt(jnp.sum(x * x, axis=1, keepdims=True))
            gshape = (1, -1) + (1,) * (x.ndim - 2)
            return x / jnp.maximum(n, 1e-12) * g.reshape(gshape) * jnp.sqrt(jnp.asarray(x.shape[1], x.dtype))

        def _axial_attn(q_ft, k_ft, v_map, rep, Wq, Wk, Wv, mem_kv, Wo, bo, gq, gk, gv):
            b = q_ft.shape[0]
            q = jnp.einsum('hdc,bcq->bhqd', Wq.reshape(HEADS, DH, -1), _rms(q_ft, gq))
            k = jnp.einsum('hdc,bck->bhkd', Wk.reshape(HEADS, DH, -1), _rms(k_ft, gk))
            v = jnp.einsum('hdc,bckr->bhkrd', Wv.reshape(HEADS, DH, -1), _rms(v_map, gv))
            v_sum = v.sum(axis=3)
            mem_k, mem_v = (mem_kv[0], mem_kv[1])
            s_k = jnp.einsum('bhqd,bhkd->bhqk', q, k) * SCALE
            s_m = jnp.einsum('bhqd,hjd->bhqj', q, mem_k) * SCALE
            mx = jnp.maximum(s_k.max(-1), s_m.max(-1))
            e_k = jnp.exp(s_k - mx[..., None])
            e_m = jnp.exp(s_m - mx[..., None])
            Z = e_m.sum(-1) + rep * e_k.sum(-1)
            out = (jnp.einsum('bhqj,hjd->bhqd', e_m, mem_v) + jnp.einsum('bhqk,bhkd->bhqd', e_k, v_sum)) / Z[..., None]
            out = out.transpose(0, 2, 1, 3).reshape(b, -1, HID)
            return jnp.einsum('ck,bqk->bcq', Wo, out) + bo[None, :, None]
        key = jax.random.key(seed)
        ks = jax.random.split(key, 8)
        std = 0.05
        return {'x': jax.random.normal(ks[0], (B, C, N, M), jnp.float32), 'gq': jnp.ones((C,), jnp.float32), 'gk': jnp.ones((C,), jnp.float32), 'gv': jnp.ones((C,), jnp.float32), 'Wq': jax.random.normal(ks[1], (HID, C), jnp.float32) * std, 'Wk': jax.random.normal(ks[2], (HID, C), jnp.float32) * std, 'Wv': jax.random.normal(ks[3], (HID, C), jnp.float32) * std, 'mem_kv': jax.random.normal(ks[4], (2, HEADS, NMEM, DH), jnp.float32), 'Wo': jax.random.normal(ks[5], (C, HID), jnp.float32) * std, 'bo': jnp.zeros((C,), jnp.float32), 'Wr': jax.random.normal(ks[6], (C, 2 * C), jnp.float32) * std}
    _L1_conv_all = _L1_conv_setup()
    _L1_conv_in = {k: v for k, v in _L1_conv_all.items() if k in ('gq', 'gk', 'gv', 'Wq', 'Wk', 'Wv', 'mem_kv', 'Wo', 'bo', 'Wr', )}
    del _L1_conv_all

    return {
        "x": x,
        "L0_conv_z": _L0_conv_in["z"],
        "L0_conv_W1": _L0_conv_in["W1"],
        "L0_conv_b1": _L0_conv_in["b1"],
        "L0_conv_f1": _L0_conv_in["f1"],
        "L0_conv_W2": _L0_conv_in["W2"],
        "L0_conv_b2": _L0_conv_in["b2"],
        "L0_conv_f2": _L0_conv_in["f2"],
        "L0_conv_W3": _L0_conv_in["W3"],
        "L0_conv_deltas": _L0_conv_in["deltas"],
        "L0_conv_shift": _L0_conv_in["shift"],
        "L0_conv_bias": _L0_conv_in["bias"],
        "L0_conv_distance_map": _L0_conv_in["distance_map"],
        "L1_conv_gq": _L1_conv_in["gq"],
        "L1_conv_gk": _L1_conv_in["gk"],
        "L1_conv_gv": _L1_conv_in["gv"],
        "L1_conv_Wq": _L1_conv_in["Wq"],
        "L1_conv_Wk": _L1_conv_in["Wk"],
        "L1_conv_Wv": _L1_conv_in["Wv"],
        "L1_conv_mem_kv": _L1_conv_in["mem_kv"],
        "L1_conv_Wo": _L1_conv_in["Wo"],
        "L1_conv_bo": _L1_conv_in["bo"],
        "L1_conv_Wr": _L1_conv_in["Wr"],
    }

def reference(x, L0_conv_z, L0_conv_W1, L0_conv_b1, L0_conv_f1, L0_conv_W2, L0_conv_b2, L0_conv_f2, L0_conv_W3, L0_conv_deltas, L0_conv_shift, L0_conv_bias, L0_conv_distance_map, L1_conv_gq, L1_conv_gk, L1_conv_gv, L1_conv_Wq, L1_conv_Wk, L1_conv_Wv, L1_conv_mem_kv, L1_conv_Wo, L1_conv_bo, L1_conv_Wr):
    import jax
    import jax.numpy as jnp
    def _L0_conv_ref(x, z, W1, b1, f1, W2, b2, f2, W3, deltas, shift, bias, distance_map):
        import math
        import jax, jax.numpy as jnp
        import numpy as np

        def _positionalencoding2d(d_model, height, width):
            pe = np.zeros((d_model, height, width), dtype=np.float32)
            dm = d_model // 2
            div_term = np.exp(np.arange(0.0, dm, 2.0) * -(math.log(10000.0) / dm))
            pos_w = np.arange(0.0, width)[:, None]
            pos_h = np.arange(0.0, height)[:, None]
            sw = np.sin(pos_w * div_term).T[:, None, :]
            cw = np.cos(pos_w * div_term).T[:, None, :]
            sh = np.sin(pos_h * div_term).T[:, :, None]
            ch = np.cos(pos_h * div_term).T[:, :, None]
            pe[0:dm:2] = np.repeat(sw, height, axis=1)
            pe[1:dm:2] = np.repeat(cw, height, axis=1)
            pe[dm::2] = np.repeat(sh, width, axis=2)
            pe[dm + 1::2] = np.repeat(ch, width, axis=2)
            return pe

        def _distance_tensor(k):
            i = np.arange(k, dtype=np.float32) + 0.5 - k / 2.0
            d = np.sqrt(i[:, None] ** 2 + i[None, :] ** 2)
            return d.astype(np.float32)
        h = jnp.einsum('bchw,oc->bohw', z, W1) + b1[None, :, None, None]
        h = jnp.sin(f1 * h)
        h = jnp.einsum('bchw,oc->bohw', h, W2) + b2[None, :, None, None]
        h = jnp.sin(f2 * h)
        k = jnp.einsum('bchw,oc->bohw', h, W3)
        decay = jnp.exp(-distance_map * jnp.abs(deltas))
        k = k * (decay + shift)
        B, C, H, W = x.shape
        Kh, Kw = (k.shape[-2], k.shape[-1])
        s = (H + Kh - 1, W + Kw - 1)
        xf = jnp.fft.rfft2(x, s)
        kf = jnp.fft.rfft2(k[0], s)
        y = jnp.fft.irfft2(xf * kf[None], s)
        y = y[..., Kh // 2:Kh // 2 + H, Kw // 2:Kw // 2 + W]
        return y + bias * x

    def _L1_conv_ref(x, gq, gk, gv, Wq, Wk, Wv, mem_kv, Wo, bo, Wr):
        import jax, jax.numpy as jnp
        import numpy as np
        B, C, N, M = (4, 192, 160, 160)
        HEADS, DH = (4, 32)
        HID = HEADS * DH
        NMEM = 4
        SCALE = DH ** (-0.5)

        def _rms(x, g):
            n = jnp.sqrt(jnp.sum(x * x, axis=1, keepdims=True))
            gshape = (1, -1) + (1,) * (x.ndim - 2)
            return x / jnp.maximum(n, 1e-12) * g.reshape(gshape) * jnp.sqrt(jnp.asarray(x.shape[1], x.dtype))

        def _axial_attn(q_ft, k_ft, v_map, rep, Wq, Wk, Wv, mem_kv, Wo, bo, gq, gk, gv):
            b = q_ft.shape[0]
            q = jnp.einsum('hdc,bcq->bhqd', Wq.reshape(HEADS, DH, -1), _rms(q_ft, gq))
            k = jnp.einsum('hdc,bck->bhkd', Wk.reshape(HEADS, DH, -1), _rms(k_ft, gk))
            v = jnp.einsum('hdc,bckr->bhkrd', Wv.reshape(HEADS, DH, -1), _rms(v_map, gv))
            v_sum = v.sum(axis=3)
            mem_k, mem_v = (mem_kv[0], mem_kv[1])
            s_k = jnp.einsum('bhqd,bhkd->bhqk', q, k) * SCALE
            s_m = jnp.einsum('bhqd,hjd->bhqj', q, mem_k) * SCALE
            mx = jnp.maximum(s_k.max(-1), s_m.max(-1))
            e_k = jnp.exp(s_k - mx[..., None])
            e_m = jnp.exp(s_m - mx[..., None])
            Z = e_m.sum(-1) + rep * e_k.sum(-1)
            out = (jnp.einsum('bhqj,hjd->bhqd', e_m, mem_v) + jnp.einsum('bhqk,bhkd->bhqd', e_k, v_sum)) / Z[..., None]
            out = out.transpose(0, 2, 1, 3).reshape(b, -1, HID)
            return jnp.einsum('ck,bqk->bcq', Wo, out) + bo[None, :, None]
        row_ft = x.mean(axis=3)
        col_ft = x.mean(axis=2)
        row_attn = _axial_attn(row_ft, col_ft, x.transpose(0, 1, 3, 2), N, Wq, Wk, Wv, mem_kv, Wo, bo, gq, gk, gv)
        col_attn = _axial_attn(col_ft, row_ft, x, M, Wq, Wk, Wv, mem_kv, Wo, bo, gq, gk, gv)
        Wr1, Wr2 = (Wr[:, :C], Wr[:, C:])
        out = jnp.einsum('dc,bcn->bdn', Wr1, row_attn)[:, :, :, None] + jnp.einsum('dc,bcm->bdm', Wr2, col_attn)[:, :, None, :]
        return out

    def _gn(v, G=32, eps=1e-5):
        B_, C_, H_, W_ = v.shape
        g = v.reshape(B_, G, C_ // G, H_, W_)
        m = jnp.mean(g, axis=(2, 3, 4), keepdims=True)
        s = jnp.var(g, axis=(2, 3, 4), keepdims=True)
        return ((g - m) / jnp.sqrt(s + eps)).reshape(v.shape)

    def _ln_c(v, eps=1e-6):
        m = jnp.mean(v, axis=1, keepdims=True)
        s = jnp.var(v, axis=1, keepdims=True)
        return (v - m) / jnp.sqrt(s + eps)

    def _ln_t(v, eps=1e-5):
        m = jnp.mean(v, axis=-1, keepdims=True)
        s = jnp.var(v, axis=-1, keepdims=True)
        return (v - m) / jnp.sqrt(s + eps)

    def _to_tokens(v):
        B_, C_, H_, W_ = v.shape
        return v.reshape(B_, C_, H_ * W_).transpose(0, 2, 1)
    def _from_tokens(t, like):
        B_, C_, H_, W_ = like.shape
        return t.transpose(0, 2, 1).reshape(B_, C_, H_, W_)

    x = x + _L0_conv_ref(_gn(x), L0_conv_z, L0_conv_W1, L0_conv_b1, L0_conv_f1, L0_conv_W2, L0_conv_b2, L0_conv_f2, L0_conv_W3, L0_conv_deltas, L0_conv_shift, L0_conv_bias, L0_conv_distance_map)
    x = x + _L1_conv_ref(_gn(x), L1_conv_gq, L1_conv_gk, L1_conv_gv, L1_conv_Wq, L1_conv_Wk, L1_conv_Wv, L1_conv_mem_kv, L1_conv_Wo, L1_conv_bo, L1_conv_Wr)
    return x


_drawn_inputs = setup_inputs


def setup_inputs(seed=0):
    import zlib

    import numpy as np

    out = dict(_drawn_inputs(seed))
    spreads = {'L0_conv_b1': (0.0, 0.1),
     'L0_conv_f1': (1.0, 0.2),
     'L0_conv_b2': (0.0, 0.1),
     'L0_conv_f2': (1.0, 0.2),
     'L0_conv_shift': (0.0, 0.1),
     'L1_conv_gq': (1.0, 0.6),
     'L1_conv_gk': (1.0, 0.6),
     'L1_conv_gv': (1.0, 0.6),
     'L1_conv_bo': (0.0, 1.29)}
    factors = {'L1_conv_Wq': 8.0,
     'L1_conv_Wk': 8.0,
     'L1_conv_Wv': 6.388,
     'L1_conv_mem_kv': 8.0,
     'L1_conv_Wo': 6.308}
    for name, (base, spread) in spreads.items():
        noise = np.random.default_rng([zlib.crc32(name.encode()), seed]).standard_normal(out[name].shape)
        drawn = base * np.exp(spread * noise) if base else spread * noise
        out[name] = jnp.asarray(drawn.astype(out[name].dtype))
    for name, factor in factors.items():
        out[name] = (out[name] * factor).astype(out[name].dtype)
    return out
```

```python
from contextlib import ExitStack

import numpy as np

import concourse.bass as bass
from concourse import mybir

ALU = mybir.AluOpType
ACT = mybir.ActivationFunctionType
F32 = mybir.dt.float32
AX = mybir.AxisListType

B, C, H, W = 64, 192, 56, 56
KH = 55
MID = KH // 2
GROUPS, CG = 32, C // 32
FEMB, FORD = 32, 64
L = H + MID
U = L // 2 + 1
NE = 2 * W - 1
HB = B // 2
HALF = 64
KP = HALF + H
EPS = 1e-5
WP = 64
HC = C // 2

A_UNITS = [3, 3, 3, 3, 2, 2]
B_UNITS, B_MM = 6, 7
T_UNITS, T_MM = 8, 4
D_UNITS, D_BQ = 4, 8
assert B_UNITS * B_MM == U and T_UNITS * T_MM == HB and D_UNITS * D_BQ == HB and 2 * sum(A_UNITS) == HB


def constants():
    h, u, i = np.arange(H), np.arange(U), np.arange(KH)
    th = 2 * np.pi / L * (np.outer(h, u) % L)
    fwd = np.zeros((KP, 2, 2, U), np.float64)
    inv = np.zeros((2, U, 2, KP), np.float64)
    mean = np.zeros((KP, KP), np.float64)
    weight = np.where(u == 0, 1.0, 2.0) / L
    for p in range(2):
        rows = slice(HALF * p, HALF * p + H)
        fwd[rows, 0, p] = np.cos(th)
        fwd[rows, 1, p] = -np.sin(th)
        inv[p, :, 0, rows] = (np.cos(th) * weight).T
        inv[p, :, 1, rows] = (-np.sin(th) * weight).T
        mean[rows, rows] = 1.0 / (2 * H)
    tk = 2 * np.pi / L * (np.outer(i - MID, u) % L)
    taps = np.concatenate([np.cos(tk), -np.sin(tk)], axis=1)
    centre = (np.arange(KH) == MID).astype(np.float64)[:, None]
    f = lambda a: np.ascontiguousarray(a, dtype=np.float32)
    return {
        "k_fwd": f(fwd.reshape(KP, 4 * U)), "k_inv": f(inv.reshape(2 * U, 2 * KP)), "k_mean": f(mean),
        "k_gmean": f(np.kron(np.eye(HC // CG), np.full((CG, CG), 1.0 / (CG * H * W)))),
        "k_taps": f(taps), "k_centre": f(centre), "k_eye": f(np.eye(128)),
    }


def filters(nc, d, khat):
    NPOS = KH * KH
    NCH = 7
    CH = NPOS // 7 + 1
    chunks = [(a, min(a + CH, NPOS)) for a in range(0, NPOS, CH)]
    PI = float(np.pi)
    INV2PI = float(np.float32(1 / (2 * np.pi)))
    ROUND = float(1.5 * 2 ** 23)
    TWO_PI_HI = 6.28125
    TWO_PI_LO = float(np.float32(2 * np.pi - 6.28125))
    PI_IN = 3.1415925
    JB = 5
    with ExitStack() as ctx:
        sb = lambda n, s: ctx.enter_context(nc.sbuf_tensor("f_" + n, s, F32))
        sem = lambda n: ctx.enter_context(nc.semaphore("f_" + n))
        z = sb("z", [FEMB, NPOS])
        arg = sb("arg", [FORD, NPOS])
        turns = sb("turns", [FORD, NPOS])
        h1 = sb("h1", [FORD, NPOS])
        w1T = sb("w1T", [FEMB, FORD])
        w2T = sb("w2T", [FORD, FORD])
        w3T = sb("w3T", [FORD, C])
        vec = sb("vec", [FORD, 4])
        dist = sb("dist", [KH, KH])
        ndist = sb("ndist", [KH, KH])
        chan = sb("chan", [KH, 3, C])
        absd = sb("absd", [KH, C])
        centre = sb("centre", [KH, 1])
        taps_dft = sb("taps", [KH, 2 * U])
        k = sb("k", [KH, KH, C])
        kf = sb("kf", [HC, 3, NE, U])
        pnet = ctx.enter_context(nc.psum_tensor("f_pnet", [128, 2, 512], F32))
        pk = ctx.enter_context(nc.psum_tensor("f_pk", [128, 2, 512], F32))
        pf = ctx.enter_context(nc.psum_tensor("f_pf", [128, 2, 512], F32))
        loaded, absed = sem("loaded"), sem("absed")
        net_mm, arg_made, red, sine = sem("net_mm"), sem("arg_made"), sem("red"), sem("sine")
        decayed, shifted, tap_mm, tap_made, biased = sem("decayed"), sem("shifted"), sem("tap_mm"), sem("tap_made"), sem("biased")
        dft_mm, dft_re, dft_im, zeroed, negated = sem("dft_mm"), sem("dft_re"), sem("dft_im"), sem("zeroed"), sem("negated")
        stored = sem("stored")
        NB = KH // JB
        with nc.Block() as block:

            @block.sync
            def _(sp):
                def whole(dst, src):
                    sp.dma_start(dst, src).then_inc(loaded, 16)
                whole(z[:], d["z"])
                whole(w1T[:], d["W1T"])
                whole(w2T[:], d["W2T"])
                whole(w3T[:], d["W3T"])
                for n, name in enumerate(("b1", "f1", "b2", "f2")):
                    whole(vec[:, n:n + 1], d[name])
                whole(dist[:], d["distance_map"])
                for n, name in enumerate(("deltas", "shift", "bias")):
                    v = d[name]
                    whole(chan[:, n, :], bass.AP(tensor=v.tensor, offset=v.offset, ap=[[0, KH], [1, C]]))
                whole(centre[:], d["k_centre"])
                whole(taps_dft[:], d["k_taps"])
                for m in range(2):
                    sp.wait_ge(dft_re, NB * (m + 1))
                    sp.wait_ge(dft_im, NB * (m + 1))
                    sp.wait_ge(negated, NB * (m + 1))
                    sp.wait_ge(zeroed, 2)
                    sp.dma_start(khat[HC * m:HC * m + HC].rearrange("c a n -> c (a n)"),
                                 kf[:].rearrange("c a e u -> c (a e u)")).then_inc(stored, 16)
                sp.wait_ge(stored, 32)

            LOADS = 14 * 16

            @block.tensor
            def _(pe):
                pe.wait_ge(loaded, LOADS)
                for layer in range(2):
                    lhs, rhs = ((w1T, z), (w2T, h1))[layer]
                    if layer:
                        pe.wait_ge(sine, NCH)
                    for n, (a, b) in enumerate(chunks):
                        g = layer * NCH + n
                        if g >= 2:
                            pe.wait_ge(arg_made, g - 1)
                        pe.matmul(pnet[0:FORD, g % 2, 0:b - a], lhs[:], rhs[:, a:b],
                                  start=True, stop=True).then_inc(net_mm, 1)
                pe.wait_ge(sine, 2 * NCH)
                cols = h1[:].rearrange("p (i j) -> p j i", j=KH)
                for g in range((KH + 1) // 2):
                    if g >= 2:
                        pe.wait_ge(tap_made, g - 1)
                    for j in range(2 * g, min(2 * g + 2, KH)):
                        mm = pe.matmul(pk[0:KH, g % 2, C * (j % 2):C * (j % 2) + C], cols[:, j, :], w3T[:],
                                       start=True, stop=True)
                    mm.then_inc(tap_mm, 1)
                pe.wait_ge(biased, 1)
                for m in range(2):
                    for g in range(NB):
                        n = m * NB + g
                        if n >= 2:
                            pe.wait_ge(dft_re, n - 1)
                            pe.wait_ge(dft_im, n - 1)
                        for j in range(JB):
                            mm = pe.matmul(pf[0:HC, n % 2, 2 * U * j:2 * U * j + 2 * U],
                                           k[:, KH - 1 - (JB * g + j), HC * m:HC * m + HC], taps_dft[:],
                                           start=True, stop=True)
                        mm.then_inc(dft_mm, 1)

            @block.scalar
            def _(act):
                act.wait_ge(loaded, LOADS)
                nc.scalar.activation(absd[:], chan[:, 0, :], ACT.Abs).then_inc(absed, 1)
                act.wait_ge(absed, 2)
                for j in range(KH):
                    e = nc.scalar.activation(k[:, j, :], absd[:], ACT.Exp, scale=ndist[:, j:j + 1])
                e.then_inc(decayed, 1)
                for g in range(2 * NCH):
                    a, b = chunks[g % NCH]
                    act.wait_ge(red, 5 * g + 5)
                    nc.scalar.activation(h1[:, a:b], arg[:, a:b], ACT.Sin).then_inc(sine, 1)
                for n in range(2 * NB):
                    m, g = divmod(n, NB)
                    act.wait_ge(dft_mm, n + 1)
                    if n == 0:
                        act.wait_ge(zeroed, 2)
                    if n == NB:
                        act.wait_ge(stored, 16)
                    src = pf[0:HC, n % 2, 0:2 * U * JB].rearrange("p (j r u) -> p r j u", j=JB, r=2)
                    e0 = W - 1 - MID + JB * g
                    nc.scalar.activation(kf[:, 0, e0:e0 + JB, :], src[:, 0], ACT.Copy).then_inc(dft_re, 1)
                    nc.scalar.activation(kf[:, 1, e0:e0 + JB, :], src[:, 1], ACT.Copy).then_inc(dft_im, 1)

            @block.gpsimd
            def _(pool):
                lo = W - 1 - MID
                for a in range(3):
                    x = pool.memset(kf[:, a, 0:lo, :], 0.0)
                x.then_inc(zeroed, 1)
                for a in range(3):
                    x = pool.memset(kf[:, a, lo + KH:NE, :], 0.0)
                x.then_inc(zeroed, 1)

            @block.vector
            def _(dve):
                dve.wait_ge(loaded, LOADS)
                nc.vector.tensor_scalar(ndist[:], dist[:], -1.0, None, ALU.mult).then_inc(absed, 1)
                for g in range(2 * NCH):
                    layer, n = divmod(g, NCH)
                    a, b = chunks[n]
                    x, t = arg[:, a:b], turns[:, a:b]
                    bcol, fcol = vec[:, 2 * layer:2 * layer + 1], vec[:, 2 * layer + 1:2 * layer + 2]
                    dve.wait_ge(net_mm, g + 1)
                    if layer:
                        dve.wait_ge(sine, n + 1)
                    nc.vector.tensor_scalar(x, pnet[0:FORD, g % 2, 0:b - a], bcol, fcol, ALU.add, ALU.mult)\
                        .then_inc(arg_made, 1)
                    dve.wait_ge(arg_made, g + 1)
                    nc.vector.tensor_scalar(t, x, INV2PI, ROUND, ALU.mult, ALU.add).then_inc(red, 1)
                    dve.wait_ge(red, 5 * g + 1)
                    nc.vector.tensor_scalar(t, t, ROUND, None, ALU.subtract).then_inc(red, 1)
                    dve.wait_ge(red, 5 * g + 2)
                    nc.vector.scalar_tensor_tensor(x, t, -TWO_PI_HI, x, ALU.mult, ALU.add).then_inc(red, 1)
                    dve.wait_ge(red, 5 * g + 3)
                    nc.vector.scalar_tensor_tensor(x, t, -TWO_PI_LO, x, ALU.mult, ALU.add).then_inc(red, 1)
                    dve.wait_ge(red, 5 * g + 4)
                    nc.vector.tensor_scalar(x, x, PI_IN, -PI_IN, ALU.min, ALU.max).then_inc(red, 1)
                dve.wait_ge(decayed, 1)
                shift = chan[:, 1:2, :].broadcast_to([KH, KH, C])
                nc.vector.tensor_tensor(k[:], k[:], shift, ALU.add).then_inc(shifted, 1)
                dve.wait_ge(shifted, 1)
                for g in range((KH + 1) // 2):
                    js = slice(2 * g, min(2 * g + 2, KH))
                    n = js.stop - js.start
                    dve.wait_ge(tap_mm, g + 1)
                    nc.vector.tensor_tensor(k[:, js, :], k[:, js, :],
                                            pk[0:KH, g % 2, 0:C * n].rearrange("p (j c) -> p j c", j=n),
                                            ALU.mult).then_inc(tap_made, 1)
                dve.wait_ge(tap_made, (KH + 1) // 2)
                nc.vector.scalar_tensor_tensor(k[:, MID, :], chan[:, 2, :], centre[:, 0:1], k[:, MID, :],
                                               ALU.mult, ALU.add).then_inc(biased, 1)
                for n in range(2 * NB):
                    m, g = divmod(n, NB)
                    dve.wait_ge(dft_im, n + 1)
                    if n == 0:
                        dve.wait_ge(zeroed, 2)
                    e0 = W - 1 - MID + JB * g
                    nc.vector.tensor_scalar(kf[:, 2, e0:e0 + JB, :], kf[:, 1, e0:e0 + JB, :], -1.0, None,
                                            ALU.mult).then_inc(negated, 1)


def convolution(nc, d, khat, x1, rsum, groups=GROUPS):
    IT = groups // 2
    CI = 2 * CG
    NA, NBU, NT, ND = len(A_UNITS) * CI, B_UNITS * CI, T_UNITS * CI, D_UNITS * CI
    RING = 4 * T_MM
    STAT_CH = {1: range(0, 11), 2: range(11, 22), 3: range(22, 32)}
    with ExitStack() as ctx:
        sb = lambda n, s: ctx.enter_context(nc.sbuf_tensor("c_" + n, s, F32))
        ps = lambda n: ctx.enter_context(nc.psum_tensor("c_" + n, [128, 2, 512], F32))
        sem = lambda n: ctx.enter_context(nc.semaphore("c_" + n))
        x = sb("x", [128, 2, CG, HB, W])
        xn = sb("xn", [128, CG, HB, WP])
        xhat = sb("xhat", [128, 2 * U, HB])
        toep = sb("toep", [128, 2, 2, W, U])
        prod = sb("prod", [2 * W, HB, 2, U])
        prodT = sb("prodT", [2 * U, RING, 2, W])
        fwd = sb("fwd", [KP, 4 * U])
        inv = sb("inv", [2 * U, 2, KP])
        eye = sb("eye", [128, 128])
        mean = sb("mean", [KP, KP])
        stats = sb("stats", [KP, HB, 6])
        part = sb("part", [KP, 4, HB])
        q = sb("q", [KP, 2, HB])
        mv = sb("mv", [KP, 4, HB])
        scale, shift = part[:, 0, :], part[:, 1, :]
        rs = sb("rs", [KP, CI, 2, HB])
        square = sb("square", [KP, HB // 2, W])
        pa, pb, pt, pd = ps("pa"), ps("pb"), ps("pt"), ps("pd")
        const_in, cleared = sem("const_in"), sem("cleared")
        x_in = [sem("x_in0"), sem("x_in1")]
        toep_in = [sem("toep_in0"), sem("toep_in1")]
        a_mm, a_act, a_dve = sem("a_mm"), sem("a_act"), sem("a_dve")
        b_mm, b_act = sem("b_mm"), sem("b_act")
        t_mm, t_act, t_dve = sem("t_mm"), sem("t_act"), sem("t_dve")
        d_mm, d_dve = sem("d_mm"), sem("d_dve")
        st, q_made, mean_mm, mv_read, var_made, std_made, sc = (
            sem("st"), sem("q_made"), sem("mean_mm"), sem("mv_read"), sem("var_made"), sem("std_made"), sem("sc"))
        normed, summed, squared, sq_summed = sem("normed"), sem("summed"), sem("squared"), sem("sq_summed")
        stored = [sem("stored0"), sem("stored1")]

        with nc.Block() as block:

            @block.sync
            def _(sp):
                for dst, name in ((fwd[:], "k_fwd"), (inv[:].rearrange("p r h -> p (r h)"), "k_inv"),
                                  (eye[:], "k_eye"), (mean[:], "k_mean")):
                    sp.dma_start(dst, d[name]).then_inc(const_in, 16)
                sp.wait_ge(cleared, 3)

                def load_x(slot, c, channel):
                    for p in range(2):
                        sp.dma_start(x[HALF * p:HALF * p + H, slot, c, :, :], d["x"][channel, p])\
                            .then_inc(x_in[slot], 16)

                def load_toep(par, channel):
                    for p, r, a in ((0, 0, 0), (0, 1, 1), (1, 0, 2), (1, 1, 0)):
                        src = khat[channel, a, 0:W * U]
                        src = bass.AP(tensor=src.tensor, offset=src.offset, ap=[[U, W], [1, W * U]])
                        sp.dma_start(toep[HALF * p:HALF * p + W, par, r, :, :].rearrange("w v u -> w (v u)"), src)\
                            .then_inc(toep_in[par], 16)

                def step(it, n, last):
                    s, c = divmod(n, CG)
                    channel = it * CI + n
                    sp.wait_ge(summed, it * CI + n + 1)
                    sp.wait_ge(sq_summed, (it * CI + n) * 2 + 3)
                    for p in range(2):
                        sp.dma_start(x1[HB * p:HB * p + HB, channel].rearrange("b h w -> h b w"),
                                     x[HALF * p:HALF * p + H, s, c, :, :]).then_inc(stored[n % 2], 16)
                        sp.dma_start(rsum[channel, :, p].rearrange("a h b -> h a b"), rs[HALF * p:HALF * p + H, n])\
                            .then_inc(stored[n % 2], 16)
                    if not last or n + 2 < CI:
                        load_toep(n % 2, channel + 2)
                    if not last and n > 0:
                        refill(it, n - 1)
                    if not last and n == CI - 1:
                        refill(it, n)

                def refill(it, n):
                    s, c = divmod(n, CG)
                    sp.wait_ge(stored[n % 2], 64 * (it * (CI // 2) + n // 2 + 1))
                    load_x(s, c, it * CI + n + CI)

                for s in range(2):
                    for c in range(CG):
                        load_x(s, c, s * CG + c)
                    if s == 0:
                        load_toep(0, 0)
                        load_toep(1, 1)
                if IT > 1:
                    with sp.Fori(0, IT - 1) as it:
                        for n in range(CI):
                            step(it, n, False)
                for n in range(CI):
                    step(IT - 1, n, True)
                for s in range(2):
                    sp.wait_ge(stored[s], 64 * IT * (CI // 2))

            @block.gpsimd
            def _(pool):
                pool.memset(x[32:64, 0], 0.0).then_inc(cleared, 1)
                pool.memset(x[32:64, 1], 0.0).then_inc(cleared, 1)
                pool.memset(toep[32:64], 0.0).then_inc(cleared, 1)
                pool.wait_ge(cleared, 3)
                pool.memset(xn[:, :, :, W:WP], 0.0).then_inc(cleared, 1)

            @block.tensor
            def _(pe):
                def forward(it, n):
                    s, c = divmod(n, CG)
                    m = 0
                    for k, size in enumerate(A_UNITS):
                        unit = n * len(A_UNITS) + k
                        pe.wait_ge(a_act, it * NA + unit + 1)
                        pe.wait_ge(a_dve, it * NA + unit + 1)
                        for r in range(size):
                            cols = xn[0:KP, c, 2 * m:2 * m + 2, :].rearrange("p b w -> p (b w)")
                            mm = pe.matmul(pa[:, unit % 2, 4 * U * r:4 * U * r + 4 * U], cols, fwd[:],
                                           start=True, stop=True)
                            m += 1
                        mm.then_inc(a_mm, 1)

                def toeplitz(it, n):
                    pe.wait_ge(toep_in[n % 2], 64 * (it * (CI // 2) + n // 2 + 1))
                    pe.wait_ge(a_act, it * NA + (n + 1) * len(A_UNITS) + 2)
                    pe.wait_ge(a_dve, it * NA + (n + 1) * len(A_UNITS) + 2)
                    by_u = xhat[:].rearrange("p (a u) b -> p u a b", a=2)
                    for k in range(B_UNITS):
                        unit = n * B_UNITS + k
                        pe.wait_ge(b_act, it * NBU + unit + 1)
                        for r in range(B_MM):
                            u = k * B_MM + r
                            mm = pe.matmul(pb[0:2 * W, unit % 2, B * r:B * r + B],
                                           toep[0:KP, n % 2, :, :, u].rearrange("p r v -> p (r v)"),
                                           by_u[0:KP, u], start=True, stop=True)
                        mm.then_inc(b_mm, 1)

                def turn(it, n, k):
                    unit = n * T_UNITS + k
                    if k == 0:
                        pe.wait_ge(b_act, it * NBU + (n + 1) * B_UNITS + 2)
                    if unit % 2 == 0:
                        pe.wait_ge(t_act, it * (NT // 2) + unit // 2 + 1)
                    else:
                        pe.wait_ge(t_dve, it * (NT // 2) + unit // 2 + 1)
                    for r in range(T_MM):
                        mm = pe.transpose(pt[0:2 * U, unit % 2, 2 * W * r:2 * W * r + 2 * W],
                                          prod[:, T_MM * k + r].rearrange("p a u -> p (a u)"), eye[0:2 * W, 0:2 * W])
                    mm.then_inc(t_mm, 1)

                def inverse(it, n, k):
                    unit = n * D_UNITS + k
                    pe.wait_ge(d_dve, it * ND + unit + 1)
                    pe.wait_ge(t_act, it * (NT // 2) + (n * T_UNITS + 2 * k) // 2 + 2)
                    pe.wait_ge(t_dve, it * (NT // 2) + (n * T_UNITS + 2 * k) // 2 + 2)
                    for r in range(2):
                        mm = pe.matmul(pd[0:KP, unit % 2, 0:D_BQ * W], inv[:, r, :],
                                       prodT[:, D_BQ * k % RING:D_BQ * k % RING + D_BQ, r, :], start=(r == 0), stop=(r == 1))
                    mm.then_inc(d_mm, 1)

                def group_mean(count):
                    pe.wait_ge(q_made, count)
                    pe.matmul(pd[0:KP, 0, 0:2 * HB], mean[:], q[:].rearrange("p a b -> p (a b)"),
                              start=True, stop=True).then_inc(mean_mm, 1)

                def channels(it, last):
                    for s in range(2):
                        more = not (last and s == 1)
                        pe.wait_ge(normed, it * 2 + s + 1)
                        forward(it, s * CG)
                        for c in range(CG):
                            n = s * CG + c
                            toeplitz(it, n)
                            if c == CG - 2 and more:
                                pe.wait_ge(d_dve, it * ND + n * D_UNITS + 2)
                                group_mean(it * 2 + s + 2)
                            if c < CG - 1:
                                forward(it, n + 1)
                            if c == CG - 2 and more:
                                pe.wait_ge(mv_read, it * 2 + s + 2)
                            for k in range(T_UNITS):
                                turn(it, n, k)
                                if k >= 3 and k % 2 == 1:
                                    inverse(it, n, k // 2 - 1)
                            inverse(it, n, D_UNITS - 1)

                pe.wait_ge(const_in, 64)
                pe.wait_ge(cleared, 4)
                group_mean(1)
                pe.wait_ge(mv_read, 1)
                if IT > 1:
                    with pe.Fori(0, IT - 1) as it:
                        channels(it, False)
                channels(IT - 1, True)

            @block.scalar
            def _(act):
                def std(count):
                    act.wait_ge(var_made, count)
                    nc.scalar.activation(mv[:, 3, :], mv[:, 2, :], ACT.Sqrt).then_inc(std_made, 1)

                def forward_out(it, n):
                    for k, size in enumerate(A_UNITS):
                        unit = n * len(A_UNITS) + k
                        act.wait_ge(a_mm, it * NA + unit + 1)
                        copy_xhat(nc.scalar, 0, unit, k, size).then_inc(a_act, 1)

                def copy_xhat(eng, j, unit, k, size):
                    m0 = sum(A_UNITS[:k])
                    for r in range(2):
                        src = pa[HALF * j:HALF * j + 64, unit % 2, 0:4 * U * size]\
                            .rearrange("p (m r u) -> p r m u", m=size, r=2)[:, r]
                        dst = xhat[64 * r:64 * r + 64].rearrange("p u (m j) -> p j m u", j=2)[:, j, m0:m0 + size]
                        ins = eng.activation(dst, src, ACT.Copy)
                    return ins

                def product_out(it, n):
                    for k in range(B_UNITS):
                        unit = n * B_UNITS + k
                        act.wait_ge(b_mm, it * NBU + unit + 1)
                        nc.scalar.activation(
                            prod[:].rearrange("p b a u -> p u a b")[:, B_MM * k:B_MM * k + B_MM],
                            pb[0:2 * W, unit % 2, 0:B_MM * B].rearrange("p (u a b) -> p u a b", a=2, b=HB), ACT.Copy)\
                            .then_inc(b_act, 1)

                def turn_out(it, n, k):
                    unit = n * T_UNITS + k
                    act.wait_ge(t_mm, it * NT + unit + 1)
                    nc.scalar.activation(
                        prodT[:, T_MM * k % RING:T_MM * k % RING + T_MM].rearrange("p b r v -> p (b r v)"),
                        pt[0:2 * U, unit % 2, 0:T_MM * 2 * W], ACT.Copy).then_inc(t_act, 1)

                def squares(it, n, k):
                    s, c = divmod(n, CG)
                    act.wait_ge(sq_summed, (it * CI + n) * 2 + k + 1)
                    act.wait_ge(d_dve, it * ND + n * D_UNITS + 2 * k + 2 + 2)
                    nc.scalar.activation(square[:], x[0:KP, s, c, HB // 2 * k:HB // 2 * k + HB // 2, :],
                                         ACT.Square).then_inc(squared, 1)

                def channels(it, last):
                    for s in range(2):
                        forward_out(it, s * CG)
                        for c in range(CG):
                            n = s * CG + c
                            product_out(it, n)
                            if c < CG - 1:
                                forward_out(it, n + 1)
                            for k in range(0, T_UNITS, 2):
                                turn_out(it, n, k)
                            for k in range(2):
                                squares(it, n, k)
                            if c == CG - 2 and not (last and s == 1):
                                std(it * 2 + s + 2)

                act.sem_inc(a_act, 2)
                act.sem_inc(b_act, 2)
                act.sem_inc(t_act, 1)
                std(1)
                if IT > 1:
                    with act.Fori(0, IT - 1) as it:
                        channels(it, False)
                channels(IT - 1, True)

            @block.vector
            def _(dve):
                def bn(slot, images):
                    for b in images:
                        ins = nc.vector.bn_stats(stats[:, b, :], x[0:KP, slot, :, b, :])
                    ins.then_inc(st, 1)

                def q_of(count, first):
                    dve.wait_ge(st, 3 * count)
                    me, ve, mo, vo = (stats[:, :, i] for i in (1, 2, 4, 5))
                    if not first:
                        dve.wait_ge(mean_mm, count - 1)
                    nc.vector.tensor_tensor(q[:, 0, :], me, mo, ALU.add).then_inc(sc, 1)
                    nc.vector.tensor_tensor(part[:, 0, :], me, me, ALU.mult).then_inc(sc, 1)
                    nc.vector.tensor_tensor(part[:, 1, :], mo, mo, ALU.mult).then_inc(sc, 1)
                    nc.vector.tensor_tensor(part[:, 2, :], ve, vo, ALU.add).then_inc(sc, 1)
                    dve.wait_ge(sc, 9 * (count - 1) + 4)
                    nc.vector.tensor_tensor(part[:, 3, :], part[:, 0, :], part[:, 1, :], ALU.add).then_inc(sc, 1)
                    dve.wait_ge(sc, 9 * (count - 1) + 5)
                    nc.vector.scalar_tensor_tensor(q[:, 1, :], part[:, 2, :], 2.0 / (CG * W), part[:, 3, :],
                                                   ALU.mult, ALU.add).then_inc(q_made, 1)

                def var_of(count):
                    dve.wait_ge(mean_mm, count)
                    nc.vector.tensor_copy(mv[:, 0:2, :], pd[0:KP, 0, 0:2 * HB].rearrange("p (a b) -> p a b", a=2))\
                        .then_inc(mv_read, 1)
                    dve.wait_ge(mv_read, count)
                    nc.vector.tensor_tensor(part[:, 0, :], mv[:, 0, :], mv[:, 0, :], ALU.mult).then_inc(sc, 1)
                    dve.wait_ge(sc, 9 * (count - 1) + 6)
                    nc.vector.tensor_tensor(part[:, 1, :], mv[:, 1, :], part[:, 0, :], ALU.subtract).then_inc(sc, 1)
                    dve.wait_ge(sc, 9 * (count - 1) + 7)
                    nc.vector.tensor_scalar(mv[:, 2, :], part[:, 1, :], 0.0, EPS, ALU.max, ALU.add)\
                        .then_inc(var_made, 1)

                def normalise(slot, count):
                    dve.wait_ge(std_made, count)
                    nc.vector.reciprocal(scale, mv[:, 3, :]).then_inc(sc, 1)
                    dve.wait_ge(sc, 9 * (count - 1) + 8)
                    nc.vector.scalar_tensor_tensor(shift, mv[:, 0, :], -1.0, scale, ALU.mult, ALU.mult)\
                        .then_inc(sc, 1)
                    dve.wait_ge(sc, 9 * count)
                    for b in range(HB):
                        ins = nc.vector.tensor_scalar(xn[0:KP, :, b, 0:W], x[0:KP, slot, :, b, :],
                                                      scale[:, b:b + 1], shift[:, b:b + 1], ALU.mult, ALU.add)
                    ins.then_inc(normed, 1)

                def forward_out(it, n):
                    for k, size in enumerate(A_UNITS):
                        unit = n * len(A_UNITS) + k
                        dve.wait_ge(a_mm, it * NA + unit + 1)
                        m0 = sum(A_UNITS[:k])
                        for r in range(2):
                            src = pa[HALF:HALF + 64, unit % 2, 0:4 * U * size]\
                                .rearrange("p (m r u) -> p r m u", m=size, r=2)[:, r]
                            dst = xhat[64 * r:64 * r + 64].rearrange("p u (m j) -> p j m u", j=2)[:, 1, m0:m0 + size]
                            ins = nc.vector.tensor_copy(dst, src)
                        ins.then_inc(a_dve, 1)

                def turn_out(it, n, k):
                    unit = n * T_UNITS + k
                    dve.wait_ge(t_mm, it * NT + unit + 1)
                    nc.vector.tensor_copy(
                        prodT[:, T_MM * k % RING:T_MM * k % RING + T_MM].rearrange("p b r v -> p (b r v)"),
                        pt[0:2 * U, unit % 2, 0:T_MM * 2 * W]).then_inc(t_dve, 1)

                def inverse_out(it, n, k):
                    s, c = divmod(n, CG)
                    unit = n * D_UNITS + k
                    dve.wait_ge(d_mm, it * ND + unit + 1)
                    rows = x[0:KP, s, c, D_BQ * k:D_BQ * k + D_BQ, :]
                    y = pd[0:KP, unit % 2, 0:D_BQ * W].rearrange("p (b w) -> p b w", w=W)[:, :, ::-1]
                    nc.vector.tensor_tensor(rows, y, rows, ALU.add)\
                        .then_inc(d_dve, 1)

                def sums(it, n):
                    s, c = divmod(n, CG)
                    dve.wait_ge(d_dve, it * ND + (n + 1) * D_UNITS + 2)
                    nc.vector.reduce_sum(rs[:, n, 0, :], x[0:KP, s, c], AX.X).then_inc(summed, 1)

                def square_sums(it, n, k):
                    dve.wait_ge(squared, (it * CI + n) * 2 + k + 1)
                    nc.vector.reduce_sum(rs[:, n, 1, HB // 2 * k:HB // 2 * k + HB // 2], square[:], AX.X)\
                        .then_inc(sq_summed, 1)

                def channels(it, last):
                    for s in range(2):
                        done = it * 2 + s + 1
                        more = not (last and s == 1)
                        forward_out(it, s * CG)
                        for c in range(CG):
                            n = s * CG + c
                            if c in STAT_CH and more:
                                if c == 1:
                                    dve.wait_ge(x_in[1 - s], 32 * CG * (it + 1 + s))
                                bn(1 - s, STAT_CH[c])
                            if c == CG - 2 and more:
                                q_of(done + 1, False)
                            if c == CG - 1 and more:
                                normalise(1 - s, done + 1)
                            if c < CG - 1:
                                forward_out(it, n + 1)
                            if c == CG - 2 and more:
                                var_of(done + 1)
                            for k in range(1, T_UNITS, 2):
                                turn_out(it, n, k)
                                if k >= 3:
                                    inverse_out(it, n, k // 2 - 1)
                            inverse_out(it, n, D_UNITS - 1)
                            sums(it, n)
                            for k in range(2):
                                square_sums(it, n, k)

                dve.sem_inc(a_dve, 2)
                dve.sem_inc(sq_summed, 1)
                dve.sem_inc(t_dve, 1)
                dve.sem_inc(d_dve, 2)
                dve.wait_ge(cleared, 4)
                dve.wait_ge(x_in[0], 32 * CG)
                for images in STAT_CH.values():
                    bn(0, images)
                q_of(1, True)
                var_of(1)
                normalise(0, 1)
                if IT > 1:
                    with dve.Fori(0, IT - 1) as it:
                        channels(it, False)
                channels(IT - 1, True)


def attention(nc, d, x1, rsum, y, images=B):
    HEADS, DH, NMEM, REP = 4, 32, 4, 160
    HID = HEADS * DH
    SCALE = DH ** -0.5
    PX = 2 * W
    BLOCKS = H * W // PX
    BC, BC_BLOCKS = 7, 4
    ROWS = BC_BLOCKS * PX // W
    KEYS = 68
    MEM = HALF
    N = ROWS * W
    FOURS = images // 4
    with ExitStack() as ctx:
        sb = lambda n, s: ctx.enter_context(nc.sbuf_tensor("t_" + n, s, F32))
        ps = lambda n, k=1: ctx.enter_context(nc.psum_tensor("t_" + n, [128, k, 512], F32))
        sem = lambda n: ctx.enter_context(nc.semaphore("t_" + n))
        x = sb("x", [HC, 4, 2, H, W])
        sq = sb("sq", [HC, 2, H * W])
        xw = sb("xw", [HC, 2, H, W])
        spread = sb("spread", [PX, BLOCKS, PX])
        sums = sb("sums", [HC, 2, 2, H, HB])
        squares = x[:, 2:4].rearrange("p k m h w -> p (k m h w)")[:, 0:4 * H * HB]\
            .rearrange("p (m g h q) -> p m g h q", m=2, g=2, h=H)
        stat = sb("stat", [HC, 4, 2, B])
        cols = sb("cols", [HC, 4, 4, 2])
        raw = sb("raw", [HC, 2, 2, W])
        feat = sb("feat", [HC, 2, 2, W])
        vraw = sb("vraw", [HC, 2, 2, W])
        vfeat = vraw
        fn = sb("fn", [HID, 2 * W])
        Q = sb("Q", [HID, 2, W])
        K = sb("K", [HID, 2, HEADS, KEYS])
        E = sb("E", [W, 2, HEADS, KEYS])
        zs = sb("zs", [W, 5, 2 * HEADS])
        ET_fsq = sb("ET_fsq", [128, 2 * HEADS * W])
        ET = ET_fsq[0:KEYS].rearrange("p (t h w) -> p t h w", t=2, h=HEADS)
        fsq = ET_fsq[0:HC, 0:4 * W].rearrange("p (m t w) -> p m t w", m=2, t=2)
        V = sb("V", [KEYS, 2, HID])
        O = Q
        term = sb("term", [HC, 2, 2, 2, W])
        nrm = sb("nrm", [PX, BLOCKS])
        wq, wk, wv = (sb(n, [HC, 2, HID]) for n in ("wq", "wk", "wv"))
        gains = sb("gains", [HC, 3, 2])
        first = xw[:].rearrange("p m h w -> p (m h w)")
        wo = first[:, 0:2 * HID].rearrange("p (m c) -> p m c", m=2)
        wr = first[:, 256:256 + 4 * C].rearrange("p (m t c) -> p m t c", m=2, t=2)
        tot = first[:, 1024:1024 + 4 * B].rearrange("p (a m b) -> p a m b", a=2, m=2)
        gmean = first[:, 1280:1280 + HC]
        var = first[:, 1376:1376 + 2 * B].rearrange("p (m b) -> p m b", m=2)
        bo = first[:, 1504:1506]
        wc = sb("wc", [HID, 2, C])
        bias = sb("bias", [HC, 2, 2])
        eye = sb("eye", [128, 128])
        ones = sb("ones", [128, 128])
        pn, pbc, pcs, pq, psc, pt = ps("pn"), ps("pbc", 2), ps("pcs"), ps("pq"), ps("psc", 2), ps("pt")
        names = """w_in k_in v_in sum_in cleared scaled gm_mm tots gm_copy v1 v2 v3 v4 v5 v6 wc_mm wc_made
            sqd n2_mm n_sqrt n_max n_inv spread_made bc_mm weighted cs_mm cs_made row_made col_made fetched
            f_made fsq_made fn_mm fn_sqrt fn_max fn_inv qk_mm qk_made s_mm mx_made s_sub e_made z_k z_m z_made z_inv
            e_norm t_mm et_made v_mm v_made o_mm o_made term_mm term_made row_added added v_ready rows_in""".split()
        S = {n: sem(n) for n in names}
        x_in = [sem(f"x_in{k}") for k in range(4)]
        stored = [sem(f"stored{k}") for k in range(4)]

        def wait(eng, name, value):
            if not (isinstance(value, int) and value <= 0):
                eng.wait_ge(S[name], value)

        def schedule(eng, step):
            step(0, -1, True, False, False)
            step(0, 0, True, True, False)
            passes = (images - 2) // 4
            if passes:
                with eng.Fori(0, passes) as it:
                    for j in range(1, 5):
                        step(it, j, True, True, True)
            for j in range(4 * passes + 1, images + 1):
                step(0, j, j + 1 < images, j < images, True)

        with nc.Block() as block:

            @block.sync
            def _(sp):
                for dst, src, s in (
                        (wq[:], d["WqT"], "w_in"), (wk[:], d["WkT"], "w_in"), (wv[:], d["WvT"], "w_in"),
                        (wo, d["Wo"], "w_in"), (wr, d["WrT"], "w_in"), (bo, d["bo"], "w_in"),
                        (gains[:], d["gains"], "w_in"), (eye[:], d["k_eye"], "w_in"), (gmean, d["k_gmean"], "w_in")):
                    sp.dma_start(dst, src).then_inc(S[s], 16)
                for m in range(2):
                    for dst, a in ((sums, 0), (squares, 1)):
                        sp.dma_start(dst[:, m], rsum[HC * m:HC * m + HC, a]).then_inc(S["sum_in"], 16)
                sp.wait_ge(S["cleared"], 4)
                for t in range(2):
                    for j in range(3):
                        for h in range(HEADS):
                            sp.dma_start(K[DH * h:DH * h + DH, t, h, W + NMEM * j:W + NMEM * j + NMEM],
                                         d["mem_kT"][h]).then_inc(S["k_in"], 16)
                    sp.dma_start(V[MEM:MEM + NMEM, t, :], d["mem_v"]).then_inc(S["v_in"], 16)

                def where(four, k):
                    return HB * (k // 2) + four * 2 + k % 2

                def load(four, k):
                    sp.dma_start(x[:, k], x1[where(four, k)].rearrange("(m p) h w -> p m h w", p=HC))\
                        .then_inc(x_in[k], 16)

                def store(four, k):
                    sp.dma_start(y[where(four, k)].rearrange("(m p) h w -> p m h w", p=HC), x[:, k])\
                        .then_inc(stored[k], 16)

                for k in range(4):
                    if k == 2:
                        sp.wait_ge(S["tots"], 2)
                    load(0, k)
                fours = FOURS
                if fours > 1:
                    with sp.Fori(0, fours - 1) as it:
                        for k in range(4):
                            sp.wait_ge(S["added"], it * 4 + k + 3)
                            store(it, k)
                            sp.wait_ge(stored[k], it * 16 + 16)
                            load(it + 1, k)
                for k in range(4):
                    sp.wait_ge(S["added"], (fours - 1) * 4 + k + 3)
                    store(fours - 1, k)
                for k in range(4):
                    sp.wait_ge(stored[k], 16 * fours)

            @block.gpsimd
            def _(pool):
                pool.sem_inc(S["added"], 2)
                pool.memset(K[:], 0.0).then_inc(S["cleared"], 1)
                pool.memset(ones[:], 1.0).then_inc(S["cleared"], 1)
                pool.memset(bias[:], 0.0).then_inc(S["cleared"], 1)
                pool.memset(V[:], 0.0).then_inc(S["cleared"], 1)

                def step(it, j, norms, weigh, attend):
                    if attend:
                        i, slot = it * 4 + (j - 1), (j - 1) % 4
                        wait(pool, "term_made", i + 2)
                        nc.gpsimd.tensor_tensor(
                            x[:, slot], x[:, slot],
                            term[:, slot % 2, 0].rearrange("p m (h a) -> p m h a", a=1).broadcast_to([HC, 2, H, W]), ALU.add)\
                            .then_inc(S["row_added"], 1)
                        wait(pool, "row_added", i + 1)
                        nc.gpsimd.tensor_tensor(
                            x[:, slot], x[:, slot],
                            term[:, slot % 2, 1].rearrange("p m (a w) -> p m a w", a=1).broadcast_to([HC, 2, H, W]), ALU.add)\
                            .then_inc(S["added"], 1)
                schedule(pool, step)

            @block.tensor
            def _(pe):
                def before():
                    pe.wait_ge(S["w_in"], 9 * 16)
                    pe.wait_ge(S["cleared"], 4)
                    pe.wait_ge(S["tots"], 2)
                    pe.matmul(pq[0:HC, 0, 0:4 * B], gmean, tot.rearrange("p a m b -> p (a m b)"),
                              start=True, stop=True).then_inc(S["gm_mm"], 1)
                    for t in range(2):
                        for m in range(2):
                            pe.matmul(psc[0:HID, t, 0:C], wo[:, m, :], wr[:, m, t, :], start=(m == 0), stop=(m == 1))
                    for o in range(2):
                        for t in range(2):
                            for m in range(2):
                                mm = pe.matmul(pt[0:HC, 0, o:o + 1], wr[:, m, t, HC * o:HC * o + HC], bo[:, m:m + 1],
                                               start=(t + m == 0), stop=(t + m == 2))
                    mm.then_inc(S["wc_mm"], 1)
                    pe.wait_ge(S["scaled"], 3)
                    pe.wait_ge(S["wc_made"], 3)
                    pe.wait_ge(S["gm_copy"], 1)
                    pe.wait_ge(S["k_in"], 16 * 24)
                    pe.wait_ge(S["v_in"], 16 * 2)

                def colsum(i, slot, m):
                    wait(pe, "cs_made", i * 2 + m)
                    for g in range(H // ROWS):
                        mm = pe.matmul(pcs[0:HC, 0, 0:N], eye[0:HC, 0:HC],
                                       x[:, slot, m, ROWS * g:ROWS * g + ROWS, :].rearrange("p h w -> p (h w)"),
                                       start=(g == 0), stop=(g == H // ROWS - 1))
                    mm.then_inc(S["cs_mm"], 1)

                def bc(n, j, g):
                    wait(pe, "weighted", n * BC + (g - 1))
                    pe.matmul(pbc[0:HC, (j + g) % 2, 0:N], ones[0:PX, 0:HC],
                              spread[:, BC_BLOCKS * g:BC_BLOCKS * g + BC_BLOCKS, :].rearrange("p a b -> p (a b)"),
                              start=True, stop=True).then_inc(S["bc_mm"], 1)

                def norms2(i, b0, b1):
                    for b in range(b0, b1):
                        for m in range(2):
                            mm = pe.matmul(pn[0:PX, 0, b:b + 1], sq[:, m, PX * b:PX * b + PX], ones[0:HC, 0:1],
                                           start=(m == 0), stop=(m == 1))
                    if b1 == BLOCKS:
                        mm.then_inc(S["n2_mm"], 1)

                def step(it, j, norms, weigh, attend):
                    n, i = it * 4 + j, it * 4 + (j - 1)
                    k = j % 4
                    if weigh:
                        wait(pe, "spread_made", n + 1)
                        bc(n, j, 0)
                        bc(n, j, 1)
                    if attend:
                        wait(pe, "fsq_made", i + 1)
                        for m in range(2):
                            mm = pe.matmul(pt[0:HID, 0, 0:2 * W], ones[0:HC, :], fsq[:, m].rearrange("p t w -> p (t w)"),
                                           start=(m == 0), stop=(m == 1))
                        mm.then_inc(S["fn_mm"], 1)
                        for a, w in enumerate((wq, wk)):
                            for m in range(2):
                                mm = pe.matmul(pqk(a), w[:, m, :], feat[:, m].rearrange("p t w -> p (t w)"),
                                               start=(m == 0), stop=(m == 1))
                        mm.then_inc(S["qk_mm"], 1)
                    if weigh:
                        bc(n, j, 2)
                        bc(n, j, 3)
                        colsum(n, k, 0)
                    if attend:
                        wait(pe, "qk_made", i * 5 + 5)
                        wait(pe, "term_made", i + 1)
                        for t in range(2):
                            mm = pe.matmul(psc[0:W, t, 0:HEADS * KEYS], Q[:, t, :],
                                           K[:, 1 - t].rearrange("p h j -> p (h j)"), start=True, stop=True)
                        mm.then_inc(S["s_mm"], 1)
                        wait(pe, "v_ready", i + 1)
                        for t in range(2):
                            for m in range(2):
                                mm = pe.matmul(pq[0:W, 0, HID * t:HID * t + HID], vfeat[:, m, 1 - t, :], wv[:, m, :],
                                               start=(m == 0), stop=(m == 1))
                        mm.then_inc(S["v_mm"], 1)
                    if weigh:
                        for g in range(4, BC):
                            bc(n, j, g)
                        colsum(n, k, 1)
                    if norms:
                        wait(pe, "sqd", n * 2 + 4)
                        wait(pe, "n_sqrt", n + 1)
                        norms2(n + 1, 0, BLOCKS // 2 - 1)
                    if attend:
                        wait(pe, "e_norm", i + 1)
                    if norms:
                        norms2(n + 1, BLOCKS // 2 - 1, BLOCKS // 2)
                    if attend:
                        for t in range(2):
                            for h in range(HEADS):
                                a = (t * HEADS + h) * W
                                mm = pe.transpose(pt[0:KEYS, 0, a:a + W], E[:, t, h, :], eye[0:W, 0:W])
                        mm.then_inc(S["t_mm"], 1)
                    if norms:
                        norms2(n + 1, BLOCKS // 2, BLOCKS)
                    if attend:
                        wait(pe, "et_made", i + 1)
                        wait(pe, "v_made", i + 1)
                        for h in range(HEADS):
                            for t in range(2):
                                mm = pe.matmul(psc[DH * h:DH * h + DH, 0, W * t:W * t + W], V[:, t, DH * h:DH * h + DH],
                                               ET[:, t, h, :], start=True, stop=True)
                        mm.then_inc(S["o_mm"], 1)
                        wait(pe, "o_made", i + 1)
                        for t in range(2):
                            for m in range(2):
                                a = (t * 2 + m) * W
                                mm = pe.matmul(psc[0:HC, 1, a:a + W], wc[:, t, HC * m:HC * m + HC], O[:, t, :],
                                               start=True, stop=True)
                        mm.then_inc(S["term_mm"], 1)

                def pqk(a):
                    return pq[0:HID, 0, 2 * W * (a + 1):2 * W * (a + 2)]

                before()
                schedule(pe, step)

            @block.scalar
            def _(act):
                def before():
                    act.wait_ge(S["v4"], 1)
                    nc.scalar.activation(stat[:, 1], var, ACT.Sqrt).then_inc(S["v5"], 1)
                    act.wait_ge(S["wc_mm"], 1)
                    for t in range(2):
                        nc.scalar.activation(wc[:, t, :], psc[0:HID, t, 0:C], ACT.Copy).then_inc(S["wc_made"], 1)
                    act.wait_ge(S["cleared"], 3)
                    nc.scalar.activation(bias[:, 0, :], pt[0:HC, 0, 0:2], ACT.Copy).then_inc(S["wc_made"], 1)

                def step(it, j, norms, weigh, attend):
                    n, i = it * 4 + j, it * 4 + (j - 1)
                    k = (j + 1) % 4
                    if attend:
                        wait(act, "fn_mm", i + 1)
                        nc.scalar.activation(fn[:], pt[0:HID, 0, 0:2 * W], ACT.Sqrt).then_inc(S["fn_sqrt"], 1)
                    if norms:
                        act.wait_ge(x_in[k], it * 16 + 16 * ((j + 1) // 4 + 1))
                        wait(act, "fetched", n + 2)
                        wait(act, "n2_mm", n + 1)
                        for m in range(2):
                            nc.scalar.activation(sq[:, m, :], x[:, k, m].rearrange("p h w -> p (h w)"),
                                                 ACT.Square, bias=cols[:, k, 1, m:m + 1],
                                                 scale=cols[:, k, 3, m:m + 1]).then_inc(S["sqd"], 1)
                    if attend:
                        wait(act, "v_mm", i + 1)
                        nc.scalar.activation(V[0:W].rearrange("p t c -> p (t c)"), pq[0:W, 0, 0:2 * HID], ACT.Copy)\
                            .then_inc(S["v_made"], 1)
                        wait(act, "s_sub", i + 1)
                        nc.scalar.activation(E[:], E[:], ACT.Exp, scale=SCALE).then_inc(S["e_made"], 1)
                        wait(act, "t_mm", i + 1)
                        nc.scalar.activation(ET_fsq[0:KEYS], pt[0:KEYS, 0, 0:2 * HEADS * W],
                                             ACT.Copy).then_inc(S["et_made"], 1)
                    if norms:
                        wait(act, "n2_mm", n + 2)
                        nc.scalar.activation(nrm[:], pn[0:PX, 0, 0:BLOCKS], ACT.Sqrt).then_inc(S["n_sqrt"], 1)
                    if attend:
                        wait(act, "o_mm", i + 1)
                        nc.scalar.activation(O[:].rearrange("p t w -> p (t w)"), psc[0:HID, 0, 0:2 * W], ACT.Copy)\
                            .then_inc(S["o_made"], 1)

                before()
                schedule(act, step)

            @block.vector
            def _(dve):
                dve.sem_inc(S["term_made"], 1)

                def before():
                    dve.wait_ge(S["w_in"], 9 * 16)
                    root = float(C) ** 0.5
                    for j, w in enumerate((wq, wk, wv)):
                        for m in range(2):
                            ins = nc.vector.tensor_scalar(w[:, m, :], w[:, m, :], gains[:, j, m:m + 1], root,
                                                          ALU.mult, ALU.mult)
                        ins.then_inc(S["scaled"], 1)
                    dve.wait_ge(S["sum_in"], 64)
                    for a in range(2):
                        for m in range(2):
                            ins = nc.vector.reduce_sum(
                                tot[:, a, m, :].rearrange("p (g q) -> p g q", g=2),
                                (sums, squares)[a][:, m].rearrange("p g h q -> p g q h"), AX.X)
                        ins.then_inc(S["tots"], 1)
                    both = lambda a: a.rearrange("p m b -> p (m b)")
                    dve.wait_ge(S["gm_mm"], 1)
                    nc.vector.tensor_scalar(both(stat[:, 2]), pq[0:HC, 0, 0:2 * B], -1.0, None, ALU.mult)\
                        .then_inc(S["v1"], 1)
                    dve.wait_ge(S["v1"], 1)
                    nc.vector.tensor_tensor(both(stat[:, 3]), both(stat[:, 2]), both(stat[:, 2]), ALU.mult)\
                        .then_inc(S["v2"], 1)
                    dve.wait_ge(S["v2"], 1)
                    nc.vector.tensor_tensor(both(var), pq[0:HC, 0, 2 * B:4 * B], both(stat[:, 3]), ALU.subtract)\
                        .then_inc(S["gm_copy"], 1)
                    dve.wait_ge(S["gm_copy"], 1)
                    nc.vector.tensor_scalar(var, var, 0.0, EPS, ALU.max, ALU.add).then_inc(S["v4"], 1)
                    dve.wait_ge(S["v5"], 1)
                    nc.vector.reciprocal(stat[:, 3], stat[:, 1]).then_inc(S["v3"], 1)
                    dve.wait_ge(S["v3"], 1)
                    nc.vector.tensor_scalar(stat[:, 0], stat[:, 3], 1.0 / W, None, ALU.mult).then_inc(S["v6"], 1)
                    nc.vector.tensor_tensor(stat[:, 1], stat[:, 2], stat[:, 3], ALU.mult).then_inc(S["v6"], 1)
                    dve.wait_ge(S["v6"], 2)

                def step(it, j, norms, weigh, attend):
                    n, i = it * 4 + j, it * 4 + (j - 1)
                    k, slot, ahead = j % 4, (j - 1) % 4, (j + 1) % 4

                    def place(offset):
                        r = (j + offset) % 4
                        return r // 2, it * 2 + ((j + offset) // 4 * 2 + r % 2)

                    def weigh_bank(g):
                        wait(dve, "bc_mm", n * BC + (g + 1))
                        for m in range(2):
                            ins = nc.vector.scalar_tensor_tensor(
                                xw[:, m, ROWS * g:ROWS * g + ROWS, :].rearrange("p h w -> p (h w)"),
                                x[:, k, m, ROWS * g:ROWS * g + ROWS, :].rearrange("p h w -> p (h w)"),
                                cols[:, k, 2, m:m + 1], pbc[0:HC, (j + g) % 2, 0:N], ALU.add, ALU.mult)
                        ins.then_inc(S["weighted"], 1)

                    def column_sums(m):
                        wait(dve, "cs_mm", n * 2 + (m + 1))
                        nc.vector.reduce_sum(raw[:, m, 1, :], pcs[0:HC, 0, 0:N].rearrange("p (r w) -> p w r", r=ROWS),
                                             AX.X).then_inc(S["cs_made"], 1)

                    if attend:
                        wait(dve, "cs_made", i * 2 + 2)
                        wait(dve, "col_made", i * 2 + 2)
                        for m in range(2):
                            ins = nc.vector.tensor_scalar(feat[:, m], raw[:, m], cols[:, slot, 0, m:m + 1],
                                                          cols[:, slot, 1, m:m + 1], ALU.mult, ALU.add)
                        ins.then_inc(S["f_made"], 1)
                        wait(dve, "f_made", i + 1)
                        nc.vector.tensor_tensor(fsq, feat[:], feat[:], ALU.mult).then_inc(S["fsq_made"], 1)
                        for m in range(2):
                            ins = nc.vector.tensor_scalar(vfeat[:, m], vraw[:, m], cols[:, slot, 3, m:m + 1], None,
                                                          ALU.mult)
                        ins.then_inc(S["v_ready"], 1)
                    if norms:
                        half, at = place(1)
                        nc.vector.tensor_copy(cols[:, ahead], stat[:, 0:4, :, bass.ds(at + HB * half, 1)]
                                              .rearrange("p a m o -> p a (m o)")).then_inc(S["fetched"], 1)
                    if weigh:
                        half, at = place(0)
                        nc.vector.tensor_copy(raw[:, :, 0, :], sums[:, :, half, :, bass.ds(at, 1)]
                                              .rearrange("p m h o -> p m (h o)")).then_inc(S["rows_in"], 1)
                        wait(dve, "fetched", n + 1)
                        weigh_bank(0)
                        weigh_bank(1)
                    if attend:
                        wait(dve, "fn_sqrt", i + 1)
                        nc.vector.tensor_scalar(fn[:], fn[:], 1e-12, None, ALU.max).then_inc(S["fn_max"], 1)
                        wait(dve, "fn_max", i + 1)
                        nc.vector.reciprocal(fn[:], fn[:]).then_inc(S["fn_inv"], 1)
                        wait(dve, "fn_inv", i + 1)
                        wait(dve, "qk_mm", i + 1)
                        nc.vector.tensor_tensor(Q[:].rearrange("p t w -> p (t w)"), pq[0:HID, 0, 2 * W:4 * W],
                                                fn[:], ALU.mult).then_inc(S["qk_made"], 1)
                        for h in range(HEADS):
                            r = slice(DH * h, DH * h + DH)
                            nc.vector.tensor_tensor(K[r, :, h, 0:W],
                                                    pq[r, 0, 4 * W:6 * W].rearrange("p (t w) -> p t w", t=2),
                                                    fn[r, :].rearrange("p (t w) -> p t w", t=2), ALU.mult)\
                                .then_inc(S["qk_made"], 1)
                    if weigh:
                        weigh_bank(2)
                        weigh_bank(3)
                        column_sums(0)
                    if attend:
                        wait(dve, "s_mm", i + 1)
                        scores = psc[0:W, :, 0:HEADS * KEYS].rearrange("p t (h j) -> p t h j", h=HEADS)
                        over = lambda z: z.rearrange("p (t h o) -> p t h o", t=2, o=1).broadcast_to([W, 2, HEADS, KEYS])
                        nc.vector.reduce_max(zs[:, 0, :].rearrange("p (t h) -> p t h", t=2), scores, AX.X)\
                            .then_inc(S["mx_made"], 1)
                        wait(dve, "mx_made", i + 1)
                        nc.vector.tensor_tensor(E[:], scores, over(zs[:, 0, :]), ALU.subtract).then_inc(S["s_sub"], 1)
                    if weigh:
                        for g in range(4, BC):
                            weigh_bank(g)
                        column_sums(1)
                        wait(dve, "weighted", n * BC + BC)
                        if attend:
                            wait(dve, "v_mm", i + 1)
                        nc.vector.reduce_sum(vraw[:, 0, 0, :], xw[:, 0], AX.X).then_inc(S["col_made"], 0 + 1)
                    if attend:
                        wait(dve, "e_made", i + 1)
                        th = lambda z: z.rearrange("p (t h) -> p t h", t=2)
                        nc.vector.reduce_sum(th(zs[:, 1, :]), E[:, :, :, 0:W], AX.X).then_inc(S["z_k"], 1)
                        nc.vector.reduce_sum(th(zs[:, 2, :]), E[:, :, :, KEYS - NMEM:KEYS], AX.X).then_inc(S["z_m"], 1)
                        wait(dve, "z_m", i + 1)
                        nc.vector.scalar_tensor_tensor(zs[:, 3, :], zs[:, 1, :], float(REP), zs[:, 2, :],
                                                       ALU.mult, ALU.add).then_inc(S["z_made"], 1)
                        wait(dve, "z_made", i + 1)
                        nc.vector.reciprocal(zs[:, 4, :], zs[:, 3, :]).then_inc(S["z_inv"], 1)
                        wait(dve, "z_inv", i + 1)
                        nc.vector.tensor_tensor(E[:], E[:], over(zs[:, 4, :]), ALU.mult).then_inc(S["e_norm"], 1)
                    if weigh:
                        nc.vector.reduce_sum(vraw[:, 1, 0, :], xw[:, 1], AX.X).then_inc(S["row_made"], 1)
                        nc.vector.reduce_sum(vraw[:, 0, 1, :], xw[:, 0].rearrange("p h w -> p w h"), AX.X)\
                            .then_inc(S["row_made"], 1)
                    if norms:
                        wait(dve, "n_sqrt", n + 2)
                        nc.vector.tensor_scalar(nrm[:], nrm[:], 1e-12, None, ALU.max).then_inc(S["n_max"], 1)
                        wait(dve, "n_max", n + 2)
                        nc.vector.reciprocal(nrm[:], nrm[:]).then_inc(S["n_inv"], 1)
                        wait(dve, "n_inv", n + 2)
                        nc.vector.tensor_tensor(
                            spread[:], eye[0:PX, 0:PX].rearrange("p (a q) -> p a q", a=1).broadcast_to([PX, BLOCKS, PX]),
                            nrm[:].rearrange("p (b a) -> p b a", a=1).broadcast_to([PX, BLOCKS, PX]), ALU.mult)\
                            .then_inc(S["spread_made"], 1)
                    if weigh:
                        nc.vector.reduce_sum(vraw[:, 1, 1, :], xw[:, 1].rearrange("p h w -> p w h"), AX.X)\
                            .then_inc(S["col_made"], 1)
                    if attend:
                        wait(dve, "term_mm", i + 1)
                        wait(dve, "added", i + 1)
                        nc.vector.tensor_tensor(
                            term[:, slot % 2],
                            psc[0:HC, 1, 0:4 * W].rearrange("p (t m w) -> p t m w", t=2, m=2),
                            bias[:].rearrange("p t (m o) -> p t m o", o=1).broadcast_to([HC, 2, 2, W]), ALU.add)\
                            .then_inc(S["term_made"], 1)

                before()
                schedule(dve, step)


def laid_out(a):
    t = {n.split("conv_")[-1]: np.asarray(v) for n, v in a.items()}
    out = {
        "x": t["x"].reshape(2, HB, C, H, W).transpose(2, 0, 3, 1, 4),
        "z": t["z"].reshape(FEMB, KH * KH),
        "W1T": t["W1"].T, "W2T": t["W2"].T, "W3T": t["W3"].T,
        "distance_map": t["distance_map"].reshape(KH, KH),
    }
    for n in ("b1", "f1", "b2", "f2"):
        out[n] = t[n].reshape(FORD, 1)
    for n in ("deltas", "shift", "bias"):
        out[n] = t[n].reshape(1, C)
    halves = lambda a: np.moveaxis(a.reshape((2, HC) + a.shape[1:]), 0, 1)
    for n in ("Wq", "Wk", "Wv"):
        out[n + "T"] = halves(t[n].T)
    out["Wo"], out["bo"] = halves(t["Wo"]), halves(t["bo"])
    out["WrT"] = halves(t["Wr"].reshape(C, 2, C).transpose(2, 1, 0))
    out["gains"] = halves(np.stack([t["gq"], t["gk"], t["gv"]], axis=1)).transpose(0, 2, 1)
    out["mem_kT"] = t["mem_kv"][0].transpose(0, 2, 1)
    out["mem_v"] = t["mem_kv"][1].transpose(1, 0, 2).reshape(t["mem_kv"].shape[2], -1)
    return out


def program(nc, d, y):
    khat = nc.dram_tensor("khat", (C, 3, NE * U), F32, kind="Internal").ap()
    x1 = nc.dram_tensor("x1", (B, C, H, W), F32, kind="Internal").ap()
    rsum = nc.dram_tensor("rsum", (C, 2, 2, H, HB), F32, kind="Internal").ap()
    filters(nc, d, khat)
    convolution(nc, d, khat, x1, rsum)
    attention(nc, d, x1, rsum, y)


def kernel(**inputs):
    import concourse.bacc as bacc
    from concourse.bass_utils import run_bass_kernel_spmd

    nc = bacc.Bacc("TRN2", target_bir_lowering=False, num_devices=1)
    arrays, d = {}, {}
    for name, a in {**laid_out(inputs), **constants()}.items():
        arrays[f"in_{name}"] = np.ascontiguousarray(a)
        d[name] = nc.dram_tensor(f"in_{name}", a.shape, F32, kind="ExternalInput").ap()
    y = nc.dram_tensor("out", (B, C, H, W), F32, kind="ExternalOutput").ap()
    program(nc, d, y)
    return run_bass_kernel_spmd(nc, [arrays], core_ids=[0]).results[0]["out"]
```

```python
from contextlib import ExitStack

import numpy as np

import concourse.bass as bass
from concourse import mybir

ALU = mybir.AluOpType
ACT = mybir.ActivationFunctionType
F32 = mybir.dt.float32
AX = mybir.AxisListType

B, C, H, W = 64, 192, 56, 56
KH = 55
MID = KH // 2
GROUPS, CG = 32, C // 32
FEMB, FORD = 32, 64
L = H + MID
U = L // 2 + 1
NE = 2 * W - 1
HB = B // 2
HALF = 64
KP = HALF + H
EPS = 1e-5
WP = 64
HC = C // 2

A_UNITS = [3, 3, 3, 3, 2, 2]
B_UNITS, B_MM = 6, 7
T_UNITS, T_MM = 8, 4
D_UNITS, D_BQ = 4, 8
assert B_UNITS * B_MM == U and T_UNITS * T_MM == HB and D_UNITS * D_BQ == HB and 2 * sum(A_UNITS) == HB


def constants():
    h, u, i = np.arange(H), np.arange(U), np.arange(KH)
    th = 2 * np.pi / L * (np.outer(h, u) % L)
    fwd = np.zeros((KP, 2, 2, U), np.float64)
    inv = np.zeros((2, U, 2, KP), np.float64)
    mean = np.zeros((KP, KP), np.float64)
    weight = np.where(u == 0, 1.0, 2.0) / L
    for p in range(2):
        rows = slice(HALF * p, HALF * p + H)
        fwd[rows, 0, p] = np.cos(th)
        fwd[rows, 1, p] = -np.sin(th)
        inv[p, :, 0, rows] = (np.cos(th) * weight).T
        inv[p, :, 1, rows] = (-np.sin(th) * weight).T
        mean[rows, rows] = 1.0 / (2 * H)
    tk = 2 * np.pi / L * (np.outer(i - MID, u) % L)
    taps = np.concatenate([np.cos(tk), -np.sin(tk)], axis=1)
    centre = (np.arange(KH) == MID).astype(np.float64)[:, None]
    f = lambda a: np.ascontiguousarray(a, dtype=np.float32)
    return {
        "k_fwd": f(fwd.reshape(KP, 4 * U)), "k_inv": f(inv.reshape(2 * U, 2 * KP)), "k_mean": f(mean),
        "k_gmean": f(np.kron(np.eye(HC // CG), np.full((CG, CG), 1.0 / (CG * H * W)))),
        "k_taps": f(taps), "k_centre": f(centre),
        "k_ind": f(np.hstack([np.kron(np.eye(2), np.ones((W, 1))), np.tile(np.eye(W), (2, 1))])), "k_eye": f(np.eye(128)), "k_eye_2w": f(np.eye(2 * W)),
    }


def filters(nc, d, khat):
    NPOS = KH * KH
    NCH = 7
    CH = NPOS // 7 + 1
    chunks = [(a, min(a + CH, NPOS)) for a in range(0, NPOS, CH)]
    PI = float(np.pi)
    INV2PI = float(np.float32(1 / (2 * np.pi)))
    ROUND = float(1.5 * 2 ** 23)
    TWO_PI_HI = 6.28125
    TWO_PI_LO = float(np.float32(2 * np.pi - 6.28125))
    PI_IN = 3.1415925
    JB = 5
    with ExitStack() as ctx:
        sb = lambda n, s: ctx.enter_context(nc.sbuf_tensor("f_" + n, s, F32))
        sem = lambda n: ctx.enter_context(nc.semaphore("f_" + n))
        z = sb("z", [FEMB, NPOS])
        arg = sb("arg", [FORD, NPOS])
        turns = sb("turns", [FORD, NPOS])
        h1 = sb("h1", [FORD, NPOS])
        w1T = sb("w1T", [FEMB, FORD])
        w2T = sb("w2T", [FORD, FORD])
        w3T = sb("w3T", [FORD, C])
        vec = sb("vec", [FORD, 4])
        dist = sb("dist", [KH, KH])
        ndist = sb("ndist", [KH, KH])
        chan = sb("chan", [KH, 3, C])
        absd = sb("absd", [KH, C])
        centre = sb("centre", [KH, 1])
        taps_dft = sb("taps", [KH, 2 * U])
        k = sb("k", [KH, KH, C])
        kf = sb("kf", [HC, 3, NE, U])
        pnet = ctx.enter_context(nc.psum_tensor("f_pnet", [128, 2, 512], F32))
        pk = ctx.enter_context(nc.psum_tensor("f_pk", [128, 2, 512], F32))
        pf = ctx.enter_context(nc.psum_tensor("f_pf", [128, 2, 512], F32))
        loaded, absed = sem("loaded"), sem("absed")
        net_mm, arg_made, red, sine = sem("net_mm"), sem("arg_made"), sem("red"), sem("sine")
        decayed, shifted, tap_mm, tap_made, biased = sem("decayed"), sem("shifted"), sem("tap_mm"), sem("tap_made"), sem("biased")
        dft_mm, dft_re, dft_im, zeroed, negated = sem("dft_mm"), sem("dft_re"), sem("dft_im"), sem("zeroed"), sem("negated")
        stored = sem("stored")
        NB = KH // JB
        with nc.Block() as block:

            @block.sync
            def _(sp):
                def whole(dst, src):
                    sp.dma_start(dst, src).then_inc(loaded, 16)
                whole(z[:], d["z"])
                whole(w1T[:], d["W1T"])
                whole(w2T[:], d["W2T"])
                whole(w3T[:], d["W3T"])
                for n, name in enumerate(("b1", "f1", "b2", "f2")):
                    whole(vec[:, n:n + 1], d[name])
                whole(dist[:], d["distance_map"])
                for n, name in enumerate(("deltas", "shift", "bias")):
                    v = d[name]
                    whole(chan[:, n, :], bass.AP(tensor=v.tensor, offset=v.offset, ap=[[0, KH], [1, C]]))
                whole(centre[:], d["k_centre"])
                whole(taps_dft[:], d["k_taps"])
                for m in range(2):
                    sp.wait_ge(dft_re, NB * (m + 1))
                    sp.wait_ge(dft_im, NB * (m + 1))
                    sp.wait_ge(negated, NB * (m + 1))
                    sp.wait_ge(zeroed, 2)
                    sp.dma_start(khat[HC * m:HC * m + HC].rearrange("c a n -> c (a n)"),
                                 kf[:].rearrange("c a e u -> c (a e u)")).then_inc(stored, 16)
                sp.wait_ge(stored, 32)

            LOADS = 14 * 16

            @block.tensor
            def _(pe):
                pe.wait_ge(loaded, LOADS)
                for layer in range(2):
                    lhs, rhs = ((w1T, z), (w2T, h1))[layer]
                    if layer:
                        pe.wait_ge(sine, NCH)
                    for n, (a, b) in enumerate(chunks):
                        g = layer * NCH + n
                        if g >= 2:
                            pe.wait_ge(arg_made, g - 1)
                        pe.matmul(pnet[0:FORD, g % 2, 0:b - a], lhs[:], rhs[:, a:b],
                                  start=True, stop=True).then_inc(net_mm, 1)
                pe.wait_ge(sine, 2 * NCH)
                cols = h1[:].rearrange("p (i j) -> p j i", j=KH)
                for g in range((KH + 1) // 2):
                    if g >= 2:
                        pe.wait_ge(tap_made, g - 1)
                    for j in range(2 * g, min(2 * g + 2, KH)):
                        mm = pe.matmul(pk[0:KH, g % 2, C * (j % 2):C * (j % 2) + C], cols[:, j, :], w3T[:],
                                       start=True, stop=True)
                    mm.then_inc(tap_mm, 1)
                pe.wait_ge(biased, 1)
                for m in range(2):
                    for g in range(NB):
                        n = m * NB + g
                        if n >= 2:
                            pe.wait_ge(dft_re, n - 1)
                            pe.wait_ge(dft_im, n - 1)
                        for j in range(JB):
                            mm = pe.matmul(pf[0:HC, n % 2, 2 * U * j:2 * U * j + 2 * U],
                                           k[:, KH - 1 - (JB * g + j), HC * m:HC * m + HC], taps_dft[:],
                                           start=True, stop=True)
                        mm.then_inc(dft_mm, 1)

            @block.scalar
            def _(act):
                act.wait_ge(loaded, LOADS)
                nc.scalar.activation(absd[:], chan[:, 0, :], ACT.Abs).then_inc(absed, 1)
                act.wait_ge(absed, 2)
                for j in range(KH):
                    e = nc.scalar.activation(k[:, j, :], absd[:], ACT.Exp, scale=ndist[:, j:j + 1])
                e.then_inc(decayed, 1)
                for g in range(2 * NCH):
                    a, b = chunks[g % NCH]
                    act.wait_ge(red, 5 * g + 5)
                    nc.scalar.activation(h1[:, a:b], arg[:, a:b], ACT.Sin).then_inc(sine, 1)
                for n in range(2 * NB):
                    m, g = divmod(n, NB)
                    act.wait_ge(dft_mm, n + 1)
                    if n == 0:
                        act.wait_ge(zeroed, 2)
                    if n == NB:
                        act.wait_ge(stored, 16)
                    src = pf[0:HC, n % 2, 0:2 * U * JB].rearrange("p (j r u) -> p r j u", j=JB, r=2)
                    e0 = W - 1 - MID + JB * g
                    nc.scalar.activation(kf[:, 0, e0:e0 + JB, :], src[:, 0], ACT.Copy).then_inc(dft_re, 1)
                    nc.scalar.activation(kf[:, 1, e0:e0 + JB, :], src[:, 1], ACT.Copy).then_inc(dft_im, 1)

            @block.gpsimd
            def _(pool):
                lo = W - 1 - MID
                for a in range(3):
                    x = pool.memset(kf[:, a, 0:lo, :], 0.0)
                x.then_inc(zeroed, 1)
                for a in range(3):
                    x = pool.memset(kf[:, a, lo + KH:NE, :], 0.0)
                x.then_inc(zeroed, 1)

            @block.vector
            def _(dve):
                dve.wait_ge(loaded, LOADS)
                nc.vector.tensor_scalar(ndist[:], dist[:], -1.0, None, ALU.mult).then_inc(absed, 1)
                for g in range(2 * NCH):
                    layer, n = divmod(g, NCH)
                    a, b = chunks[n]
                    x, t = arg[:, a:b], turns[:, a:b]
                    bcol, fcol = vec[:, 2 * layer:2 * layer + 1], vec[:, 2 * layer + 1:2 * layer + 2]
                    dve.wait_ge(net_mm, g + 1)
                    if layer:
                        dve.wait_ge(sine, n + 1)
                    nc.vector.tensor_scalar(x, pnet[0:FORD, g % 2, 0:b - a], bcol, fcol, ALU.add, ALU.mult)\
                        .then_inc(arg_made, 1)
                    dve.wait_ge(arg_made, g + 1)
                    nc.vector.tensor_scalar(t, x, INV2PI, ROUND, ALU.mult, ALU.add).then_inc(red, 1)
                    dve.wait_ge(red, 5 * g + 1)
                    nc.vector.tensor_scalar(t, t, ROUND, None, ALU.subtract).then_inc(red, 1)
                    dve.wait_ge(red, 5 * g + 2)
                    nc.vector.scalar_tensor_tensor(x, t, -TWO_PI_HI, x, ALU.mult, ALU.add).then_inc(red, 1)
                    dve.wait_ge(red, 5 * g + 3)
                    nc.vector.scalar_tensor_tensor(x, t, -TWO_PI_LO, x, ALU.mult, ALU.add).then_inc(red, 1)
                    dve.wait_ge(red, 5 * g + 4)
                    nc.vector.tensor_scalar(x, x, PI_IN, -PI_IN, ALU.min, ALU.max).then_inc(red, 1)
                dve.wait_ge(decayed, 1)
                shift = chan[:, 1:2, :].broadcast_to([KH, KH, C])
                nc.vector.tensor_tensor(k[:], k[:], shift, ALU.add).then_inc(shifted, 1)
                dve.wait_ge(shifted, 1)
                for g in range((KH + 1) // 2):
                    js = slice(2 * g, min(2 * g + 2, KH))
                    n = js.stop - js.start
                    dve.wait_ge(tap_mm, g + 1)
                    nc.vector.tensor_tensor(k[:, js, :], k[:, js, :],
                                            pk[0:KH, g % 2, 0:C * n].rearrange("p (j c) -> p j c", j=n),
                                            ALU.mult).then_inc(tap_made, 1)
                dve.wait_ge(tap_made, (KH + 1) // 2)
                nc.vector.scalar_tensor_tensor(k[:, MID, :], chan[:, 2, :], centre[:, 0:1], k[:, MID, :],
                                               ALU.mult, ALU.add).then_inc(biased, 1)
                for n in range(2 * NB):
                    m, g = divmod(n, NB)
                    dve.wait_ge(dft_im, n + 1)
                    if n == 0:
                        dve.wait_ge(zeroed, 2)
                    e0 = W - 1 - MID + JB * g
                    nc.vector.tensor_scalar(kf[:, 2, e0:e0 + JB, :], kf[:, 1, e0:e0 + JB, :], -1.0, None,
                                            ALU.mult).then_inc(negated, 1)


def convolution(nc, d, khat, x1, rsum, groups=GROUPS):
    IT = groups // 2
    CI = 2 * CG
    NA, NBU, NT, ND = len(A_UNITS) * CI, B_UNITS * CI, T_UNITS * CI, D_UNITS * CI
    RING = 4 * T_MM
    FIRST, REST = range(len(A_UNITS) - 1), range(len(A_UNITS) - 1, len(A_UNITS))
    AHEAD = 2
    A_FREE = len(A_UNITS) * CG
    STAT_CH = {1: range(0, 11), 2: range(11, 22), 3: range(22, 32)}
    with ExitStack() as ctx:
        sb = lambda n, s: ctx.enter_context(nc.sbuf_tensor("c_" + n, s, F32))
        ps = lambda n: ctx.enter_context(nc.psum_tensor("c_" + n, [128, 2, 512], F32))
        sem = lambda n: ctx.enter_context(nc.semaphore("c_" + n))
        x = sb("x", [128, 2, CG, HB, W])
        xn = sb("xn", [128, CG, HB, WP])
        xhat = sb("xhat", [128, 2 * U, HB])
        toep = sb("toep", [128, 2, 2, W, U])
        prod = sb("prod", [2 * W, HB, 2, U])
        prodT = sb("prodT", [2 * U, RING, 2, W])
        fwd = sb("fwd", [KP, 4 * U])
        inv = sb("inv", [2 * U, 2, KP])
        eye = sb("eye", [2 * W, 2 * W])
        mean = sb("mean", [KP, KP])
        stats = sb("stats", [KP, HB, 6])
        part = sb("part", [KP, 3, HB])
        q = sb("q", [KP, 2, HB])
        mv = sb("mv", [KP, 3, HB])
        scale = sb("scale", [KP, HB])
        shift = sb("shift", [KP, HB])
        rs = sb("rs", [KP, CI, 2, HB])
        square = sb("square", [KP, HB // 2, W])
        pa, pb, pt, pd = ps("pa"), ps("pb"), ps("pt"), ps("pd")
        const_in, cleared = sem("const_in"), sem("cleared")
        x_in = [sem("x_in0"), sem("x_in1")]
        toep_in = [sem("toep_in0"), sem("toep_in1")]
        a_mm, a_act, a_dve = sem("a_mm"), sem("a_act"), sem("a_dve")
        b_mm, b_act = sem("b_mm"), sem("b_act")
        t_mm, t_act, t_dve = sem("t_mm"), sem("t_act"), sem("t_dve")
        d_mm, d_dve = sem("d_mm"), sem("d_dve")
        st, q_made, mean_mm, mv_read, var_made, std_made, sc = (
            sem("st"), sem("q_made"), sem("mean_mm"), sem("mv_read"), sem("var_made"), sem("std_made"), sem("sc"))
        scaled, multiplied, normed, summed, squared, sq_summed = sem("scaled"), sem("multiplied"), sem("normed"), sem("summed"), sem("squared"), sem("sq_summed")
        stored = [sem("stored0"), sem("stored1")]

        with nc.Block() as block:

            @block.sync
            def _(sp):
                for dst, name in ((fwd[:], "k_fwd"), (inv[:].rearrange("p r h -> p (r h)"), "k_inv"),
                                  (eye[:], "k_eye_2w"), (mean[:], "k_mean")):
                    sp.dma_start(dst, d[name]).then_inc(const_in, 16)
                sp.wait_ge(cleared, 3)

                def load_x(slot, c, channel):
                    for p in range(2):
                        sp.dma_start(x[HALF * p:HALF * p + H, slot, c, :, :], d["x"][channel, p])\
                            .then_inc(x_in[slot], 16)

                def load_toep(par, channel):
                    for p, r, a in ((0, 0, 0), (0, 1, 1), (1, 0, 2), (1, 1, 0)):
                        src = khat[channel, a, 0:W * U]
                        src = bass.AP(tensor=src.tensor, offset=src.offset, ap=[[U, W], [1, W * U]])
                        sp.dma_start(toep[HALF * p:HALF * p + W, par, r, :, :].rearrange("w v u -> w (v u)"), src)\
                            .then_inc(toep_in[par], 16)

                def step(it, n, last):
                    s, c = divmod(n, CG)
                    channel = it * CI + n
                    sp.wait_ge(summed, it * CI + n + 1)
                    sp.wait_ge(sq_summed, (it * CI + n) * 2 + 3)
                    for p in range(2):
                        sp.dma_start(x1[HB * p:HB * p + HB, channel].rearrange("b h w -> h b w"),
                                     x[HALF * p:HALF * p + H, s, c, :, :]).then_inc(stored[n % 2], 16)
                        sp.dma_start(rsum[channel, :, p].rearrange("a h b -> h a b"), rs[HALF * p:HALF * p + H, n])\
                            .then_inc(stored[n % 2], 16)
                    if not last or n + 3 < CI:
                        sp.wait_ge(b_mm, it * NBU + (n + 2) * B_UNITS)
                        load_toep((n + 1) % 2, channel + 3)
                    if not last:
                        sp.wait_ge(stored[n % 2], 64 * (it * (CI // 2) + n // 2 + 1))
                        load_x(s, c, channel + CI)

                for s in range(2):
                    for c in range(CG):
                        load_x(s, c, s * CG + c)
                    if s == 0:
                        load_toep(0, 0)
                        load_toep(1, 1)
                sp.wait_ge(b_mm, B_UNITS)
                load_toep(0, 2)
                if IT > 1:
                    with sp.Fori(0, IT - 1) as it:
                        for n in range(CI):
                            step(it, n, False)
                for n in range(CI):
                    step(IT - 1, n, True)
                for s in range(2):
                    sp.wait_ge(stored[s], 64 * IT * (CI // 2))

            @block.gpsimd
            def _(pool):
                pool.memset(x[32:64, 0], 0.0).then_inc(cleared, 1)
                pool.memset(x[32:64, 1], 0.0).then_inc(cleared, 1)
                pool.memset(toep[32:64], 0.0).then_inc(cleared, 1)
                pool.wait_ge(cleared, 3)
                pool.memset(xn[:, :, :, W:WP], 0.0).then_inc(cleared, 1)

                def normalise(it, n):
                    s, c = divmod(n % CI, CG)
                    over = lambda a: a[:].rearrange("p (b o) -> p b o", o=1).broadcast_to([KP, HB, W])
                    if c == 0:
                        pool.wait_ge(scaled, 2 * (it * 2 + n // CG + 1))
                    pool.wait_ge(a_mm, it * NA + (n + 1) * len(A_UNITS))
                    nc.gpsimd.tensor_tensor(xn[0:KP, c, :, 0:W], x[0:KP, s, c], over(scale), ALU.mult)\
                        .then_inc(multiplied, 1)
                    pool.wait_ge(multiplied, it * CI + n + 1)
                    nc.gpsimd.tensor_tensor(xn[0:KP, c, :, 0:W], xn[0:KP, c, :, 0:W], over(shift), ALU.add)\
                        .then_inc(normed, 1)

                pool.wait_ge(cleared, 4)
                for n in range(AHEAD):
                    normalise(0, n)
                if IT > 1:
                    with pool.Fori(0, IT - 1) as it:
                        for n in range(CI):
                            normalise(it, n + AHEAD)
                for n in range(CI - AHEAD):
                    normalise(IT - 1, n + AHEAD)

            @block.tensor
            def _(pe):
                def forward(it, n, units=range(len(A_UNITS))):
                    s, c = divmod(n, CG)
                    for k in units:
                        size, m = A_UNITS[k], sum(A_UNITS[:k])
                        unit = n * len(A_UNITS) + k
                        if k == 0:
                            pe.wait_ge(normed, it * CI + n + 1)
                        pe.wait_ge(a_act, it * NA + unit + 1)
                        pe.wait_ge(a_dve, it * NA + unit + 1)
                        for r in range(size):
                            cols = xn[0:KP, c, 2 * m:2 * m + 2, :].rearrange("p b w -> p (b w)")
                            mm = pe.matmul(pa[:, unit % 2, 4 * U * r:4 * U * r + 4 * U], cols, fwd[:],
                                           start=True, stop=True)
                            m += 1
                        mm.then_inc(a_mm, 1)

                def toeplitz(it, n):
                    pe.wait_ge(toep_in[n % 2], 64 * (it * (CI // 2) + n // 2 + 1))
                    pe.wait_ge(a_act, it * NA + (n + 1) * len(A_UNITS) + 2)
                    pe.wait_ge(a_dve, it * NA + (n + 1) * len(A_UNITS) + 2)
                    by_u = xhat[:].rearrange("p (a u) b -> p u a b", a=2)
                    for k in range(B_UNITS):
                        unit = n * B_UNITS + k
                        pe.wait_ge(b_act, it * NBU + unit + 1)
                        for r in range(B_MM):
                            u = k * B_MM + r
                            mm = pe.matmul(pb[0:2 * W, unit % 2, B * r:B * r + B],
                                           toep[0:KP, n % 2, :, :, u].rearrange("p r v -> p (r v)"),
                                           by_u[0:KP, u], start=True, stop=True)
                        mm.then_inc(b_mm, 1)

                def turn(it, n, k):
                    unit = n * T_UNITS + k
                    if k == 0:
                        pe.wait_ge(b_act, it * NBU + (n + 1) * B_UNITS + 2)
                    if unit % 2 == 0:
                        pe.wait_ge(t_act, it * (NT // 2) + unit // 2 + 1)
                    else:
                        pe.wait_ge(t_dve, it * (NT // 2) + unit // 2 + 1)
                    for r in range(T_MM):
                        mm = pe.transpose(pt[0:2 * U, unit % 2, 2 * W * r:2 * W * r + 2 * W],
                                          prod[:, T_MM * k + r].rearrange("p a u -> p (a u)"), eye[0:2 * W, 0:2 * W])
                    mm.then_inc(t_mm, 1)

                def inverse(it, n, k):
                    unit = n * D_UNITS + k
                    pe.wait_ge(d_dve, it * ND + unit + 1)
                    pe.wait_ge(t_act, it * (NT // 2) + (n * T_UNITS + 2 * k) // 2 + 2)
                    pe.wait_ge(t_dve, it * (NT // 2) + (n * T_UNITS + 2 * k) // 2 + 2)
                    for r in range(2):
                        mm = pe.matmul(pd[0:KP, unit % 2, 0:D_BQ * W], inv[:, r, :],
                                       prodT[:, D_BQ * k % RING:D_BQ * k % RING + D_BQ, r, :], start=(r == 0), stop=(r == 1))
                    mm.then_inc(d_mm, 1)

                def group_mean(count):
                    pe.wait_ge(q_made, count)
                    pe.matmul(pd[0:KP, 0, 0:2 * HB], mean[:], q[:].rearrange("p a b -> p (a b)"),
                              start=True, stop=True).then_inc(mean_mm, 1)

                def channels(it, last):
                    for s in range(2):
                        more = not (last and s == 1)
                        for c in range(CG):
                            n = s * CG + c
                            if c == CG - 2 and more:
                                pe.wait_ge(d_dve, it * ND + n * D_UNITS + 2)
                                group_mean(it * 2 + s + 2)
                            toeplitz(it, n)
                            if n < CI - 1 or more:
                                forward(it, n + 1, FIRST)
                            for k in range(T_UNITS):
                                turn(it, n, k)
                                if k == 1 and (n < CI - 1 or more):
                                    forward(it, n + 1, REST)
                                if k == 1 and c == CG - 2 and more:
                                    pe.wait_ge(mv_read, it * 2 + s + 2)
                                if k >= 3 and k % 2 == 1:
                                    inverse(it, n, k // 2 - 1)
                            inverse(it, n, D_UNITS - 1)

                pe.sem_inc(a_mm, A_FREE)
                pe.wait_ge(const_in, 64)
                pe.wait_ge(cleared, 4)
                group_mean(1)
                pe.wait_ge(mv_read, 1)
                forward(0, 0)
                if IT > 1:
                    with pe.Fori(0, IT - 1) as it:
                        channels(it, False)
                channels(IT - 1, True)

            @block.scalar
            def _(act):
                def std(count):
                    act.wait_ge(var_made, count)
                    nc.scalar.activation(mv[:, 2, :], mv[:, 2, :], ACT.Sqrt).then_inc(std_made, 1)

                def forward_out(it, n, units=range(len(A_UNITS))):
                    for k in units:
                        size = A_UNITS[k]
                        unit = n * len(A_UNITS) + k
                        act.wait_ge(a_mm, it * NA + A_FREE + unit + 1)
                        copy_xhat(nc.scalar, 0, unit, k, size).then_inc(a_act, 1)

                def copy_xhat(eng, j, unit, k, size):
                    m0 = sum(A_UNITS[:k])
                    for r in range(2):
                        src = pa[HALF * j:HALF * j + 64, unit % 2, 0:4 * U * size]\
                            .rearrange("p (m r u) -> p r m u", m=size, r=2)[:, r]
                        dst = xhat[64 * r:64 * r + 64].rearrange("p u (m j) -> p j m u", j=2)[:, j, m0:m0 + size]
                        ins = eng.activation(dst, src, ACT.Copy)
                    return ins

                def product_out(it, n, std_count):
                    for k in range(B_UNITS):
                        if k == 1 and std_count is not None:
                            std(std_count)
                        unit = n * B_UNITS + k
                        act.wait_ge(b_mm, it * NBU + unit + 1)
                        nc.scalar.activation(
                            prod[:].rearrange("p b a u -> p u a b")[:, B_MM * k:B_MM * k + B_MM],
                            pb[0:2 * W, unit % 2, 0:B_MM * B].rearrange("p (u a b) -> p u a b", a=2, b=HB), ACT.Copy)\
                            .then_inc(b_act, 1)

                def turn_out(it, n, k):
                    unit = n * T_UNITS + k
                    act.wait_ge(t_mm, it * NT + unit + 1)
                    nc.scalar.activation(
                        prodT[:, T_MM * k % RING:T_MM * k % RING + T_MM].rearrange("p b r v -> p (b r v)"),
                        pt[0:2 * U, unit % 2, 0:T_MM * 2 * W], ACT.Copy).then_inc(t_act, 1)

                def squares(it, n, k):
                    s, c = divmod(n, CG)
                    act.wait_ge(sq_summed, (it * CI + n) * 2 + k + 1)
                    act.wait_ge(d_dve, it * ND + n * D_UNITS + 2 * k + 2 + 2)
                    nc.scalar.activation(square[:], x[0:KP, s, c, HB // 2 * k:HB // 2 * k + HB // 2, :],
                                         ACT.Square).then_inc(squared, 1)

                def channels(it, last):
                    for s in range(2):
                        more = not (last and s == 1)
                        for c in range(CG):
                            n = s * CG + c
                            product_out(it, n, it * 2 + s + 2 if c == CG - 2 and more else None)
                            if n < CI - 1 or more:
                                forward_out(it, n + 1, FIRST)
                            for k in range(0, T_UNITS, 2):
                                turn_out(it, n, k)
                                if k == 0 and (n < CI - 1 or more):
                                    forward_out(it, n + 1, REST)
                            for k in range(2):
                                squares(it, n, k)

                act.sem_inc(a_act, 2)
                act.sem_inc(b_act, 2)
                act.sem_inc(t_act, 1)
                std(1)
                forward_out(0, 0)
                if IT > 1:
                    with act.Fori(0, IT - 1) as it:
                        channels(it, False)
                channels(IT - 1, True)

            @block.vector
            def _(dve):
                def bn(slot, images):
                    for b in images:
                        ins = nc.vector.bn_stats(stats[:, b, :], x[0:KP, slot, :, b, :])
                    ins.then_inc(st, 1)

                def q_of(count, first):
                    dve.wait_ge(st, 3 * count)
                    me, ve, mo, vo = (stats[:, :, i] for i in (1, 2, 4, 5))
                    if not first:
                        dve.wait_ge(mean_mm, count - 1)
                    nc.vector.tensor_tensor(q[:, 0, :], me, mo, ALU.add).then_inc(sc, 1)
                    nc.vector.tensor_tensor(part[:, 0, :], me, me, ALU.mult).then_inc(sc, 1)
                    nc.vector.tensor_tensor(part[:, 1, :], mo, mo, ALU.mult).then_inc(sc, 1)
                    nc.vector.tensor_tensor(part[:, 2, :], ve, vo, ALU.add).then_inc(sc, 1)
                    dve.wait_ge(sc, 7 * (count - 1) + 4)
                    nc.vector.tensor_tensor(part[:, 0, :], part[:, 0, :], part[:, 1, :], ALU.add).then_inc(sc, 1)
                    dve.wait_ge(sc, 7 * (count - 1) + 5)
                    nc.vector.scalar_tensor_tensor(q[:, 1, :], part[:, 2, :], 2.0 / (CG * W), part[:, 0, :],
                                                   ALU.mult, ALU.add).then_inc(q_made, 1)

                def scales(count, first):
                    dve.wait_ge(mean_mm, count)
                    nc.vector.tensor_copy(mv[:, 0:2, :], pd[0:KP, 0, 0:2 * HB].rearrange("p (a b) -> p a b", a=2))\
                        .then_inc(mv_read, 1)
                    dve.wait_ge(mv_read, count)
                    nc.vector.tensor_tensor(part[:, 0, :], mv[:, 0, :], mv[:, 0, :], ALU.mult).then_inc(sc, 1)
                    dve.wait_ge(sc, 7 * (count - 1) + 6)
                    nc.vector.tensor_tensor(part[:, 1, :], mv[:, 1, :], part[:, 0, :], ALU.subtract).then_inc(sc, 1)
                    dve.wait_ge(sc, 7 * (count - 1) + 7)
                    nc.vector.tensor_scalar(mv[:, 2, :], part[:, 1, :], 0.0, EPS, ALU.max, ALU.add)\
                        .then_inc(var_made, 1)
                    if not first:
                        dve.wait_ge(normed, CG * (count - 1))
                    dve.wait_ge(std_made, count)
                    nc.vector.reciprocal(scale[:], mv[:, 2, :]).then_inc(scaled, 1)
                    dve.wait_ge(scaled, 2 * count - 1)
                    nc.vector.scalar_tensor_tensor(shift[:], mv[:, 0, :], -1.0, scale[:], ALU.mult, ALU.mult)\
                        .then_inc(scaled, 1)

                def forward_out(it, n, units=range(len(A_UNITS))):
                    for k in units:
                        size = A_UNITS[k]
                        unit = n * len(A_UNITS) + k
                        dve.wait_ge(a_mm, it * NA + A_FREE + unit + 1)
                        m0 = sum(A_UNITS[:k])
                        for r in range(2):
                            src = pa[HALF:HALF + 64, unit % 2, 0:4 * U * size]\
                                .rearrange("p (m r u) -> p r m u", m=size, r=2)[:, r]
                            dst = xhat[64 * r:64 * r + 64].rearrange("p u (m j) -> p j m u", j=2)[:, 1, m0:m0 + size]
                            ins = nc.vector.tensor_copy(dst, src)
                        ins.then_inc(a_dve, 1)

                def turn_out(it, n, k):
                    unit = n * T_UNITS + k
                    dve.wait_ge(t_mm, it * NT + unit + 1)
                    nc.vector.tensor_copy(
                        prodT[:, T_MM * k % RING:T_MM * k % RING + T_MM].rearrange("p b r v -> p (b r v)"),
                        pt[0:2 * U, unit % 2, 0:T_MM * 2 * W]).then_inc(t_dve, 1)

                def inverse_out(it, n, k):
                    s, c = divmod(n, CG)
                    unit = n * D_UNITS + k
                    dve.wait_ge(d_mm, it * ND + unit + 1)
                    rows = x[0:KP, s, c, D_BQ * k:D_BQ * k + D_BQ, :]
                    y = pd[0:KP, unit % 2, 0:D_BQ * W].rearrange("p (b w) -> p b w", w=W)[:, :, ::-1]
                    nc.vector.tensor_tensor(rows, y, rows, ALU.add)\
                        .then_inc(d_dve, 1)

                def sums(it, n):
                    s, c = divmod(n, CG)
                    dve.wait_ge(d_dve, it * ND + (n + 1) * D_UNITS + 2)
                    nc.vector.reduce_sum(rs[:, n, 0, :], x[0:KP, s, c], AX.X).then_inc(summed, 1)

                def square_sums(it, n, k):
                    dve.wait_ge(squared, (it * CI + n) * 2 + k + 1)
                    nc.vector.reduce_sum(rs[:, n, 1, HB // 2 * k:HB // 2 * k + HB // 2], square[:], AX.X)\
                        .then_inc(sq_summed, 1)

                def channels(it, last):
                    for s in range(2):
                        done = it * 2 + s + 1
                        more = not (last and s == 1)
                        for c in range(CG):
                            n = s * CG + c
                            if c in STAT_CH and more:
                                if c == 1:
                                    dve.wait_ge(x_in[1 - s], 32 * CG * (it + 1 + s))
                                bn(1 - s, STAT_CH[c])
                                if c == CG - 3:
                                    q_of(done + 1, False)
                            if c == CG - 2 and more:
                                scales(done + 1, False)
                            if n < CI - 1 or more:
                                forward_out(it, n + 1, FIRST)
                            for k in range(1, T_UNITS, 2):
                                turn_out(it, n, k)
                                if k == 1 and (n < CI - 1 or more):
                                    forward_out(it, n + 1, REST)
                                if k >= 3:
                                    inverse_out(it, n, k // 2 - 1)
                            square_sums(it, n, 0)
                            inverse_out(it, n, D_UNITS - 1)
                            sums(it, n)
                            square_sums(it, n, 1)

                dve.sem_inc(a_dve, 2)
                dve.sem_inc(sq_summed, 1)
                dve.sem_inc(t_dve, 1)
                dve.sem_inc(d_dve, 2)
                dve.wait_ge(cleared, 4)
                dve.wait_ge(x_in[0], 32 * CG)
                for images in STAT_CH.values():
                    bn(0, images)
                q_of(1, True)
                scales(1, True)
                forward_out(0, 0)
                if IT > 1:
                    with dve.Fori(0, IT - 1) as it:
                        channels(it, False)
                channels(IT - 1, True)


def attention(nc, d, x1, rsum, y, images=B):
    HEADS, DH, NMEM, REP = 4, 32, 4, 160
    HID = HEADS * DH
    SCALE = DH ** -0.5
    PX = 2 * W
    BLOCKS = H * W // PX
    UNITS, UB = BLOCKS // 2, 2
    TERMS = H + W
    KEYS = 68
    MEM = HALF
    FOURS = images // 4
    LAPS = UNITS - 2
    with ExitStack() as ctx:
        sb = lambda n, s: ctx.enter_context(nc.sbuf_tensor("t_" + n, s, F32))
        ps = lambda n, k=1: ctx.enter_context(nc.psum_tensor("t_" + n, [128, k, 512], F32))
        sem = lambda n: ctx.enter_context(nc.semaphore("t_" + n))
        x = sb("x", [HC + 1, 4, 2, H, W])
        xT = sb("xT", [PX, 2, BLOCKS, C])
        diag = sb("diag", [HC + 1, 2, 2, HC])
        shifts = sb("shifts", [HC, 2, HC])
        weights = sb("weights", [PX, BLOCKS * (TERMS + UB)])
        by_block = weights[:, 0:BLOCKS * TERMS].rearrange("p (b k) -> p b k", b=BLOCKS)
        row_places = weights[:].rearrange("p (b k) -> p b k", b=BLOCKS)[:, :, 0:UB]
        ind = sb("ind", [PX, UB + W])
        junk = sb("junk", [PX, 2, UB, C])
        n2 = sb("n2", [PX, BLOCKS])
        sums = sb("sums", [HC, 2, 2, H, HB])
        squares = x[0:HC, 2:4].rearrange("p k m h w -> p (k m h w)")[:, 0:4 * H * HB]\
            .rearrange("p (m g h q) -> p m g h q", m=2, g=2, h=H)
        stat = sb("stat", [HC, 4, 2, B])
        cols = sb("cols", [HC, 4, 4, 2])
        raw = sb("raw", [HC, 2, 2, W])
        feat = sb("feat", [HC, 2, 2, W])
        vfeat = sb("vfeat", [HC, 2, 2, W])
        fn = sb("fn", [HID, 2 * W])
        Q = sb("Q", [HID, 2, W])
        K = sb("K", [HID, 2, HEADS, KEYS])
        E = sb("E", [W, 2, HEADS, KEYS])
        zs = sb("zs", [W, 5, 2 * HEADS])
        ET_fsq = sb("ET_fsq", [128, 2 * HEADS * W])
        ET = ET_fsq[0:KEYS].rearrange("p (t h w) -> p t h w", t=2, h=HEADS)
        fsq = ET_fsq[0:HC, 0:4 * W].rearrange("p (m t w) -> p m t w", m=2, t=2)
        V = sb("V", [KEYS, 2, HID])
        O = Q
        term = sb("term", [HC, 2, 2, 2, W])
        nrm = sb("nrm", [PX, BLOCKS])
        wq, wk, wv = (sb(n, [HC, 2, HID]) for n in ("wq", "wk", "wv"))
        gains = sb("gains", [HC, 3, 2])
        first = xT[0:HC, 0].rearrange("p b c -> p (b c)")
        wo = first[:, 0:2 * HID].rearrange("p (m c) -> p m c", m=2)
        wr = first[:, 256:256 + 4 * C].rearrange("p (m t c) -> p m t c", m=2, t=2)
        tot = first[:, 1024:1024 + 4 * B].rearrange("p (a m b) -> p a m b", a=2, m=2)
        gmean = first[:, 1280:1280 + HC]
        var = first[:, 1376:1376 + 2 * B].rearrange("p (m b) -> p m b", m=2)
        bo = first[:, 1504:1506]
        wc = sb("wc", [HID, 2, C])
        bias = sb("bias", [HC, 2, 2])
        eye = sb("eye", [128, 128])
        ones = sb("ones", [128, 128])
        pturn, psum, pshift = ps("pturn", 2), ps("psum"), ps("pshift")
        pq, psc, pt = ps("pq"), ps("psc", 2), ps("pt")
        names = """w_in k_in v_in sum_in cleared scaled gm_mm tots gm_copy v1 v2 v3 v4 v5 v6 wc_mm wc_made
            fetched diag_made shift_mm shift_in turn_mm turned n_sqrt n_max n_inv weighted sums_mm v_ready cs_made
            f_made fsq_made fn_mm fn_sqrt fn_max fn_inv qk_mm qk_made s_mm mx_made s_sub e_made z_k z_m z_made z_inv
            e_norm t_mm et_made v_mm v_made o_mm o_made term_mm term_made row_added added row_added0 added0 rows_in""".split()
        S = {n: sem(n) for n in names}
        x_in = [sem(f"x_in{k}") for k in range(4)]
        stored = [[sem(f"stored{k}_{m}") for m in range(2)] for k in range(4)]

        def wait(eng, name, value):
            if not (isinstance(value, int) and value <= 0):
                eng.wait_ge(S[name], value)

        def along_rows(slot, m):
            return term[:, slot % 2, 0, m].rearrange("p (h o) -> p h o", o=1).broadcast_to([HC, H, W])

        def along_columns(slot, m):
            return term[:, slot % 2, 1, m].rearrange("p (o w) -> p o w", o=1).broadcast_to([HC, H, W])

        def schedule(eng, step):
            for j in range(-2, 2):
                step(0, j, True, j >= -1, j >= 0, j >= 1)
            passes = (images - 4) // 4
            if passes:
                with eng.Fori(0, passes) as it:
                    for j in range(2, 6):
                        step(it, j, True, True, True, True)
            for j in range(4 * passes + 2, images + 1):
                step(0, j, j + 2 < images, j + 1 < images, j < images, True)

        with nc.Block() as block:

            @block.sync
            def _(sp):
                for dst, src, s in (
                        (wq[:], d["WqT"], "w_in"), (wk[:], d["WkT"], "w_in"), (wv[:], d["WvT"], "w_in"),
                        (wo, d["Wo"], "w_in"), (wr, d["WrT"], "w_in"), (bo, d["bo"], "w_in"),
                        (gains[:], d["gains"], "w_in"), (eye[:], d["k_eye"], "w_in"), (ind[:], d["k_ind"], "w_in"), (gmean, d["k_gmean"], "w_in")):
                    sp.dma_start(dst, src).then_inc(S[s], 16)
                for m in range(2):
                    for dst, a in ((sums, 0), (squares, 1)):
                        sp.dma_start(dst[:, m], rsum[HC * m:HC * m + HC, a]).then_inc(S["sum_in"], 16)
                sp.wait_ge(S["cleared"], 6)
                for t in range(2):
                    for j in range(3):
                        for h in range(HEADS):
                            sp.dma_start(K[DH * h:DH * h + DH, t, h, W + NMEM * j:W + NMEM * j + NMEM],
                                         d["mem_kT"][h]).then_inc(S["k_in"], 16)
                    sp.dma_start(V[MEM:MEM + NMEM, t, :], d["mem_v"]).then_inc(S["v_in"], 16)

                def where(four, k):
                    return HB * (k // 2) + four * 2 + k % 2

                def load(four, k, m):
                    sp.dma_start(x[0:HC, k, m], x1[where(four, k), HC * m:HC * m + HC]).then_inc(x_in[k], 16)

                def store(four, k, m):
                    sp.dma_start(y[where(four, k), HC * m:HC * m + HC], x[0:HC, k, m]).then_inc(stored[k][m], 16)

                def leave(four, k):
                    sp.wait_ge(S["added0"], four * 4 + k + 1)
                    store(four, k, 0)
                    sp.wait_ge(S["added"], four * 4 + k + 3)
                    store(four, k, 1)

                for k in range(4):
                    if k == 2:
                        sp.wait_ge(S["tots"], 2)
                    for m in range(2):
                        load(0, k, m)
                if FOURS > 1:
                    with sp.Fori(0, FOURS - 1) as it:
                        for k in range(4):
                            leave(it, k)
                            for m in range(2):
                                sp.wait_ge(stored[k][m], it * 16 + 16)
                                load(it + 1, k, m)
                for k in range(4):
                    leave(FOURS - 1, k)
                for k in range(4):
                    for m in range(2):
                        sp.wait_ge(stored[k][m], 16 * FOURS)

            @block.gpsimd
            def _(pool):
                pool.sem_inc(S["added"], 2)
                pool.memset(K[:], 0.0).then_inc(S["cleared"], 1)
                pool.memset(ones[:], 1.0).then_inc(S["cleared"], 1)
                pool.memset(bias[:], 0.0).then_inc(S["cleared"], 1)
                pool.memset(V[:], 0.0).then_inc(S["cleared"], 1)
                pool.memset(weights[:], 0.0).then_inc(S["cleared"], 1)
                pool.wait_ge(S["cleared"], 5)
                pool.memset(x[HC:HC + 1], 1.0).then_inc(S["cleared"], 1)

                def step(it, j, prep, turn, weigh, attend):
                    if attend:
                        i, slot = it * 4 + (j - 1), (j - 1) % 4
                        wait(pool, "term_made", i + 2)
                        nc.gpsimd.tensor_tensor(x[0:HC, slot, 1], x[0:HC, slot, 1], along_rows(slot, 1), ALU.add)\
                            .then_inc(S["row_added"], 1)
                        wait(pool, "row_added", i + 1)
                        nc.gpsimd.tensor_tensor(x[0:HC, slot, 1], x[0:HC, slot, 1], along_columns(slot, 1), ALU.add)\
                            .then_inc(S["added"], 1)
                schedule(pool, step)

            @block.tensor
            def _(pe):
                def before():
                    pe.wait_ge(S["w_in"], 10 * 16)
                    pe.wait_ge(S["cleared"], 6)
                    pe.wait_ge(S["tots"], 2)
                    pe.matmul(pq[0:HC, 0, 0:4 * B], gmean, tot.rearrange("p a m b -> p (a m b)"),
                              start=True, stop=True).then_inc(S["gm_mm"], 1)
                    for t in range(2):
                        for m in range(2):
                            pe.matmul(psc[0:HID, t, 0:C], wo[:, m, :], wr[:, m, t, :], start=(m == 0), stop=(m == 1))
                    for o in range(2):
                        for t in range(2):
                            for m in range(2):
                                mm = pe.matmul(pt[0:HC, 0, o:o + 1], wr[:, m, t, HC * o:HC * o + HC], bo[:, m:m + 1],
                                               start=(t + m == 0), stop=(t + m == 2))
                    mm.then_inc(S["wc_mm"], 1)
                    pe.wait_ge(S["scaled"], 3)
                    pe.wait_ge(S["wc_made"], 3)
                    pe.wait_ge(S["gm_copy"], 1)
                    pe.wait_ge(S["k_in"], 16 * 24)
                    pe.wait_ge(S["v_in"], 16 * 2)

                def turned_block(n, j, u):
                    m, k, par = n + 1, (j + 1) % 4, (j + 1) % 2
                    if u > 1:
                        wait(pe, "turned", m * UNITS + (u - 1))
                    elif not (isinstance(n, int) and n < 0):
                        wait(pe, "turned", n * UNITS + (UNITS + u - 1))
                    for r in range(UB):
                        for h in range(2):
                            b = UB * u + r
                            mm = pe.matmul(pturn[0:PX, u % 2, C * r + HC * h:C * r + HC * h + HC],
                                           x[:, k, h, UB * b:UB * b + UB, :].rearrange("p h w -> p (h w)"),
                                           diag[:, par, h, :], start=True, stop=True)
                    mm.then_inc(S["turn_mm"], 1)

                def weighted_sums(j, a, b):
                    for g in range(a, b):
                        h, block = divmod(g, BLOCKS)
                        mm = pe.matmul(psum[0:HC, 0, TERMS * h:TERMS * h + TERMS],
                                       xT[:, j % 2, block, HC * h:HC * h + HC], by_block[:, block, :],
                                       start=(block == 0), stop=(block == BLOCKS - 1))
                    if b == 2 * BLOCKS:
                        mm.then_inc(S["sums_mm"], 1)

                def step(it, j, prep, turn, weigh, attend):
                    n, i = it * 4 + j, it * 4 + (j - 1)
                    if turn:
                        pe.wait_ge(x_in[(j + 1) % 4], it * 32 + 32 * ((j + 1) // 4 + 1))
                        wait(pe, "diag_made", n * 2 + 4)
                        wait(pe, "shift_in", n + 2)
                        for u in range(2):
                            turned_block(n, j, u)
                    if attend:
                        wait(pe, "fsq_made", i + 1)
                        for m in range(2):
                            mm = pe.matmul(pt[0:HID, 0, 0:2 * W], ones[0:HC, :], fsq[:, m].rearrange("p t w -> p (t w)"),
                                           start=(m == 0), stop=(m == 1))
                        mm.then_inc(S["fn_mm"], 1)
                        for a, w in enumerate((wq, wk)):
                            for m in range(2):
                                mm = pe.matmul(pqk(a), w[:, m, :], feat[:, m].rearrange("p t w -> p (t w)"),
                                               start=(m == 0), stop=(m == 1))
                        mm.then_inc(S["qk_mm"], 1)
                    if weigh:
                        wait(pe, "weighted", n * 2 + 2)
                        if not (isinstance(n, int) and n <= 0):
                            wait(pe, "v_ready", n)
                    for lap in range(LAPS):
                        if lap == 6 and attend:
                            wait(pe, "e_norm", i + 1)
                        if turn:
                            turned_block(n, j, 2 + lap)
                        if weigh:
                            weighted_sums(j, 2 * BLOCKS * lap // LAPS, 2 * BLOCKS * (lap + 1) // LAPS)
                        if lap == 1 and attend:
                            wait(pe, "qk_made", i * 5 + 5)
                            wait(pe, "term_made", i + 1)
                            for t in range(2):
                                mm = pe.matmul(psc[0:W, t, 0:HEADS * KEYS], Q[:, t, :],
                                               K[:, 1 - t].rearrange("p h j -> p (h j)"), start=True, stop=True)
                            mm.then_inc(S["s_mm"], 1)
                            wait(pe, "v_ready", i + 1)
                            for t in range(2):
                                for m in range(2):
                                    mm = pe.matmul(pq[0:W, 0, HID * t:HID * t + HID], vfeat[:, m, 1 - t, :], wv[:, m, :],
                                                   start=(m == 0), stop=(m == 1))
                            mm.then_inc(S["v_mm"], 1)
                        if lap == 6 and attend:
                            for t in range(2):
                                for h in range(HEADS):
                                    a = (t * HEADS + h) * W
                                    mm = pe.transpose(pt[0:KEYS, 0, a:a + W], E[:, t, h, :], eye[0:W, 0:W])
                            mm.then_inc(S["t_mm"], 1)
                        if lap == 7 and attend:
                            wait(pe, "et_made", i + 1)
                            wait(pe, "v_made", i + 1)
                            for h in range(HEADS):
                                for t in range(2):
                                    mm = pe.matmul(psc[DH * h:DH * h + DH, 0, W * t:W * t + W],
                                                   V[:, t, DH * h:DH * h + DH], ET[:, t, h, :], start=True, stop=True)
                            mm.then_inc(S["o_mm"], 1)
                        if lap == 8 and attend:
                            wait(pe, "o_made", i + 1)
                            for t in range(2):
                                for m in range(2):
                                    a = (t * 2 + m) * W
                                    mm = pe.matmul(psc[0:HC, 1, a:a + W], wc[:, t, HC * m:HC * m + HC], O[:, t, :],
                                                   start=True, stop=True)
                            mm.then_inc(S["term_mm"], 1)
                        if lap == 4 and prep:
                            wait(pe, "diag_made", n * 2 + 6)
                            if not (isinstance(n, int) and n < -1):
                                wait(pe, "shift_in", n + 2)
                            pe.matmul(pshift[0:HC + 1, 0, 0:C], ones[0:HC, 0:HC + 1],
                                      shifts[:].rearrange("p m c -> p (m c)"), start=True, stop=True)\
                                .then_inc(S["shift_mm"], 1)

                def pqk(a):
                    return pq[0:HID, 0, 2 * W * (a + 1):2 * W * (a + 2)]

                before()
                schedule(pe, step)

            @block.scalar
            def _(act):
                def before():
                    act.wait_ge(S["v4"], 1)
                    nc.scalar.activation(stat[:, 1], var, ACT.Sqrt).then_inc(S["v5"], 1)
                    act.wait_ge(S["wc_mm"], 1)
                    for t in range(2):
                        nc.scalar.activation(wc[:, t, :], psc[0:HID, t, 0:C], ACT.Copy).then_inc(S["wc_made"], 1)
                    act.wait_ge(S["cleared"], 3)
                    nc.scalar.activation(bias[:, 0, :], pt[0:HC, 0, 0:2], ACT.Copy).then_inc(S["wc_made"], 1)

                def turn_out(n, j, u):
                    wait(act, "turn_mm", n * UNITS + (UNITS + u + 1))
                    nc.scalar.activation(xT[:, (j + 1) % 2, UB * u:UB * u + UB, :].rearrange("p b c -> p (b c)"),
                                         pturn[0:PX, u % 2, 0:UB * C], ACT.Copy)
                    if u > 1:
                        wait(act, "turned", n * UNITS + (UNITS + u - 1))
                    elif u == 0:
                        wait(act, "n_sqrt", n + 1)
                    for r in range(UB):
                        ins = nc.scalar.activation(junk[:, u % 2, r], pturn[0:PX, u % 2, C * r:C * r + C], ACT.Square,
                                                   accum_out=n2[:, UB * u + r:UB * u + r + 1])
                    ins.then_inc(S["turned"], 1)

                def step(it, j, prep, turn, weigh, attend):
                    n, i = it * 4 + j, it * 4 + (j - 1)

                    def turn_units(a, b):
                        if turn:
                            for u in range(a, b):
                                turn_out(n, j, u)

                    if weigh:
                        wait(act, "turned", n * UNITS + UNITS)
                        nc.scalar.activation(nrm[:], n2[:], ACT.Sqrt).then_inc(S["n_sqrt"], 1)
                    if attend:
                        wait(act, "sums_mm", i + 1)
                        nc.scalar.activation(vfeat[:].rearrange("p m t w -> p (m t w)"), psum[0:HC, 0, 0:2 * TERMS],
                                             ACT.Copy).then_inc(S["v_ready"], 1)
                    turn_units(0, 2)
                    if attend:
                        wait(act, "fn_mm", i + 1)
                        nc.scalar.activation(fn[:], pt[0:HID, 0, 0:2 * W], ACT.Sqrt).then_inc(S["fn_sqrt"], 1)
                    turn_units(2, 4)
                    if attend:
                        wait(act, "v_mm", i + 1)
                        nc.scalar.activation(V[0:W].rearrange("p t c -> p (t c)"), pq[0:W, 0, 0:2 * HID], ACT.Copy)\
                            .then_inc(S["v_made"], 1)
                        wait(act, "s_sub", i + 1)
                        nc.scalar.activation(E[:], E[:], ACT.Exp, scale=SCALE).then_inc(S["e_made"], 1)
                    turn_units(4, 7)
                    if prep:
                        wait(act, "shift_mm", n + 3)
                        nc.scalar.activation(diag[HC:HC + 1, j % 2].rearrange("p m c -> p (m c)"),
                                             pshift[HC:HC + 1, 0, 0:C], ACT.Copy).then_inc(S["shift_in"], 1)
                    turn_units(7, 9)
                    if attend:
                        wait(act, "t_mm", i + 1)
                        nc.scalar.activation(ET_fsq[0:KEYS], pt[0:KEYS, 0, 0:2 * HEADS * W],
                                             ACT.Copy).then_inc(S["et_made"], 1)
                    turn_units(9, 10)
                    if attend:
                        wait(act, "o_mm", i + 1)
                        nc.scalar.activation(O[:].rearrange("p t w -> p (t w)"), psc[0:HID, 0, 0:2 * W], ACT.Copy)\
                            .then_inc(S["o_made"], 1)
                    turn_units(10, UNITS)

                before()
                schedule(act, step)

            @block.vector
            def _(dve):
                dve.sem_inc(S["term_made"], 1)

                def before():
                    dve.wait_ge(S["w_in"], 10 * 16)
                    root = float(C) ** 0.5
                    for j, w in enumerate((wq, wk, wv)):
                        for m in range(2):
                            ins = nc.vector.tensor_scalar(w[:, m, :], w[:, m, :], gains[:, j, m:m + 1], root,
                                                          ALU.mult, ALU.mult)
                        ins.then_inc(S["scaled"], 1)
                    dve.wait_ge(S["sum_in"], 64)
                    for a in range(2):
                        for m in range(2):
                            ins = nc.vector.reduce_sum(
                                tot[:, a, m, :].rearrange("p (g q) -> p g q", g=2),
                                (sums, squares)[a][:, m].rearrange("p g h q -> p g q h"), AX.X)
                        ins.then_inc(S["tots"], 1)
                    both = lambda a: a.rearrange("p m b -> p (m b)")
                    dve.wait_ge(S["gm_mm"], 1)
                    nc.vector.tensor_scalar(both(stat[:, 2]), pq[0:HC, 0, 0:2 * B], -1.0, None, ALU.mult)\
                        .then_inc(S["v1"], 1)
                    dve.wait_ge(S["v1"], 1)
                    nc.vector.tensor_tensor(both(stat[:, 3]), both(stat[:, 2]), both(stat[:, 2]), ALU.mult)\
                        .then_inc(S["v2"], 1)
                    dve.wait_ge(S["v2"], 1)
                    nc.vector.tensor_tensor(both(var), pq[0:HC, 0, 2 * B:4 * B], both(stat[:, 3]), ALU.subtract)\
                        .then_inc(S["gm_copy"], 1)
                    dve.wait_ge(S["gm_copy"], 1)
                    nc.vector.tensor_scalar(var, var, 0.0, EPS, ALU.max, ALU.add).then_inc(S["v4"], 1)
                    dve.wait_ge(S["v5"], 1)
                    nc.vector.reciprocal(stat[:, 3], stat[:, 1]).then_inc(S["v3"], 1)
                    dve.wait_ge(S["v3"], 1)
                    nc.vector.tensor_scalar(stat[:, 0], stat[:, 3], 1.0 / W, None, ALU.mult).then_inc(S["v6"], 1)
                    nc.vector.tensor_tensor(stat[:, 1], stat[:, 2], stat[:, 3], ALU.mult).then_inc(S["v6"], 1)
                    dve.wait_ge(S["v6"], 2)

                def step(it, j, prep, turn, weigh, attend):
                    n, i = it * 4 + j, it * 4 + (j - 1)
                    k, slot, later = j % 4, (j - 1) % 4, (j + 2) % 4
                    late, late_slot = j >= 2, (j - 2) % 4
                    last = isinstance(it, int) and j == images

                    def place(offset):
                        r = (j + offset) % 4
                        return r // 2, it * 2 + ((j + offset) // 4 * 2 + r % 2)

                    def column_sums(m):
                        nc.vector.reduce_sum(raw[:, m, 1, :], x[0:HC, k, m].rearrange("p h w -> p w h"), AX.X)\
                            .then_inc(S["cs_made"], 1)

                    if weigh:
                        wait(dve, "n_sqrt", n + 1)
                        nc.vector.tensor_scalar(nrm[:], nrm[:], 1e-12, None, ALU.max).then_inc(S["n_max"], 1)
                        wait(dve, "n_max", n + 1)
                        nc.vector.reciprocal(nrm[:], nrm[:]).then_inc(S["n_inv"], 1)
                        wait(dve, "n_inv", n + 1)
                        if not (isinstance(n, int) and n <= 0):
                            wait(dve, "sums_mm", n)
                        inv = lambda w: nrm[:].rearrange("p (b o) -> p b o", o=1).broadcast_to([PX, BLOCKS, w])
                        which = lambda a, w: ind[:, a:a + w].rearrange("p (o w) -> p o w", o=1)\
                            .broadcast_to([PX, BLOCKS, w])
                        nc.vector.tensor_tensor(row_places, which(0, UB), inv(UB), ALU.mult).then_inc(S["weighted"], 1)
                        nc.vector.tensor_tensor(by_block[:, :, H:TERMS], which(UB, W), inv(W), ALU.mult)\
                            .then_inc(S["weighted"], 1)
                    if attend:
                        wait(dve, "fn_sqrt", i + 1)
                        nc.vector.tensor_scalar(fn[:], fn[:], 1e-12, None, ALU.max).then_inc(S["fn_max"], 1)
                        wait(dve, "fn_max", i + 1)
                        nc.vector.reciprocal(fn[:], fn[:]).then_inc(S["fn_inv"], 1)
                        wait(dve, "fn_inv", i + 1)
                        wait(dve, "qk_mm", i + 1)
                        nc.vector.tensor_tensor(Q[:].rearrange("p t w -> p (t w)"), pq[0:HID, 0, 2 * W:4 * W],
                                                fn[:], ALU.mult).then_inc(S["qk_made"], 1)
                        for h in range(HEADS):
                            r = slice(DH * h, DH * h + DH)
                            nc.vector.tensor_tensor(K[r, :, h, 0:W],
                                                    pq[r, 0, 4 * W:6 * W].rearrange("p (t w) -> p t w", t=2),
                                                    fn[r, :].rearrange("p (t w) -> p t w", t=2), ALU.mult)\
                                .then_inc(S["qk_made"], 1)
                    if late:
                        nc.vector.tensor_tensor(x[0:HC, late_slot, 0], x[0:HC, late_slot, 0],
                                                along_columns(late_slot, 0), ALU.add).then_inc(S["added0"], 1)
                    if weigh:
                        half, at = place(0)
                        nc.vector.tensor_copy(raw[:, :, 0, :], sums[:, :, half, :, bass.ds(at, 1)]
                                              .rearrange("p m h o -> p m (h o)")).then_inc(S["rows_in"], 1)
                    if attend:
                        wait(dve, "s_mm", i + 1)
                        scores = psc[0:W, :, 0:HEADS * KEYS].rearrange("p t (h j) -> p t h j", h=HEADS)
                        over = lambda z: z.rearrange("p (t h o) -> p t h o", t=2, o=1).broadcast_to([W, 2, HEADS, KEYS])
                        nc.vector.reduce_max(zs[:, 0, :].rearrange("p (t h) -> p t h", t=2), scores, AX.X)\
                            .then_inc(S["mx_made"], 1)
                        wait(dve, "mx_made", i + 1)
                        nc.vector.tensor_tensor(E[:], scores, over(zs[:, 0, :]), ALU.subtract).then_inc(S["s_sub"], 1)
                    if prep:
                        half, at = place(2)
                        nc.vector.tensor_copy(cols[:, later], stat[:, 0:4, :, bass.ds(at + HB * half, 1)]
                                              .rearrange("p a m o -> p a (m o)")).then_inc(S["fetched"], 1)
                        wait(dve, "fetched", n + 3)
                        if not (isinstance(n, int) and n < -1):
                            wait(dve, "shift_mm", n + 2)
                        if not (isinstance(n, int) and n < 0):
                            wait(dve, "turn_mm", n * UNITS + UNITS)
                        for m in range(2):
                            ins = nc.vector.tensor_scalar(diag[0:HC, j % 2, m, :], eye[0:HC, 0:HC],
                                                          cols[:, later, 3, m:m + 1], None, ALU.mult)
                        ins.then_inc(S["diag_made"], 1)
                        for m in range(2):
                            ins = nc.vector.tensor_scalar(shifts[:, m, :], eye[0:HC, 0:HC],
                                                          cols[:, later, 1, m:m + 1], None, ALU.mult)
                        ins.then_inc(S["diag_made"], 1)
                    if attend:
                        wait(dve, "e_made", i + 1)
                        th = lambda z: z.rearrange("p (t h) -> p t h", t=2)
                        nc.vector.reduce_sum(th(zs[:, 1, :]), E[:, :, :, 0:W], AX.X).then_inc(S["z_k"], 1)
                        nc.vector.reduce_sum(th(zs[:, 2, :]), E[:, :, :, KEYS - NMEM:KEYS], AX.X).then_inc(S["z_m"], 1)
                        wait(dve, "z_m", i + 1)
                        nc.vector.scalar_tensor_tensor(zs[:, 3, :], zs[:, 1, :], float(REP), zs[:, 2, :],
                                                       ALU.mult, ALU.add).then_inc(S["z_made"], 1)
                        wait(dve, "z_made", i + 1)
                        nc.vector.reciprocal(zs[:, 4, :], zs[:, 3, :]).then_inc(S["z_inv"], 1)
                        wait(dve, "z_inv", i + 1)
                        nc.vector.tensor_tensor(E[:], E[:], over(zs[:, 4, :]), ALU.mult).then_inc(S["e_norm"], 1)
                    if weigh:
                        dve.wait_ge(x_in[k], it * 32 + 32 * (j // 4 + 1))
                        column_sums(0)
                        column_sums(1)
                    if attend:
                        wait(dve, "term_mm", i + 1)
                        wait(dve, "added", i + 1)
                        nc.vector.tensor_tensor(
                            term[:, slot % 2],
                            psc[0:HC, 1, 0:4 * W].rearrange("p (t m w) -> p t m w", t=2, m=2),
                            bias[:].rearrange("p t (m o) -> p t m o", o=1).broadcast_to([HC, 2, 2, W]), ALU.add)\
                            .then_inc(S["term_made"], 1)
                    if weigh:
                        wait(dve, "cs_made", n * 2 + 2)
                        wait(dve, "rows_in", n + 1)
                        for m in range(2):
                            ins = nc.vector.tensor_scalar(feat[:, m], raw[:, m], cols[:, k, 0, m:m + 1],
                                                          cols[:, k, 1, m:m + 1], ALU.mult, ALU.add)
                        ins.then_inc(S["f_made"], 1)
                        wait(dve, "f_made", n + 1)
                        nc.vector.tensor_tensor(fsq, feat[:], feat[:], ALU.mult).then_inc(S["fsq_made"], 1)
                    if attend:
                        wait(dve, "term_made", i + 2)
                        nc.vector.tensor_tensor(x[0:HC, slot, 0], x[0:HC, slot, 0], along_rows(slot, 0), ALU.add)\
                            .then_inc(S["row_added0"], 1)
                        if last:
                            wait(dve, "row_added0", i + 1)
                            nc.vector.tensor_tensor(x[0:HC, slot, 0], x[0:HC, slot, 0], along_columns(slot, 0), ALU.add)\
                                .then_inc(S["added0"], 1)

                before()
                schedule(dve, step)


def laid_out(a):
    t = {n.split("conv_")[-1]: np.asarray(v) for n, v in a.items()}
    out = {
        "x": t["x"].reshape(2, HB, C, H, W).transpose(2, 0, 3, 1, 4),
        "z": t["z"].reshape(FEMB, KH * KH),
        "W1T": t["W1"].T, "W2T": t["W2"].T, "W3T": t["W3"].T,
        "distance_map": t["distance_map"].reshape(KH, KH),
    }
    for n in ("b1", "f1", "b2", "f2"):
        out[n] = t[n].reshape(FORD, 1)
    for n in ("deltas", "shift", "bias"):
        out[n] = t[n].reshape(1, C)
    halves = lambda a: np.moveaxis(a.reshape((2, HC) + a.shape[1:]), 0, 1)
    for n in ("Wq", "Wk", "Wv"):
        out[n + "T"] = halves(t[n].T)
    out["Wo"], out["bo"] = halves(t["Wo"]), halves(t["bo"])
    out["WrT"] = halves(t["Wr"].reshape(C, 2, C).transpose(2, 1, 0))
    out["gains"] = halves(np.stack([t["gq"], t["gk"], t["gv"]], axis=1)).transpose(0, 2, 1)
    out["mem_kT"] = t["mem_kv"][0].transpose(0, 2, 1)
    out["mem_v"] = t["mem_kv"][1].transpose(1, 0, 2).reshape(t["mem_kv"].shape[2], -1)
    return out


def program(nc, d, y):
    khat = nc.dram_tensor("khat", (C, 3, NE * U), F32, kind="Internal").ap()
    x1 = nc.dram_tensor("x1", (B, C, H, W), F32, kind="Internal").ap()
    rsum = nc.dram_tensor("rsum", (C, 2, 2, H, HB), F32, kind="Internal").ap()
    filters(nc, d, khat)
    convolution(nc, d, khat, x1, rsum)
    attention(nc, d, x1, rsum, y)


def kernel(**inputs):
    import concourse.bacc as bacc
    from concourse.bass_utils import run_bass_kernel_spmd

    nc = bacc.Bacc("TRN2", target_bir_lowering=False, num_devices=1)
    arrays, d = {}, {}
    for name, a in {**laid_out(inputs), **constants()}.items():
        arrays[f"in_{name}"] = np.ascontiguousarray(a)
        d[name] = nc.dram_tensor(f"in_{name}", a.shape, F32, kind="ExternalInput").ap()
    y = nc.dram_tensor("out", (B, C, H, W), F32, kind="ExternalOutput").ap()
    program(nc, d, y)
    return run_bass_kernel_spmd(nc, [arrays], core_ids=[0]).results[0]["out"]
```

```python
from contextlib import ExitStack

import numpy as np

import concourse.bass as bass
from concourse import mybir

ALU = mybir.AluOpType
ACT = mybir.ActivationFunctionType
F32 = mybir.dt.float32
AX = mybir.AxisListType

B, C, H, W = 64, 192, 56, 56
KH = 55
MID = KH // 2
GROUPS, CG = 32, C // 32
FEMB, FORD = 32, 64
L = H + MID
U = L // 2 + 1
NE = 2 * W - 1
HB = B // 2
HALF = 64
KP = HALF + H
EPS = 1e-5
WP = 64
HC = C // 2

A_UNITS = [3, 3, 3, 3, 2, 2]
B_UNITS, B_MM = 6, 7
T_UNITS, T_MM = 8, 4
D_UNITS, D_BQ = 4, 8
MIX = "A0 A1 A2 A3 T0 T1 A4 T2 T3 D0 A5 T4 T5 D1 T6 T7 D2 D3".split()
assert B_UNITS * B_MM == U and T_UNITS * T_MM == HB and D_UNITS * D_BQ == HB and 2 * sum(A_UNITS) == HB


def constants():
    h, u, i = np.arange(H), np.arange(U), np.arange(KH)
    th = 2 * np.pi / L * (np.outer(h, u) % L)
    fwd = np.zeros((KP, 2, 2, U), np.float64)
    inv = np.zeros((2, U, 2, KP), np.float64)
    mean = np.zeros((KP, KP), np.float64)
    weight = np.where(u == 0, 1.0, 2.0) / L
    for p in range(2):
        rows = slice(HALF * p, HALF * p + H)
        fwd[rows, 0, p] = np.cos(th)
        fwd[rows, 1, p] = -np.sin(th)
        inv[p, :, 0, rows] = (np.cos(th) * weight).T
        inv[p, :, 1, rows] = (-np.sin(th) * weight).T
        mean[rows, rows] = 1.0 / (2 * H)
    tk = 2 * np.pi / L * (np.outer(i - MID, u) % L)
    taps = np.concatenate([np.cos(tk), -np.sin(tk)], axis=1)
    centre = (np.arange(KH) == MID).astype(np.float64)[:, None]
    f = lambda a: np.ascontiguousarray(a, dtype=np.float32)
    return {
        "k_fwd": f(fwd.reshape(KP, 4 * U)), "k_inv": f(inv.reshape(2 * U, 2 * KP)), "k_mean": f(mean),
        "k_gmean": f(np.kron(np.eye(HC // CG), np.full((CG, CG), 1.0 / (CG * H * W)))),
        "k_taps": f(taps), "k_centre": f(centre),
        "k_ones": f(np.ones((1, 8 * H * W))),
        "k_ind": f(np.hstack([np.kron(np.eye(2), np.ones((W, 1))), np.tile(np.eye(W), (2, 1))])),
        "k_eye": f(np.eye(128)), "k_eye_2w": f(np.eye(2 * W)),
    }


def filters(nc, d, khat, shared):
    JH = MID + 1
    NPOS = JH * KH
    NCH, CJ = 4, JH // 4
    CH = CJ * KH
    PI = float(np.pi)
    INV2PI = float(np.float32(1 / (2 * np.pi)))
    ROUND = float(1.5 * 2 ** 23)
    TWO_PI_HI = 6.28125
    TWO_PI_LO = float(np.float32(2 * np.pi - 6.28125))
    PI_IN = 3.1415925
    JB = 5
    NB = KH // JB
    LO = W - 1 - MID
    FIRST = 5
    assert NCH * CJ == JH and 2 * FORD == 128 and NB * JB == KH
    x, stats, x_in, spare_clear, st = (shared[n] for n in ("x", "stats", "x_in", "spare_clear", "st"))
    with ExitStack() as ctx:
        sb = lambda n, s: ctx.enter_context(nc.sbuf_tensor("f_" + n, s, F32))
        sem = lambda n: ctx.enter_context(nc.semaphore("f_" + n))
        arg = sb("arg", [2 * FORD, NPOS])
        turns = sb("turns", [2 * FORD, NPOS])
        h1 = sb("h1", [2 * FORD, NPOS])
        w1T = sb("w1T", [FEMB, FORD])
        w2T = sb("w2T", [2 * FORD, FORD])
        w3T = sb("w3T", [2 * FORD, 2, C])
        vec = sb("vec", [2 * FORD, 4])
        dist = sb("dist", [KH, KH])
        ndist = sb("ndist", [KH, KH])
        chan = sb("chan", [KH, 3, C])
        absd = sb("absd", [KH, C])
        centre = sb("centre", [KH, 1])
        taps_dft = sb("taps", [KH, 2 * U])
        k = sb("k", [KH, KH, C])
        kf = sb("kf", [HC, 2, NE, U])
        z = kf[0:FEMB].rearrange("p a e u -> p (a e u)")[:, 0:KH * KH]
        pnet = ctx.enter_context(nc.psum_tensor("f_pnet", [128, 2, 512], F32))
        pk = ctx.enter_context(nc.psum_tensor("f_pk", [128, 2, 512], F32))
        pf = ctx.enter_context(nc.psum_tensor("f_pf", [128, 2, 512], F32))
        net_in, loaded, absed, w3_clear = sem("net_in"), sem("loaded"), sem("absed"), sem("w3_clear")
        net_mm, arg_made, red, sine = sem("net_mm"), sem("arg_made"), sem("red"), sem("sine")
        decayed, shifted, tap_mm, tap_made, biased = sem("decayed"), sem("shifted"), sem("tap_mm"), sem("tap_made"), sem("biased")
        dft_mm, dft_re, dft_im, zeroed = sem("dft_mm"), sem("dft_re"), sem("dft_im"), sem("zeroed")
        stored = [sem("stored0"), sem("stored1")]
        NET_LOADS, LOADS = 5 * 16, 8 * 16

        def pair(g):
            return k[:, g:g + MID + 1:MID, :] if g < MID else k[:, KH - 1:KH, :]

        with nc.Block() as block:

            @block.sync
            def _(sp):
                def whole(dst, src, s):
                    sp.dma_start(dst, src).then_inc(s, 16)
                whole(z, d["z"], net_in)
                whole(w1T[:], d["W1T"], net_in)
                for h in range(2):
                    whole(vec[FORD * h:FORD * h + FORD, :], d["vec"], net_in)
                whole(w2T[0:FORD, :], d["W2T"], net_in)
                whole(w2T[FORD:2 * FORD, :], d["W2T"], loaded)
                whole(dist[:], d["distance_map"], loaded)
                v = d["chan"]
                whole(chan[:], bass.AP(tensor=v.tensor, offset=v.offset, ap=[[0, KH], [C, 3], [1, C]]), loaded)
                whole(centre[:], d["k_centre"], loaded)
                whole(taps_dft[:], d["k_taps"], loaded)
                sp.wait_ge(w3_clear, 1)
                for h in range(2):
                    whole(w3T[FORD * h:FORD * h + FORD, h, :], d["W3T"], loaded)
                whole(shared["mean"][:], d["k_mean"], loaded)
                for s in range(2):
                    sp.wait_ge(spare_clear, s + 1)
                    for c in range(CG):
                        for p in range(2):
                            sp.dma_start(x[HALF * p:HALF * p + H, s, c, :, :], d["x"][s * CG + c, p])\
                                .then_inc(x_in[s], 16)
                for m in range(2):
                    for piece, (rows, banks) in enumerate(((slice(0, LO + FIRST * JB), FIRST),
                                                           (slice(LO + FIRST * JB, NE), NB))):
                        sp.wait_ge(dft_re, NB * m + banks)
                        sp.wait_ge(dft_im, NB * m + banks)
                        sp.wait_ge(zeroed, 2)
                        dst = khat[HC * m:HC * m + HC].rearrange("c a (e u) -> c a e u", u=U)[:, :, rows, :]
                        sp.dma_start(dst.rearrange("c a e u -> c a (e u)"),
                                     kf[:, :, rows, :].rearrange("c a e u -> c a (e u)")).then_inc(stored[piece], 16)
                for piece in range(2):
                    sp.wait_ge(stored[piece], 32)

            @block.tensor
            def _(pe):
                pe.wait_ge(net_in, NET_LOADS)
                for layer in range(2):
                    if layer:
                        pe.wait_ge(loaded, LOADS)
                    for n in range(NCH):
                        g = layer * NCH + n
                        if layer:
                            pe.wait_ge(sine, n + 1)
                        if g >= 2:
                            pe.wait_ge(arg_made, g - 1)
                        for h in range(2):
                            part = slice(FORD * h, FORD * h + FORD)
                            if layer:
                                lhs, rhs = w2T[part, :], h1[part, CH * n:CH * n + CH]
                            else:
                                lhs, rhs = w1T[:], z[:, MID * KH * h + CH * n:MID * KH * h + CH * n + CH]
                            mm = pe.matmul(pnet[part, g % 2, 0:CH], lhs, rhs, start=True, stop=True)
                        mm.then_inc(net_mm, 1)
                pe.wait_ge(sine, 2 * NCH)
                for g in range(JH):
                    if g >= 2:
                        pe.wait_ge(tap_made, g - 1)
                    pe.matmul(pk[0:KH, g % 2, 0:2 * C], h1[:, KH * g:KH * g + KH],
                              w3T[:].rearrange("p h c -> p (h c)"), start=True, stop=True).then_inc(tap_mm, 1)
                pe.wait_ge(biased, 1)
                for m in range(2):
                    for g in range(NB):
                        n = m * NB + g
                        if n >= 2:
                            pe.wait_ge(dft_re, n - 1)
                            pe.wait_ge(dft_im, n - 1)
                        for j in range(JB):
                            mm = pe.matmul(pf[0:HC, n % 2, 2 * U * j:2 * U * j + 2 * U],
                                           k[:, KH - 1 - (JB * g + j), HC * m:HC * m + HC], taps_dft[:],
                                           start=True, stop=True)
                        mm.then_inc(dft_mm, 1)

            @block.scalar
            def _(act):
                for g in range(2 * NCH):
                    n = g % NCH
                    act.wait_ge(red, 5 * g + 5)
                    nc.scalar.activation(h1[:, CH * n:CH * n + CH], arg[:, CH * n:CH * n + CH], ACT.Sin)\
                        .then_inc(sine, 1)
                act.wait_ge(loaded, LOADS)
                nc.scalar.activation(absd[:], chan[:, 0, :], ACT.Abs).then_inc(absed, 1)
                act.wait_ge(absed, 2)
                for g in range(JH):
                    for j in ((g, MID + g) if g < MID else (KH - 1,)):
                        e = nc.scalar.activation(k[:, j, :], absd[:], ACT.Exp, scale=ndist[:, j:j + 1])
                    e.then_inc(decayed, 1)
                for n in range(2 * NB):
                    m, g = divmod(n, NB)
                    act.wait_ge(dft_mm, n + 1)
                    if n == 0:
                        act.wait_ge(zeroed, 2)
                    if n >= NB:
                        act.wait_ge(stored[0 if g < FIRST else 1], 16)
                    src = pf[0:HC, n % 2, 0:2 * U * JB].rearrange("p (j r u) -> p r j u", j=JB, r=2)
                    e0 = LO + JB * g
                    nc.scalar.activation(kf[:, 0, e0:e0 + JB, :], src[:, 0], ACT.Copy).then_inc(dft_re, 1)
                    nc.scalar.activation(kf[:, 1, e0:e0 + JB, :], src[:, 1], ACT.Copy).then_inc(dft_im, 1)

            @block.gpsimd
            def _(pool):
                pool.memset(w3T[:], 0.0).then_inc(w3_clear, 1)
                pool.wait_ge(w3_clear, 1)
                for s in range(2):
                    pool.memset(x[32:64, s], 0.0).then_inc(spare_clear, 1)
                pool.wait_ge(loaded, LOADS)
                pool.wait_ge(spare_clear, 2)
                for g in range(JH):
                    n = 2 if g < MID else 1
                    pool.wait_ge(decayed, g + 1)
                    nc.gpsimd.tensor_tensor(pair(g), pair(g), chan[:, 1:2, :].broadcast_to([KH, n, C]), ALU.add)\
                        .then_inc(shifted, 1)
                pool.wait_ge(shifted, JH)
                for rows in (slice(0, LO), slice(LO + KH, NE)):
                    for a in range(2):
                        y = pool.memset(kf[:, a, rows, :], 0.0)
                    y.then_inc(zeroed, 1)

            @block.vector
            def _(dve):
                for g in range(2 * NCH):
                    layer, n = divmod(g, NCH)
                    part = slice(CH * n, CH * n + CH)
                    v, t = arg[:, part], turns[:, part]
                    bcol, fcol = vec[:, 2 * layer:2 * layer + 1], vec[:, 2 * layer + 1:2 * layer + 2]
                    dve.wait_ge(net_mm, g + 1)
                    if layer:
                        dve.wait_ge(sine, n + 1)
                    nc.vector.tensor_scalar(v, pnet[:, g % 2, 0:CH], bcol, fcol, ALU.add, ALU.mult)\
                        .then_inc(arg_made, 1)
                    dve.wait_ge(arg_made, g + 1)
                    nc.vector.tensor_scalar(t, v, INV2PI, ROUND, ALU.mult, ALU.add).then_inc(red, 1)
                    dve.wait_ge(red, 5 * g + 1)
                    nc.vector.tensor_scalar(t, t, ROUND, None, ALU.subtract).then_inc(red, 1)
                    dve.wait_ge(red, 5 * g + 2)
                    nc.vector.scalar_tensor_tensor(v, t, -TWO_PI_HI, v, ALU.mult, ALU.add).then_inc(red, 1)
                    dve.wait_ge(red, 5 * g + 3)
                    nc.vector.scalar_tensor_tensor(v, t, -TWO_PI_LO, v, ALU.mult, ALU.add).then_inc(red, 1)
                    dve.wait_ge(red, 5 * g + 4)
                    nc.vector.tensor_scalar(v, v, PI_IN, -PI_IN, ALU.min, ALU.max).then_inc(red, 1)
                    if g == NCH - 1:
                        dve.wait_ge(loaded, LOADS)
                        nc.vector.tensor_scalar(ndist[:], dist[:], -1.0, None, ALU.mult).then_inc(absed, 1)
                for g in range(JH):
                    n = 2 if g < MID else 1
                    dve.wait_ge(shifted, g + 1)
                    dve.wait_ge(tap_mm, g + 1)
                    nc.vector.tensor_tensor(pair(g), pair(g), pk[0:KH, g % 2, C * (2 - n):2 * C]
                                            .rearrange("p (j c) -> p j c", j=n), ALU.mult).then_inc(tap_made, 1)
                dve.wait_ge(tap_made, JH)
                nc.vector.scalar_tensor_tensor(k[:, MID, :], chan[:, 2, :], centre[:, 0:1], k[:, MID, :],
                                               ALU.mult, ALU.add).then_inc(biased, 1)
                dve.wait_ge(x_in[0], 32 * CG)
                for b in range(HB):
                    ins = nc.vector.bn_stats(stats[:, b, :], x[0:KP, 0, :, b, :])
                ins.then_inc(st, 3)


def convolution(nc, d, khat, x1, rsum, shared, groups=GROUPS):
    IT = groups // 2
    CI = 2 * CG
    NA, NBU, NT, ND = len(A_UNITS) * CI, B_UNITS * CI, T_UNITS * CI, D_UNITS * CI
    RING = 4 * T_MM
    MEAN_AT = 2
    SPLIT = 40
    AHEAD = 2
    A_FREE = len(A_UNITS) * CG
    STAT_CH = {1: range(0, 11), 2: range(11, 22), 3: range(22, 32)}
    with ExitStack() as ctx:
        sb = lambda n, s: ctx.enter_context(nc.sbuf_tensor("c_" + n, s, F32))
        ps = lambda n: ctx.enter_context(nc.psum_tensor("c_" + n, [128, 2, 512], F32))
        sem = lambda n: ctx.enter_context(nc.semaphore("c_" + n))
        x, stats, mean, x_in, st = (shared[n] for n in ("x", "stats", "mean", "x_in", "st"))
        xn = sb("xn", [128, CG, HB, WP])
        xhat = sb("xhat", [128, 2 * U, HB])
        toep = sb("toep", [128, 2, 2, W, U])
        prod = sb("prod", [2 * W, HB, 2, U])
        prodT = sb("prodT", [2 * U, RING, 2, W])
        fwd = sb("fwd", [KP, 4 * U])
        inv = sb("inv", [2 * U, 2, KP])
        eye = sb("eye", [2 * W, 2 * W])
        part = sb("part", [KP, 3, HB])
        q = sb("q", [KP, 2, HB])
        mv = sb("mv", [KP, 3, HB])
        scale = sb("scale", [KP, HB])
        shift = sb("shift", [KP, HB])
        rs = sb("rs", [KP, CI, 2, HB])
        square = sb("square", [KP, HB // 2, W])
        pa, pb, pt, pd = ps("pa"), ps("pb"), ps("pt"), ps("pd")
        const_in, cleared = sem("const_in"), sem("cleared")
        toep_clear = [sem("toep_clear0"), sem("toep_clear1")]
        toep_made = sem("toep_made")
        toep_in = [sem("toep_in0"), sem("toep_in1")]
        a_mm, a_act, a_dve = sem("a_mm"), sem("a_act"), sem("a_dve")
        b_mm, b_act = sem("b_mm"), sem("b_act")
        t_mm, t_act, t_dve = sem("t_mm"), sem("t_act"), sem("t_dve")
        d_mm, d_dve = sem("d_mm"), sem("d_dve")
        q_made, mean_mm, mv_read, var_made, std_made, sc = (
            sem("q_made"), sem("mean_mm"), sem("mv_read"), sem("var_made"), sem("std_made"), sem("sc"))
        scaled, multiplied, normed = sem("scaled"), sem("multiplied"), sem("normed")
        summed, squared, sq_summed = sem("summed"), sem("squared"), sem("sq_summed")
        stored = [sem("stored0"), sem("stored1")]

        with nc.Block() as block:

            @block.sync
            def _(sp):
                for dst, name in ((fwd[:], "k_fwd"), (inv[:].rearrange("p r h -> p (r h)"), "k_inv"),
                                  (eye[:], "k_eye_2w")):
                    sp.dma_start(dst, d[name]).then_inc(const_in, 16)
                def load_x(slot, c, channel):
                    for p in range(2):
                        sp.dma_start(x[HALF * p:HALF * p + H, slot, c, :, :], d["x"][channel, p])\
                            .then_inc(x_in[slot], 16)

                def load_toep(par, channel):
                    src = khat[channel, 0, 0:W * U]
                    src = bass.AP(tensor=src.tensor, offset=src.offset, ap=[[U, W], [NE * U, 2], [1, W * U]])
                    sp.dma_start(toep[0:W, par].rearrange("w r v u -> w r (v u)"), src).then_inc(toep_in[par], 16)

                def step(it, n, last):
                    s, c = divmod(n, CG)
                    channel = it * CI + n
                    sp.wait_ge(summed, it * CI + n + 1)
                    sp.wait_ge(sq_summed, (it * CI + n) * 2 + 3)
                    for p in range(2):
                        sp.dma_start(x1[HB * p:HB * p + HB, channel].rearrange("b h w -> h b w"),
                                     x[HALF * p:HALF * p + H, s, c, :, :]).then_inc(stored[n % 2], 16)
                        sp.dma_start(rsum[channel, :, p].rearrange("a h b -> h a b"), rs[HALF * p:HALF * p + H, n])\
                            .then_inc(stored[n % 2], 16)
                    if not last or n + 3 < CI:
                        sp.wait_ge(b_mm, it * NBU + (n + 2) * B_UNITS)
                        load_toep((n + 1) % 2, channel + 3)
                    if not last:
                        sp.wait_ge(stored[n % 2], 64 * (it * (CI // 2) + n // 2 + 1))
                        load_x(s, c, channel + CI)

                for n in range(2):
                    sp.wait_ge(toep_clear[n], 1)
                    load_toep(n, n)
                sp.wait_ge(b_mm, B_UNITS)
                load_toep(0, 2)
                if IT > 1:
                    with sp.Fori(0, IT - 1) as it:
                        for n in range(CI):
                            step(it, n, False)
                for n in range(CI):
                    step(IT - 1, n, True)
                for s in range(2):
                    sp.wait_ge(stored[s], 64 * IT * (CI // 2))

            @block.gpsimd
            def _(pool):
                pool.memset(toep[32:64, 1], 0.0).then_inc(toep_clear[1], 1)
                pool.wait_ge(toep_clear[1], 1)
                pool.memset(xn[:, :, :, W:WP], 0.0).then_inc(cleared, 1)

                def normalise(it, n):
                    s, c = divmod(n % CI, CG)
                    over = lambda a: a[:].rearrange("p (b o) -> p b o", o=1).broadcast_to([KP, HB, W])
                    if c == 0:
                        pool.wait_ge(scaled, 2 * (it * 2 + n // CG + 1))
                    pool.wait_ge(a_mm, it * NA + (n + 1) * len(A_UNITS))
                    nc.gpsimd.tensor_tensor(xn[0:KP, c, :, 0:W], x[0:KP, s, c], over(scale), ALU.mult)\
                        .then_inc(multiplied, 1)
                    pool.wait_ge(multiplied, it * CI + n + 1)
                    nc.gpsimd.tensor_tensor(xn[0:KP, c, :, 0:W], xn[0:KP, c, :, 0:W], over(shift), ALU.add)\
                        .then_inc(normed, 1)

                pool.wait_ge(cleared, 1)
                for n in range(AHEAD):
                    normalise(0, n)
                if IT > 1:
                    with pool.Fori(0, IT - 1) as it:
                        for n in range(CI):
                            normalise(it, n + AHEAD)
                for n in range(CI - AHEAD):
                    normalise(IT - 1, n + AHEAD)

            @block.tensor
            def _(pe):
                def forward(it, n, units=range(len(A_UNITS))):
                    s, c = divmod(n, CG)
                    for k in units:
                        size, m = A_UNITS[k], sum(A_UNITS[:k])
                        unit = n * len(A_UNITS) + k
                        if k == 0:
                            pe.wait_ge(normed, it * CI + n + 1)
                        pe.wait_ge(a_act, it * NA + unit + 1)
                        pe.wait_ge(a_dve, it * NA + unit + 1)
                        for r in range(size):
                            cols = xn[0:KP, c, 2 * m:2 * m + 2, :].rearrange("p b w -> p (b w)")
                            mm = pe.matmul(pa[:, unit % 2, 4 * U * r:4 * U * r + 4 * U], cols, fwd[:],
                                           start=True, stop=True)
                            m += 1
                        mm.then_inc(a_mm, 1)

                def toeplitz(it, n, mean_count):
                    pe.wait_ge(toep_made, it * CI + n + 1)
                    pe.wait_ge(a_act, it * NA + (n + 1) * len(A_UNITS) + 2)
                    pe.wait_ge(a_dve, it * NA + (n + 1) * len(A_UNITS) + 2)
                    by_u = xhat[:].rearrange("p (a u) b -> p u a b", a=2)
                    for k in range(B_UNITS):
                        if k == MEAN_AT and mean_count is not None:
                            pe.wait_ge(d_dve, it * ND + n * D_UNITS + 2)
                            group_mean(mean_count)
                        unit = n * B_UNITS + k
                        pe.wait_ge(b_act, it * NBU + unit + 1)
                        for r in range(B_MM):
                            u = k * B_MM + r
                            mm = pe.matmul(pb[0:2 * W, unit % 2, B * r:B * r + B],
                                           toep[0:KP, n % 2, :, :, u].rearrange("p r v -> p (r v)"),
                                           by_u[0:KP, u], start=True, stop=True)
                        mm.then_inc(b_mm, 1)

                def turn(it, n, k):
                    unit = n * T_UNITS + k
                    if k == 0:
                        pe.wait_ge(b_act, it * NBU + (n + 1) * B_UNITS + 2)
                    if unit % 2 == 0:
                        pe.wait_ge(t_act, it * (NT // 2) + unit // 2 + 1)
                    else:
                        pe.wait_ge(t_dve, it * (NT // 2) + unit // 2 + 1)
                    for r in range(T_MM):
                        mm = pe.transpose(pt[0:2 * U, unit % 2, 2 * W * r:2 * W * r + 2 * W],
                                          prod[:, T_MM * k + r].rearrange("p a u -> p (a u)"), eye[0:2 * W, 0:2 * W])
                    mm.then_inc(t_mm, 1)

                def inverse(it, n, k):
                    unit = n * D_UNITS + k
                    pe.wait_ge(d_dve, it * ND + unit + 1)
                    pe.wait_ge(t_act, it * (NT // 2) + (n * T_UNITS + 2 * k) // 2 + 2)
                    pe.wait_ge(t_dve, it * (NT // 2) + (n * T_UNITS + 2 * k) // 2 + 2)
                    for r in range(2):
                        mm = pe.matmul(pd[0:KP, unit % 2, 0:D_BQ * W], inv[:, r, :],
                                       prodT[:, D_BQ * k % RING:D_BQ * k % RING + D_BQ, r, :], start=(r == 0), stop=(r == 1))
                    mm.then_inc(d_mm, 1)

                def group_mean(count):
                    pe.wait_ge(q_made, count)
                    pe.matmul(pd[0:KP, 0, 0:2 * HB], mean[:], q[:].rearrange("p a b -> p (a b)"),
                              start=True, stop=True).then_inc(mean_mm, 1)

                def channels(it, last):
                    for s in range(2):
                        more = not (last and s == 1)
                        for c in range(CG):
                            n = s * CG + c
                            toeplitz(it, n, it * 2 + s + 2 if c == CG - 2 and more else None)
                            for kind, k in MIX:
                                if kind == "A" and (n < CI - 1 or more):
                                    forward(it, n + 1, (int(k),))
                                if kind == "T":
                                    turn(it, n, int(k))
                                if kind == "D":
                                    if k == "0" and c == CG - 2 and more:
                                        pe.wait_ge(mv_read, it * 2 + s + 2)
                                    inverse(it, n, int(k))

                pe.sem_inc(a_mm, A_FREE)
                pe.wait_ge(const_in, 48)
                pe.wait_ge(cleared, 1)
                for clear in toep_clear:
                    pe.wait_ge(clear, 1)
                group_mean(1)
                pe.wait_ge(mv_read, 1)
                forward(0, 0)
                if IT > 1:
                    with pe.Fori(0, IT - 1) as it:
                        channels(it, False)
                channels(IT - 1, True)

            @block.scalar
            def _(act):
                def std(count):
                    act.wait_ge(var_made, count)
                    nc.scalar.activation(mv[:, 2, :], mv[:, 2, :], ACT.Sqrt).then_inc(std_made, 1)

                def forward_out(it, n, units=range(len(A_UNITS))):
                    for k in units:
                        size = A_UNITS[k]
                        unit = n * len(A_UNITS) + k
                        act.wait_ge(a_mm, it * NA + A_FREE + unit + 1)
                        copy_xhat(nc.scalar, 0, unit, k, size).then_inc(a_act, 1)

                def copy_xhat(eng, j, unit, k, size):
                    m0 = sum(A_UNITS[:k])
                    for r in range(2):
                        src = pa[HALF * j:HALF * j + 64, unit % 2, 0:4 * U * size]\
                            .rearrange("p (m r u) -> p r m u", m=size, r=2)[:, r]
                        dst = xhat[64 * r:64 * r + 64].rearrange("p u (m j) -> p j m u", j=2)[:, j, m0:m0 + size]
                        ins = eng.activation(dst, src, ACT.Copy)
                    return ins

                def product_out(it, n, std_count):
                    for k in range(B_UNITS):
                        if k == MEAN_AT + 1 and std_count is not None:
                            std(std_count)
                        unit = n * B_UNITS + k
                        act.wait_ge(b_mm, it * NBU + unit + 1)
                        nc.scalar.activation(
                            prod[:].rearrange("p b a u -> p u a b")[:, B_MM * k:B_MM * k + B_MM],
                            pb[0:2 * W, unit % 2, 0:B_MM * B].rearrange("p (u a b) -> p u a b", a=2, b=HB), ACT.Copy)\
                            .then_inc(b_act, 1)

                def turn_out(it, n, k):
                    unit = n * T_UNITS + k
                    act.wait_ge(t_mm, it * NT + unit + 1)
                    nc.scalar.activation(
                        prodT[:, T_MM * k % RING:T_MM * k % RING + T_MM].rearrange("p b r v -> p (b r v)"),
                        pt[0:2 * U, unit % 2, 0:T_MM * 2 * W], ACT.Copy).then_inc(t_act, 1)

                def imaginary_rows(it, n, r, a, b):
                    act.wait_ge(toep_in[n % 2], 16 * (it * (CI // 2) + n // 2 + 1))
                    return nc.scalar.activation(toep[HALF:HALF + W, n % 2, 1 - r, a:b], toep[0:W, n % 2, r, a:b],
                                                ACT.Copy, scale=(1.0, -1.0)[r])

                def squares(it, n, k):
                    s, c = divmod(n, CG)
                    act.wait_ge(sq_summed, (it * CI + n) * 2 + k + 1)
                    act.wait_ge(d_dve, it * ND + n * D_UNITS + 2 * k + 2 + 2)
                    nc.scalar.activation(square[:], x[0:KP, s, c, HB // 2 * k:HB // 2 * k + HB // 2, :],
                                         ACT.Square).then_inc(squared, 1)

                def channels(it, last):
                    for s in range(2):
                        more = not (last and s == 1)
                        for c in range(CG):
                            n = s * CG + c
                            product_out(it, n, it * 2 + s + 2 if c == CG - 2 and more else None)
                            for kind, k in MIX:
                                if kind == "A" and (n < CI - 1 or more):
                                    forward_out(it, n + 1, (int(k),))
                                if kind == "T" and int(k) % 2 == 0:
                                    turn_out(it, n, int(k))
                                    if k in "246" and (n < CI - 1 or more):
                                        r, a, b = {"2": (0, 0, W), "4": (1, 0, SPLIT), "6": (1, SPLIT, W)}[k]
                                        rows = imaginary_rows(it, n + 1, r, a, b)
                                        if k == "6":
                                            rows.then_inc(toep_made, 1)
                            for k in range(2):
                                squares(it, n, k)

                act.sem_inc(a_act, 2)
                act.sem_inc(b_act, 2)
                act.sem_inc(t_act, 1)
                std(1)
                imaginary_rows(0, 0, 0, 0, W)
                imaginary_rows(0, 0, 1, 0, W).then_inc(toep_made, 1)
                forward_out(0, 0)
                if IT > 1:
                    with act.Fori(0, IT - 1) as it:
                        channels(it, False)
                channels(IT - 1, True)

            @block.vector
            def _(dve):
                def bn(slot, images):
                    for b in images:
                        ins = nc.vector.bn_stats(stats[:, b, :], x[0:KP, slot, :, b, :])
                    ins.then_inc(st, 1)

                def q_of(count, first):
                    dve.wait_ge(st, 3 * count)
                    me, ve, mo, vo = (stats[:, :, i] for i in (1, 2, 4, 5))
                    if not first:
                        dve.wait_ge(mean_mm, count - 1)
                    nc.vector.tensor_tensor(q[:, 0, :], me, mo, ALU.add).then_inc(sc, 1)
                    nc.vector.tensor_tensor(part[:, 0, :], me, me, ALU.mult).then_inc(sc, 1)
                    nc.vector.tensor_tensor(part[:, 1, :], mo, mo, ALU.mult).then_inc(sc, 1)
                    nc.vector.tensor_tensor(part[:, 2, :], ve, vo, ALU.add).then_inc(sc, 1)
                    dve.wait_ge(sc, 7 * (count - 1) + 4)
                    nc.vector.tensor_tensor(part[:, 0, :], part[:, 0, :], part[:, 1, :], ALU.add).then_inc(sc, 1)
                    dve.wait_ge(sc, 7 * (count - 1) + 5)
                    nc.vector.scalar_tensor_tensor(q[:, 1, :], part[:, 2, :], 2.0 / (CG * W), part[:, 0, :],
                                                   ALU.mult, ALU.add).then_inc(q_made, 1)

                def scales(count, first):
                    dve.wait_ge(mean_mm, count)
                    nc.vector.tensor_copy(mv[:, 0:2, :], pd[0:KP, 0, 0:2 * HB].rearrange("p (a b) -> p a b", a=2))\
                        .then_inc(mv_read, 1)
                    dve.wait_ge(mv_read, count)
                    nc.vector.tensor_tensor(part[:, 0, :], mv[:, 0, :], mv[:, 0, :], ALU.mult).then_inc(sc, 1)
                    dve.wait_ge(sc, 7 * (count - 1) + 6)
                    nc.vector.tensor_tensor(part[:, 1, :], mv[:, 1, :], part[:, 0, :], ALU.subtract).then_inc(sc, 1)
                    dve.wait_ge(sc, 7 * (count - 1) + 7)
                    nc.vector.tensor_scalar(mv[:, 2, :], part[:, 1, :], 0.0, EPS, ALU.max, ALU.add)\
                        .then_inc(var_made, 1)
                    if not first:
                        dve.wait_ge(normed, CG * (count - 1))
                    dve.wait_ge(std_made, count)
                    nc.vector.reciprocal(scale[:], mv[:, 2, :]).then_inc(scaled, 1)
                    dve.wait_ge(scaled, 2 * count - 1)
                    nc.vector.scalar_tensor_tensor(shift[:], mv[:, 0, :], -1.0, scale[:], ALU.mult, ALU.mult)\
                        .then_inc(scaled, 1)

                def forward_out(it, n, units=range(len(A_UNITS))):
                    for k in units:
                        size = A_UNITS[k]
                        unit = n * len(A_UNITS) + k
                        dve.wait_ge(a_mm, it * NA + A_FREE + unit + 1)
                        m0 = sum(A_UNITS[:k])
                        for r in range(2):
                            src = pa[HALF:HALF + 64, unit % 2, 0:4 * U * size]\
                                .rearrange("p (m r u) -> p r m u", m=size, r=2)[:, r]
                            dst = xhat[64 * r:64 * r + 64].rearrange("p u (m j) -> p j m u", j=2)[:, 1, m0:m0 + size]
                            ins = nc.vector.tensor_copy(dst, src)
                        ins.then_inc(a_dve, 1)

                def turn_out(it, n, k):
                    unit = n * T_UNITS + k
                    dve.wait_ge(t_mm, it * NT + unit + 1)
                    nc.vector.tensor_copy(
                        prodT[:, T_MM * k % RING:T_MM * k % RING + T_MM].rearrange("p b r v -> p (b r v)"),
                        pt[0:2 * U, unit % 2, 0:T_MM * 2 * W]).then_inc(t_dve, 1)

                def inverse_out(it, n, k):
                    s, c = divmod(n, CG)
                    unit = n * D_UNITS + k
                    dve.wait_ge(d_mm, it * ND + unit + 1)
                    rows = x[0:KP, s, c, D_BQ * k:D_BQ * k + D_BQ, :]
                    y = pd[0:KP, unit % 2, 0:D_BQ * W].rearrange("p (b w) -> p b w", w=W)[:, :, ::-1]
                    nc.vector.tensor_tensor(rows, y, rows, ALU.add)\
                        .then_inc(d_dve, 1)

                def sums(it, n):
                    s, c = divmod(n, CG)
                    dve.wait_ge(d_dve, it * ND + (n + 1) * D_UNITS + 2)
                    nc.vector.reduce_sum(rs[:, n, 0, :], x[0:KP, s, c], AX.X).then_inc(summed, 1)

                def square_sums(it, n, k):
                    dve.wait_ge(squared, (it * CI + n) * 2 + k + 1)
                    nc.vector.reduce_sum(rs[:, n, 1, HB // 2 * k:HB // 2 * k + HB // 2], square[:], AX.X)\
                        .then_inc(sq_summed, 1)

                def channels(it, last):
                    for s in range(2):
                        done = it * 2 + s + 1
                        more = not (last and s == 1)
                        for c in range(CG):
                            n = s * CG + c
                            if c in STAT_CH and more:
                                if c == 1:
                                    dve.wait_ge(x_in[1 - s], 32 * CG * (it + 1 + s))
                                bn(1 - s, STAT_CH[c])
                                if c == CG - 3:
                                    q_of(done + 1, False)
                            if c == CG - 2 and more:
                                scales(done + 1, False)
                            for kind, k in MIX:
                                if kind == "A" and (n < CI - 1 or more):
                                    forward_out(it, n + 1, (int(k),))
                                if kind == "T" and int(k) % 2 == 1:
                                    turn_out(it, n, int(k))
                                if kind == "D":
                                    if int(k) == D_UNITS - 1:
                                        square_sums(it, n, 0)
                                    inverse_out(it, n, int(k))
                            sums(it, n)
                            square_sums(it, n, 1)

                dve.sem_inc(a_dve, 2)
                dve.sem_inc(sq_summed, 1)
                dve.sem_inc(t_dve, 1)
                dve.sem_inc(d_dve, 2)
                nc.vector.memset(toep[32:64, 0], 0.0).then_inc(toep_clear[0], 1)
                q_of(1, True)
                scales(1, True)
                forward_out(0, 0)
                if IT > 1:
                    with dve.Fori(0, IT - 1) as it:
                        channels(it, False)
                channels(IT - 1, True)


def attention(nc, d, x1, rsum, y, images=B):
    HEADS, DH, NMEM, REP = 4, 32, 4, 160
    HID = HEADS * DH
    SCALE = DH ** -0.5
    PX = 2 * W
    BLOCKS = H * W // PX
    UNITS, UB = BLOCKS // 2, 2
    TERMS = H + W
    KEYS = 68
    MEM = HALF
    FOURS = images // 4
    LAPS = UNITS - 2
    with ExitStack() as ctx:
        sb = lambda n, s: ctx.enter_context(nc.sbuf_tensor("t_" + n, s, F32))
        ps = lambda n, k=1: ctx.enter_context(nc.psum_tensor("t_" + n, [128, k, 512], F32))
        sem = lambda n: ctx.enter_context(nc.semaphore("t_" + n))
        x = sb("x", [HC + 1, 4, 2, H, W])
        xT = sb("xT", [PX, 2, BLOCKS, C])
        diag = sb("diag", [HC + 1, 2, 2, HC])
        shifts = sb("shifts", [HC, 2, HC])
        weights = sb("weights", [PX, BLOCKS * (TERMS + UB)])
        by_block = weights[:, 0:BLOCKS * TERMS].rearrange("p (b k) -> p b k", b=BLOCKS)
        row_places = weights[:].rearrange("p (b k) -> p b k", b=BLOCKS)[:, :, 0:UB]
        ind = sb("ind", [PX, UB + W])
        junk = sb("junk", [PX, 2, UB, C])
        n2 = sb("n2", [PX, BLOCKS])
        rooted = sb("rooted", [1, 1])
        sums = sb("sums", [HC, 2, 2, H, HB])
        squares = x[0:HC, 2:4].rearrange("p k m h w -> p (k m h w)")[:, 0:4 * H * HB]\
            .rearrange("p (m g h q) -> p m g h q", m=2, g=2, h=H)
        stat = sb("stat", [HC, 4, 2, B])
        cols = sb("cols", [HC, 4, 4, 2])
        raw = sb("raw", [HC, 2, 2, W])
        feat = sb("feat", [HC, 2, 2, W])
        vfeat = sb("vfeat", [HC, 2, 2, W])
        fn = sb("fn", [HID, 2 * W])
        Q = sb("Q", [HID, 2, W])
        K = sb("K", [HID, 2, HEADS, KEYS])
        E = sb("E", [W, 2, HEADS, KEYS])
        zs = sb("zs", [W, 5, 2 * HEADS])
        ET_fsq = sb("ET_fsq", [128, 2 * HEADS * W])
        ET = ET_fsq[0:KEYS].rearrange("p (t h w) -> p t h w", t=2, h=HEADS)
        fsq = ET_fsq[0:HC, 0:4 * W].rearrange("p (m t w) -> p m t w", m=2, t=2)
        V = sb("V", [KEYS, 2, HID])
        O = Q
        term = sb("term", [HC, 2, 2, 2, W])
        nrm = sb("nrm", [PX, BLOCKS])
        wq, wk, wv = (sb(n, [HC, 2, HID]) for n in ("wq", "wk", "wv"))
        gains = sb("gains", [HC, 3, 2])
        first = xT[0:HC, 0].rearrange("p b c -> p (b c)")
        wo = first[:, 0:2 * HID].rearrange("p (m c) -> p m c", m=2)
        wr = first[:, 256:256 + 4 * C].rearrange("p (m t c) -> p m t c", m=2, t=2)
        tot = first[:, 1024:1024 + 4 * B].rearrange("p (a m b) -> p a m b", a=2, m=2)
        gmean = first[:, 1280:1280 + HC]
        var = first[:, 1376:1376 + 2 * B].rearrange("p (m b) -> p m b", m=2)
        bo = first[:, 1504:1506]
        wc = sb("wc", [HID, 2, C])
        bias = sb("bias", [HC, 2, 2])
        eye = sb("eye", [128, 128])
        ones = sb("ones", [128, 128])
        pturn, psum, pshift = ps("pturn", 2), ps("psum"), ps("pshift")
        pq, psc, pt = ps("pq"), ps("psc", 2), ps("pt")
        names = """w_in k_in v_in cleared scaled gm_mm tots gm_copy neg_mean mean_squared inv_made var_made root_made
            stat_made wc_mm wc_made
            fetched diag_made shift_mm shift_in turn_mm turned n_sqrt n_max n_inv weighted sums_mm v_ready cs_made
            f_made fsq_made fn_mm fn_sqrt fn_max fn_inv qk_mm qk_made s_mm mx_made s_sub e_made z_k z_m z_made z_inv
            table_in e_norm t_mm et_made v_mm v_made o_mm o_made term_mm term_made row_added added row_added0 added0 rows_in""".split()
        S = {n: sem(n) for n in names}
        x_in = [sem(f"x_in{k}") for k in range(4)]
        sum_in = [[sem(f"sum_in{a}_{m}") for m in range(2)] for a in range(2)]
        stored = [[sem(f"stored{k}_{m}") for m in range(2)] for k in range(4)]

        def wait(eng, name, value):
            if not (isinstance(value, int) and value <= 0):
                eng.wait_ge(S[name], value)

        def along_rows(slot, m):
            return term[:, slot % 2, 0, m].rearrange("p (h o) -> p h o", o=1).broadcast_to([HC, H, W])

        def along_columns(slot, m):
            return term[:, slot % 2, 1, m].rearrange("p (o w) -> p o w", o=1).broadcast_to([HC, H, W])

        def schedule(eng, step):
            for j in range(-2, 2):
                step(0, j, True, j >= -1, j >= 0, j >= 1)
            passes = (images - 4) // 4
            if passes:
                with eng.Fori(0, passes) as it:
                    for j in range(2, 6):
                        step(it, j, True, True, True, True)
            for j in range(4 * passes + 2, images + 1):
                step(0, j, j + 2 < images, j + 1 < images, j < images, True)

        with nc.Block() as block:

            @block.sync
            def _(sp):
                for dst, src, s in (
                        (wq[:], d["WqT"], "w_in"), (wk[:], d["WkT"], "w_in"), (wv[:], d["WvT"], "w_in"),
                        (wo, d["Wo"], "w_in"), (wr, d["WrT"], "w_in"), (bo, d["bo"], "w_in"),
                        (gains[:], d["gains"], "w_in"), (eye[:], d["k_eye"], "w_in"), (ind[:], d["k_ind"], "w_in"), (gmean, d["k_gmean"], "w_in"),
                        (x[HC:HC + 1].rearrange("p k m h w -> p (k m h w)"), d["k_ones"], "w_in")):
                    sp.dma_start(dst, src).then_inc(S[s], 16)
                for m in range(2):
                    for dst, a in ((sums, 0), (squares, 1)):
                        sp.dma_start(dst[:, m], rsum[HC * m:HC * m + HC, a]).then_inc(sum_in[a][m], 16)
                def where(four, k):
                    return HB * (k // 2) + four * 2 + k % 2

                def load(four, k, m):
                    sp.dma_start(x[0:HC, k, m], x1[where(four, k), HC * m:HC * m + HC]).then_inc(x_in[k], 16)

                def store(four, k, m):
                    sp.dma_start(y[where(four, k), HC * m:HC * m + HC], x[0:HC, k, m]).then_inc(stored[k][m], 16)

                def leave(four, k):
                    sp.wait_ge(S["added0"], four * 4 + k + 1)
                    store(four, k, 0)
                    sp.wait_ge(S["added"], four * 4 + k + 3)
                    store(four, k, 1)

                for k in range(4):
                    if k == 0:
                        sp.wait_ge(S["cleared"], 5)
                        for t in range(2):
                            for j in range(3):
                                for h in range(HEADS):
                                    sp.dma_start(K[DH * h:DH * h + DH, t, h, W + NMEM * j:W + NMEM * j + NMEM],
                                                 d["mem_kT"][h]).then_inc(S["k_in"], 16)
                            sp.dma_start(V[MEM:MEM + NMEM, t, :], d["mem_v"]).then_inc(S["v_in"], 16)
                    if k == 2:
                        sp.wait_ge(S["tots"], 1)
                    for m in range(2):
                        load(0, k, m)
                if FOURS > 1:
                    with sp.Fori(0, FOURS - 1) as it:
                        for k in range(4):
                            leave(it, k)
                            for m in range(2):
                                sp.wait_ge(stored[k][m], it * 16 + 16)
                                load(it + 1, k, m)
                for k in range(4):
                    leave(FOURS - 1, k)
                for k in range(4):
                    for m in range(2):
                        sp.wait_ge(stored[k][m], 16 * FOURS)

            @block.gpsimd
            def _(pool):
                pool.sem_inc(S["added"], 2)
                pool.memset(K[:], 0.0).then_inc(S["cleared"], 1)
                pool.memset(ones[:], 1.0).then_inc(S["cleared"], 1)
                pool.memset(bias[:], 0.0).then_inc(S["cleared"], 1)
                pool.memset(V[:], 0.0).then_inc(S["cleared"], 1)
                pool.memset(weights[:], 0.0).then_inc(S["cleared"], 1)

                def step(it, j, prep, turn, weigh, attend):
                    if attend:
                        i, slot = it * 4 + (j - 1), (j - 1) % 4
                        wait(pool, "term_made", i + 2)
                        nc.gpsimd.tensor_tensor(x[0:HC, slot, 1], x[0:HC, slot, 1], along_rows(slot, 1), ALU.add)\
                            .then_inc(S["row_added"], 1)
                        wait(pool, "row_added", i + 1)
                        nc.gpsimd.tensor_tensor(x[0:HC, slot, 1], x[0:HC, slot, 1], along_columns(slot, 1), ALU.add)\
                            .then_inc(S["added"], 1)
                schedule(pool, step)

            @block.tensor
            def _(pe):
                def before():
                    pe.wait_ge(S["w_in"], 11 * 16)
                    pe.wait_ge(S["cleared"], 5)
                    for t in range(2):
                        for m in range(2):
                            pe.matmul(psc[0:HID, t, 0:C], wo[:, m, :], wr[:, m, t, :], start=(m == 0), stop=(m == 1))
                    for o in range(2):
                        for t in range(2):
                            for m in range(2):
                                mm = pe.matmul(pt[0:HC, 0, o:o + 1], wr[:, m, t, HC * o:HC * o + HC], bo[:, m:m + 1],
                                               start=(t + m == 0), stop=(t + m == 2))
                    mm.then_inc(S["wc_mm"], 1)
                    pe.wait_ge(S["tots"], 1)
                    pe.matmul(pq[0:HC, 0, 0:4 * B], gmean, tot.rearrange("p a m b -> p (a m b)"),
                              start=True, stop=True).then_inc(S["gm_mm"], 1)
                    pe.wait_ge(S["scaled"], 3)
                    pe.wait_ge(S["wc_made"], 3)
                    pe.wait_ge(S["gm_copy"], 1)
                    pe.wait_ge(S["k_in"], 16 * 24)
                    pe.wait_ge(S["v_in"], 16 * 2)

                def turned_block(n, j, u):
                    m, k, par = n + 1, (j + 1) % 4, (j + 1) % 2
                    if u > 1:
                        wait(pe, "turned", m * UNITS + (u - 1))
                    elif not (isinstance(n, int) and n < 0):
                        wait(pe, "turned", n * UNITS + (UNITS + u - 1))
                    for r in range(UB):
                        for h in range(2):
                            b = UB * u + r
                            mm = pe.matmul(pturn[0:PX, u % 2, C * r + HC * h:C * r + HC * h + HC],
                                           x[:, k, h, UB * b:UB * b + UB, :].rearrange("p h w -> p (h w)"),
                                           diag[:, par, h, :], start=True, stop=True)
                    mm.then_inc(S["turn_mm"], 1)

                def weighted_sums(j, a, b):
                    for g in range(a, b):
                        h, block = divmod(g, BLOCKS)
                        mm = pe.matmul(psum[0:HC, 0, TERMS * h:TERMS * h + TERMS],
                                       xT[:, j % 2, block, HC * h:HC * h + HC], by_block[:, block, :],
                                       start=(block == 0), stop=(block == BLOCKS - 1))
                    if b == 2 * BLOCKS:
                        mm.then_inc(S["sums_mm"], 1)

                def step(it, j, prep, turn, weigh, attend):
                    n, i = it * 4 + j, it * 4 + (j - 1)
                    if turn:
                        pe.wait_ge(x_in[(j + 1) % 4], it * 32 + 32 * ((j + 1) // 4 + 1))
                        wait(pe, "diag_made", n * 2 + 4)
                        wait(pe, "shift_in", n + 2)
                        for u in range(2):
                            turned_block(n, j, u)
                    if attend:
                        wait(pe, "fsq_made", i + 1)
                        for m in range(2):
                            mm = pe.matmul(pt[0:HID, 0, 0:2 * W], ones[0:HC, :], fsq[:, m].rearrange("p t w -> p (t w)"),
                                           start=(m == 0), stop=(m == 1))
                        mm.then_inc(S["fn_mm"], 1)
                        for a, w in enumerate((wq, wk)):
                            for m in range(2):
                                mm = pe.matmul(pqk(a), w[:, m, :], feat[:, m].rearrange("p t w -> p (t w)"),
                                               start=(m == 0), stop=(m == 1))
                        mm.then_inc(S["qk_mm"], 1)
                    for lap in range(LAPS):
                        if lap == 6 and attend:
                            wait(pe, "e_norm", i + 1)
                        if turn:
                            turned_block(n, j, 2 + lap)
                        if lap == 0 and weigh:
                            wait(pe, "weighted", n * 2 + 2)
                            if not (isinstance(n, int) and n <= 0):
                                wait(pe, "v_ready", n)
                        if weigh:
                            weighted_sums(j, 2 * BLOCKS * lap // LAPS, 2 * BLOCKS * (lap + 1) // LAPS)
                        if lap == 1 and attend:
                            wait(pe, "qk_made", i * 5 + 5)
                            wait(pe, "term_made", i + 1)
                            for t in range(2):
                                mm = pe.matmul(psc[0:W, t, 0:HEADS * KEYS], Q[:, t, :],
                                               K[:, 1 - t].rearrange("p h j -> p (h j)"), start=True, stop=True)
                            mm.then_inc(S["s_mm"], 1)
                            wait(pe, "v_ready", i + 1)
                            for t in range(2):
                                for m in range(2):
                                    mm = pe.matmul(pq[0:W, 0, HID * t:HID * t + HID], vfeat[:, m, 1 - t, :], wv[:, m, :],
                                                   start=(m == 0), stop=(m == 1))
                            mm.then_inc(S["v_mm"], 1)
                        if lap == 6 and attend:
                            for t in range(2):
                                for h in range(HEADS):
                                    a = (t * HEADS + h) * W
                                    mm = pe.transpose(pt[0:KEYS, 0, a:a + W], E[:, t, h, :], eye[0:W, 0:W])
                            mm.then_inc(S["t_mm"], 1)
                        if lap == 7 and attend:
                            wait(pe, "et_made", i + 1)
                            wait(pe, "v_made", i + 1)
                            for h in range(HEADS):
                                for t in range(2):
                                    mm = pe.matmul(psc[DH * h:DH * h + DH, 0, W * t:W * t + W],
                                                   V[:, t, DH * h:DH * h + DH], ET[:, t, h, :], start=True, stop=True)
                            mm.then_inc(S["o_mm"], 1)
                        if lap == 8 and attend:
                            wait(pe, "o_made", i + 1)
                            for t in range(2):
                                for m in range(2):
                                    a = (t * 2 + m) * W
                                    mm = pe.matmul(psc[0:HC, 1, a:a + W], wc[:, t, HC * m:HC * m + HC], O[:, t, :],
                                                   start=True, stop=True)
                            mm.then_inc(S["term_mm"], 1)
                        if lap == 4 and prep:
                            wait(pe, "diag_made", n * 2 + 6)
                            if not (isinstance(n, int) and n < -1):
                                wait(pe, "shift_in", n + 2)
                            pe.matmul(pshift[0:HC + 1, 0, 0:C], ones[0:HC, 0:HC + 1],
                                      shifts[:].rearrange("p m c -> p (m c)"), start=True, stop=True)\
                                .then_inc(S["shift_mm"], 1)

                def pqk(a):
                    return pq[0:HID, 0, 2 * W * (a + 1):2 * W * (a + 2)]

                before()
                schedule(pe, step)

            @block.scalar
            def _(act):
                def before():
                    act.wait_ge(S["wc_mm"], 1)
                    for t in range(2):
                        nc.scalar.activation(wc[:, t, :], psc[0:HID, t, 0:C], ACT.Copy).then_inc(S["wc_made"], 1)
                    act.wait_ge(S["cleared"], 3)
                    nc.scalar.activation(bias[:, 0, :], pt[0:HC, 0, 0:2], ACT.Copy).then_inc(S["wc_made"], 1)
                    act.wait_ge(S["var_made"], 1)
                    nc.scalar.activation(stat[:, 1], var, ACT.Sqrt).then_inc(S["root_made"], 1)

                def turn_out(n, j, u):
                    wait(act, "turn_mm", n * UNITS + (UNITS + u + 1))
                    nc.scalar.activation(xT[:, (j + 1) % 2, UB * u:UB * u + UB, :].rearrange("p b c -> p (b c)"),
                                         pturn[0:PX, u % 2, 0:UB * C], ACT.Copy)
                    if u > 1:
                        wait(act, "turned", n * UNITS + (UNITS + u - 1))
                    elif u == 0:
                        wait(act, "n_sqrt", n + 1)
                    for r in range(UB):
                        ins = nc.scalar.activation(junk[:, u % 2, r], pturn[0:PX, u % 2, C * r:C * r + C], ACT.Square,
                                                   accum_out=n2[:, UB * u + r:UB * u + r + 1])
                    ins.then_inc(S["turned"], 1)

                def step(it, j, prep, turn, weigh, attend):
                    n, i = it * 4 + j, it * 4 + (j - 1)

                    def turn_units(a, b):
                        if turn:
                            for u in range(a, b):
                                turn_out(n, j, u)

                    if weigh:
                        wait(act, "turned", n * UNITS + UNITS)
                        nc.scalar.activation(nrm[:], n2[:], ACT.Sqrt).then_inc(S["n_sqrt"], 1)
                    if attend:
                        wait(act, "sums_mm", i + 1)
                        nc.scalar.activation(vfeat[:].rearrange("p m t w -> p (m t w)"), psum[0:HC, 0, 0:2 * TERMS],
                                             ACT.Copy).then_inc(S["v_ready"], 1)
                    turn_units(0, 2)
                    if attend:
                        wait(act, "fn_mm", i + 1)
                        nc.scalar.activation(fn[:], pt[0:HID, 0, 0:2 * W], ACT.Sqrt).then_inc(S["fn_sqrt"], 1)
                    turn_units(2, 4)
                    if attend:
                        wait(act, "v_mm", i + 1)
                        nc.scalar.activation(V[0:W].rearrange("p t c -> p (t c)"), pq[0:W, 0, 0:2 * HID], ACT.Copy)\
                            .then_inc(S["v_made"], 1)
                        wait(act, "s_sub", i + 1)
                        nc.scalar.activation(E[:], E[:], ACT.Exp, scale=SCALE).then_inc(S["e_made"], 1)
                    turn_units(4, 7)
                    if prep:
                        wait(act, "shift_mm", n + 3)
                        nc.scalar.activation(diag[HC:HC + 1, j % 2].rearrange("p m c -> p (m c)"),
                                             pshift[HC:HC + 1, 0, 0:C], ACT.Copy).then_inc(S["shift_in"], 1)
                    turn_units(7, 9)
                    if attend:
                        wait(act, "t_mm", i + 1)
                        nc.scalar.activation(ET_fsq[0:KEYS], pt[0:KEYS, 0, 0:2 * HEADS * W],
                                             ACT.Copy).then_inc(S["et_made"], 1)
                    turn_units(9, 10)
                    if attend:
                        wait(act, "o_mm", i + 1)
                        nc.scalar.activation(O[:].rearrange("p t w -> p (t w)"), psc[0:HID, 0, 0:2 * W], ACT.Copy)\
                            .then_inc(S["o_made"], 1)
                    turn_units(10, UNITS - 1)
                    if attend:
                        nc.scalar.activation(rooted[0:1, 0:1], ones[0:1, 0:1], ACT.Sqrt).then_inc(S["table_in"], 1)
                        wait(act, "table_in", i + 1)
                    turn_units(UNITS - 1, UNITS)

                before()
                schedule(act, step)

            @block.vector
            def _(dve):
                dve.sem_inc(S["term_made"], 1)

                def before():
                    dve.wait_ge(S["w_in"], 11 * 16)
                    root = float(C) ** 0.5
                    for j, w in enumerate((wq, wk, wv)):
                        for m in range(2):
                            ins = nc.vector.tensor_scalar(w[:, m, :], w[:, m, :], gains[:, j, m:m + 1], root,
                                                          ALU.mult, ALU.mult)
                        ins.then_inc(S["scaled"], 1)
                    for m in range(2):
                        for a in range(2):
                            dve.wait_ge(sum_in[a][m], 16)
                            ins = nc.vector.reduce_sum(
                                tot[:, a, m, :].rearrange("p (g q) -> p g q", g=2),
                                (sums, squares)[a][:, m].rearrange("p g h q -> p g q h"), AX.X)
                    ins.then_inc(S["tots"], 1)
                    both = lambda a: a.rearrange("p m b -> p (m b)")
                    dve.wait_ge(S["gm_mm"], 1)
                    nc.vector.tensor_scalar(both(stat[:, 2]), pq[0:HC, 0, 0:2 * B], -1.0, None, ALU.mult)\
                        .then_inc(S["neg_mean"], 1)
                    dve.wait_ge(S["neg_mean"], 1)
                    nc.vector.tensor_tensor(both(stat[:, 3]), both(stat[:, 2]), both(stat[:, 2]), ALU.mult)\
                        .then_inc(S["mean_squared"], 1)
                    dve.wait_ge(S["mean_squared"], 1)
                    nc.vector.tensor_tensor(both(var), pq[0:HC, 0, 2 * B:4 * B], both(stat[:, 3]), ALU.subtract)\
                        .then_inc(S["gm_copy"], 1)
                    dve.wait_ge(S["gm_copy"], 1)
                    nc.vector.tensor_scalar(var, var, 0.0, EPS, ALU.max, ALU.add).then_inc(S["var_made"], 1)
                    dve.wait_ge(S["root_made"], 1)
                    nc.vector.reciprocal(stat[:, 3], stat[:, 1]).then_inc(S["inv_made"], 1)
                    dve.wait_ge(S["inv_made"], 1)
                    nc.vector.tensor_scalar(stat[:, 0], stat[:, 3], 1.0 / W, None, ALU.mult).then_inc(S["stat_made"], 1)
                    nc.vector.tensor_tensor(stat[:, 1], stat[:, 2], stat[:, 3], ALU.mult).then_inc(S["stat_made"], 1)
                    dve.wait_ge(S["stat_made"], 2)

                def step(it, j, prep, turn, weigh, attend):
                    n, i = it * 4 + j, it * 4 + (j - 1)
                    k, slot, later = j % 4, (j - 1) % 4, (j + 2) % 4
                    late, late_slot = j >= 2, (j - 2) % 4
                    last = isinstance(it, int) and j == images

                    def place(offset):
                        r = (j + offset) % 4
                        return r // 2, it * 2 + ((j + offset) // 4 * 2 + r % 2)

                    def column_sums(m):
                        nc.vector.reduce_sum(raw[:, m, 1, :], x[0:HC, k, m].rearrange("p h w -> p w h"), AX.X)\
                            .then_inc(S["cs_made"], 1)

                    if weigh:
                        wait(dve, "n_sqrt", n + 1)
                        nc.vector.tensor_scalar(nrm[:], nrm[:], 1e-12, None, ALU.max).then_inc(S["n_max"], 1)
                        wait(dve, "n_max", n + 1)
                        nc.vector.reciprocal(nrm[:], nrm[:]).then_inc(S["n_inv"], 1)
                        wait(dve, "n_inv", n + 1)
                        if not (isinstance(n, int) and n <= 0):
                            wait(dve, "sums_mm", n)
                        inv = lambda w: nrm[:].rearrange("p (b o) -> p b o", o=1).broadcast_to([PX, BLOCKS, w])
                        which = lambda a, w: ind[:, a:a + w].rearrange("p (o w) -> p o w", o=1)\
                            .broadcast_to([PX, BLOCKS, w])
                        nc.vector.tensor_tensor(row_places, which(0, UB), inv(UB), ALU.mult).then_inc(S["weighted"], 1)
                        nc.vector.tensor_tensor(by_block[:, :, H:TERMS], which(UB, W), inv(W), ALU.mult)\
                            .then_inc(S["weighted"], 1)
                    if attend:
                        wait(dve, "fn_sqrt", i + 1)
                        nc.vector.tensor_scalar(fn[:], fn[:], 1e-12, None, ALU.max).then_inc(S["fn_max"], 1)
                        wait(dve, "fn_max", i + 1)
                        nc.vector.reciprocal(fn[:], fn[:]).then_inc(S["fn_inv"], 1)
                        wait(dve, "fn_inv", i + 1)
                        wait(dve, "qk_mm", i + 1)
                        nc.vector.tensor_tensor(Q[:].rearrange("p t w -> p (t w)"), pq[0:HID, 0, 2 * W:4 * W],
                                                fn[:], ALU.mult).then_inc(S["qk_made"], 1)
                        for h in range(HEADS):
                            r = slice(DH * h, DH * h + DH)
                            nc.vector.tensor_tensor(K[r, :, h, 0:W],
                                                    pq[r, 0, 4 * W:6 * W].rearrange("p (t w) -> p t w", t=2),
                                                    fn[r, :].rearrange("p (t w) -> p t w", t=2), ALU.mult)\
                                .then_inc(S["qk_made"], 1)
                    if late:
                        nc.vector.tensor_tensor(x[0:HC, late_slot, 0], x[0:HC, late_slot, 0],
                                                along_columns(late_slot, 0), ALU.add).then_inc(S["added0"], 1)
                    if weigh:
                        half, at = place(0)
                        nc.vector.tensor_copy(raw[:, :, 0, :], sums[:, :, half, :, bass.ds(at, 1)]
                                              .rearrange("p m h o -> p m (h o)")).then_inc(S["rows_in"], 1)
                    if attend:
                        wait(dve, "s_mm", i + 1)
                        scores = psc[0:W, :, 0:HEADS * KEYS].rearrange("p t (h j) -> p t h j", h=HEADS)
                        over = lambda z: z.rearrange("p (t h o) -> p t h o", t=2, o=1).broadcast_to([W, 2, HEADS, KEYS])
                        nc.vector.reduce_max(zs[:, 0, :].rearrange("p (t h) -> p t h", t=2), scores, AX.X)\
                            .then_inc(S["mx_made"], 1)
                        wait(dve, "mx_made", i + 1)
                        nc.vector.tensor_tensor(E[:], scores, over(zs[:, 0, :]), ALU.subtract).then_inc(S["s_sub"], 1)
                    if prep:
                        half, at = place(2)
                        nc.vector.tensor_copy(cols[:, later], stat[:, 0:4, :, bass.ds(at + HB * half, 1)]
                                              .rearrange("p a m o -> p a (m o)")).then_inc(S["fetched"], 1)
                        wait(dve, "fetched", n + 3)
                        if not (isinstance(n, int) and n < -1):
                            wait(dve, "shift_mm", n + 2)
                        if not (isinstance(n, int) and n < 0):
                            wait(dve, "turn_mm", n * UNITS + UNITS)
                        for m in range(2):
                            ins = nc.vector.tensor_scalar(diag[0:HC, j % 2, m, :], eye[0:HC, 0:HC],
                                                          cols[:, later, 3, m:m + 1], None, ALU.mult)
                        ins.then_inc(S["diag_made"], 1)
                        for m in range(2):
                            ins = nc.vector.tensor_scalar(shifts[:, m, :], eye[0:HC, 0:HC],
                                                          cols[:, later, 1, m:m + 1], None, ALU.mult)
                        ins.then_inc(S["diag_made"], 1)
                    if attend:
                        wait(dve, "e_made", i + 1)
                        th = lambda z: z.rearrange("p (t h) -> p t h", t=2)
                        nc.vector.reduce_sum(th(zs[:, 1, :]), E[:, :, :, 0:W], AX.X).then_inc(S["z_k"], 1)
                        nc.vector.reduce_sum(th(zs[:, 2, :]), E[:, :, :, KEYS - NMEM:KEYS], AX.X).then_inc(S["z_m"], 1)
                        wait(dve, "z_m", i + 1)
                        nc.vector.scalar_tensor_tensor(zs[:, 3, :], zs[:, 1, :], float(REP), zs[:, 2, :],
                                                       ALU.mult, ALU.add).then_inc(S["z_made"], 1)
                        wait(dve, "z_made", i + 1)
                        nc.vector.reciprocal(zs[:, 4, :], zs[:, 3, :]).then_inc(S["z_inv"], 1)
                        wait(dve, "z_inv", i + 1)
                        nc.vector.tensor_tensor(E[:], E[:], over(zs[:, 4, :]), ALU.mult).then_inc(S["e_norm"], 1)
                    if weigh:
                        dve.wait_ge(x_in[k], it * 32 + 32 * (j // 4 + 1))
                        column_sums(0)
                        column_sums(1)
                    if attend:
                        wait(dve, "term_mm", i + 1)
                        wait(dve, "added", i + 1)
                        nc.vector.tensor_tensor(
                            term[:, slot % 2],
                            psc[0:HC, 1, 0:4 * W].rearrange("p (t m w) -> p t m w", t=2, m=2),
                            bias[:].rearrange("p t (m o) -> p t m o", o=1).broadcast_to([HC, 2, 2, W]), ALU.add)\
                            .then_inc(S["term_made"], 1)
                    if weigh:
                        wait(dve, "cs_made", n * 2 + 2)
                        wait(dve, "rows_in", n + 1)
                        for m in range(2):
                            ins = nc.vector.tensor_scalar(feat[:, m], raw[:, m], cols[:, k, 0, m:m + 1],
                                                          cols[:, k, 1, m:m + 1], ALU.mult, ALU.add)
                        ins.then_inc(S["f_made"], 1)
                        wait(dve, "f_made", n + 1)
                        nc.vector.tensor_tensor(fsq, feat[:], feat[:], ALU.mult).then_inc(S["fsq_made"], 1)
                    if attend:
                        wait(dve, "term_made", i + 2)
                        nc.vector.tensor_tensor(x[0:HC, slot, 0], x[0:HC, slot, 0], along_rows(slot, 0), ALU.add)\
                            .then_inc(S["row_added0"], 1)
                        if last:
                            wait(dve, "row_added0", i + 1)
                            nc.vector.tensor_tensor(x[0:HC, slot, 0], x[0:HC, slot, 0], along_columns(slot, 0), ALU.add)\
                                .then_inc(S["added0"], 1)

                before()
                schedule(dve, step)


def laid_out(a):
    t = {n.split("conv_")[-1]: np.asarray(v) for n, v in a.items()}
    out = {
        "x": t["x"].reshape(2, HB, C, H, W).transpose(2, 0, 3, 1, 4),
        "z": t["z"].reshape(FEMB, KH, KH).transpose(0, 2, 1).reshape(FEMB, KH * KH),
        "W1T": t["W1"].T, "W2T": t["W2"].T, "W3T": t["W3"].T,
        "distance_map": t["distance_map"].reshape(KH, KH),
    }
    out["vec"] = np.stack([t[n].reshape(FORD) for n in ("b1", "f1", "b2", "f2")], axis=1)
    out["chan"] = np.stack([t[n].reshape(C) for n in ("deltas", "shift", "bias")])
    halves = lambda a: np.moveaxis(a.reshape((2, HC) + a.shape[1:]), 0, 1)
    for n in ("Wq", "Wk", "Wv"):
        out[n + "T"] = halves(t[n].T)
    out["Wo"], out["bo"] = halves(t["Wo"]), halves(t["bo"])
    out["WrT"] = halves(t["Wr"].reshape(C, 2, C).transpose(2, 1, 0))
    out["gains"] = halves(np.stack([t["gq"], t["gk"], t["gv"]], axis=1)).transpose(0, 2, 1)
    out["mem_kT"] = t["mem_kv"][0].transpose(0, 2, 1)
    out["mem_v"] = t["mem_kv"][1].transpose(1, 0, 2).reshape(t["mem_kv"].shape[2], -1)
    return out


def shared_places(nc, ctx):
    sb = lambda n, s: ctx.enter_context(nc.sbuf_tensor("s_" + n, s, F32))
    sem = lambda n: ctx.enter_context(nc.semaphore("s_" + n))
    return {
        "x": sb("x", [128, 2, CG, HB, W]),
        "stats": sb("stats", [KP, HB, 6]),
        "mean": sb("mean", [KP, KP]),
        "x_in": [sem("x_in0"), sem("x_in1")], "spare_clear": sem("spare_clear"), "st": sem("st"),
    }


def program(nc, d, y):
    khat = nc.dram_tensor("khat", (C, 2, NE * U), F32, kind="Internal").ap()
    x1 = nc.dram_tensor("x1", (B, C, H, W), F32, kind="Internal").ap()
    rsum = nc.dram_tensor("rsum", (C, 2, 2, H, HB), F32, kind="Internal").ap()
    with ExitStack() as ctx:
        shared = shared_places(nc, ctx)
        filters(nc, d, khat, shared)
        convolution(nc, d, khat, x1, rsum, shared)
    attention(nc, d, x1, rsum, y)


def kernel(**inputs):
    import concourse.bacc as bacc
    from concourse.bass_utils import run_bass_kernel_spmd

    nc = bacc.Bacc("TRN2", target_bir_lowering=False, num_devices=1)
    arrays, d = {}, {}
    for name, a in {**laid_out(inputs), **constants()}.items():
        arrays[f"in_{name}"] = np.ascontiguousarray(a)
        d[name] = nc.dram_tensor(f"in_{name}", a.shape, F32, kind="ExternalInput").ap()
    y = nc.dram_tensor("out", (B, C, H, W), F32, kind="ExternalOutput").ap()
    program(nc, d, y)
    return run_bass_kernel_spmd(nc, [arrays], core_ids=[0]).results[0]["out"]
```
